# Optimizing a Trainium2 kernel written in Bass

```python
import numpy as np
import jax
import jax.numpy as jnp

def _softmax(x, axis=-1):
    return jax.nn.softmax(x, axis=axis)

def _gelu(x):
    return jax.nn.gelu(x, approximate=True)

def _silu(x):
    return jax.nn.silu(x)

def _sigmoid(x):
    return jax.nn.sigmoid(x)

def _layernorm(x, axis=-1, eps=1e-05):
    m = jnp.mean(x, axis=axis, keepdims=True)
    v = jnp.var(x, axis=axis, keepdims=True)
    return (x - m) / jnp.sqrt(v + eps)

def _scatter_add(tgt, idx, src, axis=0):
    return tgt.at[idx].add(src)

def _segment_sum(src, seg, n):
    return jax.ops.segment_sum(src, seg, n)
kernel_name = 'mk_macaron_d1_jaxref_r8_b3e3b9'

def setup_inputs(seed: int=0):
    np.random.seed(seed)
    _w = jnp.asarray

    def _L0_attn_setup():
        import jax, jax.numpy as jnp
        import numpy as np
        B, L = (2, 128)
        D_MODEL, D_CKV, D_CQ = (128, 32, 64)
        N_HEAD, D_HEAD, D_ROPE = (8, 64, 32)
        N_IDX_HEAD = 4
        K_TS, LW = (96, 64)
        ROPE_BASE = 10000.0

        def _pope(x, angles):
            cos, sin = (jnp.cos(angles), jnp.sin(angles))
            mu1, mu2 = jnp.split(jax.nn.softplus(x), 2, axis=-1)
            return jnp.concatenate([mu1 * cos - mu2 * sin, mu1 * sin + mu2 * cos], axis=-1)

        def _forward(x, W_dkv, W_uk, W_uv, W_dq, W_uq, W_qr, W_kr, W_out, idx_wq, idx_wk, idx_w, raw_delta):
            B_, L_, _ = x.shape
            c_kv = x @ W_dkv
            q_i = (x @ idx_wq).reshape(B_, L_, N_IDX_HEAD, D_HEAD)
            k_i = x @ idx_wk
            s_i = jax.nn.relu(jnp.einsum('bthd,bsd->bths', q_i, k_i))
            I = jnp.einsum('bths,h->bts', s_i, idx_w)
            qpos = jnp.arange(L_)[:, None]
            kpos = jnp.arange(L_)[None, :]
            local = (kpos >= qpos - LW + 1) & (kpos <= qpos)
            causal = kpos > qpos
            I = jnp.where(local[None], jnp.inf, I)
            I = jnp.where(causal[None], -jnp.inf, I)
            kk = min(K_TS, L_)
            _, idx = jax.lax.top_k(I, kk)
            bi = jnp.arange(B_)[:, None, None]
            key_c = (c_kv @ W_uk)[bi, idx].reshape(B_, L_, kk, N_HEAD, D_HEAD)
            value = (c_kv @ W_uv)[bi, idx].reshape(B_, L_, kk, N_HEAD, D_HEAD)
            c_q = x @ W_dq
            query_c = (c_q @ W_uq).reshape(B_, L_, N_HEAD, D_HEAD)
            half = D_ROPE // 2
            theta = 1.0 / ROPE_BASE ** (2.0 * jnp.arange(half, dtype=jnp.float32) / D_ROPE)
            delta = -2.0 * jnp.pi * jax.nn.sigmoid(raw_delta)
            angles_q = jnp.arange(L_, dtype=jnp.float32)[:, None] * theta[None, :] + delta
            query_r = _pope((c_q @ W_qr).reshape(B_, L_, N_HEAD, D_ROPE), angles_q[None, :, None, :])
            kr_sel = (x @ W_kr)[bi, idx]
            angles_k = jnp.arange(kk, dtype=jnp.float32)[:, None] * theta[None, :] + delta
            key_r = _pope(kr_sel, angles_k[None, None, :, :])
            scale = (D_HEAD + D_ROPE) ** (-0.5)
            q_c = query_c.transpose(0, 2, 1, 3)
            q_r = query_r.transpose(0, 2, 1, 3)
            k_c = key_c.transpose(0, 3, 1, 2, 4)
            v = value.transpose(0, 3, 1, 2, 4)
            scores = (jnp.einsum('bhld,bhlkd->bhlk', q_c, k_c) + jnp.einsum('bhld,blkd->bhlk', q_r, key_r)) * scale
            attn = jax.nn.softmax(scores.astype(jnp.float32), axis=-1).astype(v.dtype)
            out = jnp.einsum('bhlk,bhlkd->bhld', attn, v)
            out = out.transpose(0, 2, 1, 3).reshape(B_, L_, N_HEAD * D_HEAD)
            return out @ W_out
        key = jax.random.key(seed)
        ks = jax.random.split(key, 14)

        def w(k, shape, fan_in):
            return jax.random.normal(k, shape, dtype=jnp.float32) * fan_in ** (-0.5)
        return {'x': jax.random.normal(ks[0], (B, L, D_MODEL), dtype=jnp.float32), 'W_dkv': w(ks[1], (D_MODEL, D_CKV), D_MODEL), 'W_uk': w(ks[2], (D_CKV, N_HEAD * D_HEAD), D_CKV), 'W_uv': w(ks[3], (D_CKV, N_HEAD * D_HEAD), D_CKV), 'W_dq': w(ks[4], (D_MODEL, D_CQ), D_MODEL), 'W_uq': w(ks[5], (D_CQ, N_HEAD * D_HEAD), D_CQ), 'W_qr': w(ks[6], (D_CQ, N_HEAD * D_ROPE), D_CQ), 'W_kr': w(ks[7], (D_MODEL, D_ROPE), D_MODEL), 'W_out': w(ks[8], (N_HEAD * D_HEAD, D_MODEL), N_HEAD * D_HEAD), 'idx_wq': w(ks[9], (D_MODEL, N_IDX_HEAD * D_HEAD), D_MODEL), 'idx_wk': w(ks[10], (D_MODEL, D_HEAD), D_MODEL), 'idx_w': jnp.ones((N_IDX_HEAD,), dtype=jnp.float32), 'raw_delta': jax.random.normal(ks[11], (D_ROPE // 2,), dtype=jnp.float32) * 0.1}
    _L0_attn_in = _L0_attn_setup()

    def _L0_ffn_setup():
        import jax, jax.numpy as jnp
        import numpy as np
        B, S, H, I, E, K = (2, 64, 128, 64, 64, 8)
        key = jax.random.key(seed)
        ks = jax.random.split(key, 8)
        return {'hidden_states': jax.random.normal(ks[0], (B, S, H), dtype=jnp.float32), 'router_w': jax.random.normal(ks[1], (H, E), dtype=jnp.float32) * 0.02, 'shared_gate_w': jax.random.normal(ks[2], (H, I), dtype=jnp.float32) * 0.02, 'shared_up_w': jax.random.normal(ks[3], (H, I), dtype=jnp.float32) * 0.02, 'shared_down_w': jax.random.normal(ks[4], (I, H), dtype=jnp.float32) * 0.02, 'expert_gate_k': jax.random.normal(ks[5], (E, H, I), dtype=jnp.float32) * 0.02, 'expert_up_k': jax.random.normal(ks[6], (E, H, I), dtype=jnp.float32) * 0.02, 'expert_down_k': jax.random.normal(ks[7], (E, I, H), dtype=jnp.float32) * 0.02}
    _L0_ffn_in = _L0_ffn_setup()
    _d = {'L0_attn_x': _L0_attn_in['x'], 'L0_attn_W_dkv': _L0_attn_in['W_dkv'], 'L0_attn_W_uk': _L0_attn_in['W_uk'], 'L0_attn_W_uv': _L0_attn_in['W_uv'], 'L0_attn_W_dq': _L0_attn_in['W_dq'], 'L0_attn_W_uq': _L0_attn_in['W_uq'], 'L0_attn_W_qr': _L0_attn_in['W_qr'], 'L0_attn_W_kr': _L0_attn_in['W_kr'], 'L0_attn_W_out': _L0_attn_in['W_out'], 'L0_attn_idx_wq': _L0_attn_in['idx_wq'], 'L0_attn_idx_wk': _L0_attn_in['idx_wk'], 'L0_attn_idx_w': _L0_attn_in['idx_w'], 'L0_attn_raw_delta': _L0_attn_in['raw_delta'], 'L0_ffn_router_w': _L0_ffn_in['router_w'], 'L0_ffn_shared_gate_w': _L0_ffn_in['shared_gate_w'], 'L0_ffn_shared_up_w': _L0_ffn_in['shared_up_w'], 'L0_ffn_shared_down_w': _L0_ffn_in['shared_down_w'], 'L0_ffn_expert_gate_k': _L0_ffn_in['expert_gate_k'], 'L0_ffn_expert_up_k': _L0_ffn_in['expert_up_k'], 'L0_ffn_expert_down_k': _L0_ffn_in['expert_down_k']}
    _x0 = _d['L0_attn_x']
    _d['L0_attn_x'] = jax.random.normal(jax.random.fold_in(jax.random.key(seed), 1), (2, 1024, 128), dtype=_x0.dtype)
    del _x0
    return _d

def reference(L0_attn_x, L0_attn_W_dkv, L0_attn_W_uk, L0_attn_W_uv, L0_attn_W_dq, L0_attn_W_uq, L0_attn_W_qr, L0_attn_W_kr, L0_attn_W_out, L0_attn_idx_wq, L0_attn_idx_wk, L0_attn_idx_w, L0_attn_raw_delta, L0_ffn_router_w, L0_ffn_shared_gate_w, L0_ffn_shared_up_w, L0_ffn_shared_down_w, L0_ffn_expert_gate_k, L0_ffn_expert_up_k, L0_ffn_expert_down_k):

    def _L0_attn_ref(x, W_dkv, W_uk, W_uv, W_dq, W_uq, W_qr, W_kr, W_out, idx_wq, idx_wk, idx_w, raw_delta):
        import jax, jax.numpy as jnp
        import numpy as np
        B, L = (2, 128)
        D_MODEL, D_CKV, D_CQ = (128, 32, 64)
        N_HEAD, D_HEAD, D_ROPE = (8, 64, 32)
        N_IDX_HEAD = 4
        K_TS, LW = (96, 64)
        ROPE_BASE = 10000.0

        def _pope(x, angles):
            cos, sin = (jnp.cos(angles), jnp.sin(angles))
            mu1, mu2 = jnp.split(jax.nn.softplus(x), 2, axis=-1)
            return jnp.concatenate([mu1 * cos - mu2 * sin, mu1 * sin + mu2 * cos], axis=-1)

        def _forward(x, W_dkv, W_uk, W_uv, W_dq, W_uq, W_qr, W_kr, W_out, idx_wq, idx_wk, idx_w, raw_delta):
            B_, L_, _ = x.shape
            c_kv = x @ W_dkv
            q_i = (x @ idx_wq).reshape(B_, L_, N_IDX_HEAD, D_HEAD)
            k_i = x @ idx_wk
            s_i = jax.nn.relu(jnp.einsum('bthd,bsd->bths', q_i, k_i))
            I = jnp.einsum('bths,h->bts', s_i, idx_w)
            qpos = jnp.arange(L_)[:, None]
            kpos = jnp.arange(L_)[None, :]
            local = (kpos >= qpos - LW + 1) & (kpos <= qpos)
            causal = kpos > qpos
            I = jnp.where(local[None], jnp.inf, I)
            I = jnp.where(causal[None], -jnp.inf, I)
            kk = min(K_TS, L_)
            _, idx = jax.lax.top_k(I, kk)
            bi = jnp.arange(B_)[:, None, None]
            key_c = (c_kv @ W_uk)[bi, idx].reshape(B_, L_, kk, N_HEAD, D_HEAD)
            value = (c_kv @ W_uv)[bi, idx].reshape(B_, L_, kk, N_HEAD, D_HEAD)
            c_q = x @ W_dq
            query_c = (c_q @ W_uq).reshape(B_, L_, N_HEAD, D_HEAD)
            half = D_ROPE // 2
            theta = 1.0 / ROPE_BASE ** (2.0 * jnp.arange(half, dtype=jnp.float32) / D_ROPE)
            delta = -2.0 * jnp.pi * jax.nn.sigmoid(raw_delta)
            angles_q = jnp.arange(L_, dtype=jnp.float32)[:, None] * theta[None, :] + delta
            query_r = _pope((c_q @ W_qr).reshape(B_, L_, N_HEAD, D_ROPE), angles_q[None, :, None, :])
            kr_sel = (x @ W_kr)[bi, idx]
            angles_k = jnp.arange(kk, dtype=jnp.float32)[:, None] * theta[None, :] + delta
            key_r = _pope(kr_sel, angles_k[None, None, :, :])
            scale = (D_HEAD + D_ROPE) ** (-0.5)
            q_c = query_c.transpose(0, 2, 1, 3)
            q_r = query_r.transpose(0, 2, 1, 3)
            k_c = key_c.transpose(0, 3, 1, 2, 4)
            v = value.transpose(0, 3, 1, 2, 4)
            scores = (jnp.einsum('bhld,bhlkd->bhlk', q_c, k_c) + jnp.einsum('bhld,blkd->bhlk', q_r, key_r)) * scale
            attn = jax.nn.softmax(scores.astype(jnp.float32), axis=-1).astype(v.dtype)
            out = jnp.einsum('bhlk,bhlkd->bhld', attn, v)
            out = out.transpose(0, 2, 1, 3).reshape(B_, L_, N_HEAD * D_HEAD)
            return out @ W_out
        return _forward(x, W_dkv, W_uk, W_uv, W_dq, W_uq, W_qr, W_kr, W_out, idx_wq, idx_wk, idx_w, raw_delta)

    def _L0_ffn_ref(hidden_states, router_w, shared_gate_w, shared_up_w, shared_down_w, expert_gate_k, expert_up_k, expert_down_k):
        import jax, jax.numpy as jnp
        import numpy as np
        B, S, H, I, E, K = (2, 64, 128, 64, 64, 8)
        logits = jnp.einsum('bsh,he->bse', hidden_states.astype(jnp.float32), router_w)
        affinity = jax.nn.sigmoid(logits)
        top_scores, top_idx = jax.lax.top_k(affinity, K)
        top_w = top_scores / (jnp.sum(top_scores, axis=-1, keepdims=True) + 1e-09)
        one_hot = jax.nn.one_hot(top_idx, E, dtype=top_w.dtype)
        router_mask = jnp.einsum('bske,bsk->bse', one_hot, top_w).astype(hidden_states.dtype)
        shared = jnp.einsum('bsi,ih->bsh', jax.nn.silu(hidden_states @ shared_gate_w) * (hidden_states @ shared_up_w), shared_down_w)
        gate_out = jnp.einsum('bsh,ehi->bsei', hidden_states, expert_gate_k)
        up_out = jnp.einsum('bsh,ehi->bsei', hidden_states, expert_up_k)
        expert_act = jax.nn.silu(gate_out) * up_out
        routed = jnp.einsum('bsei,eih->bsh', expert_act * router_mask[..., None], expert_down_k)
        return shared + routed
    x = L0_attn_x
    x = x + 0.5 * _L0_ffn_ref(_layernorm(x, axis=-1), L0_ffn_router_w, L0_ffn_shared_gate_w, L0_ffn_shared_up_w, L0_ffn_shared_down_w, L0_ffn_expert_gate_k, L0_ffn_expert_up_k, L0_ffn_expert_down_k)
    x = x + _L0_attn_ref(_layernorm(x, axis=-1), L0_attn_W_dkv, L0_attn_W_uk, L0_attn_W_uv, L0_attn_W_dq, L0_attn_W_uq, L0_attn_W_qr, L0_attn_W_kr, L0_attn_W_out, L0_attn_idx_wq, L0_attn_idx_wk, L0_attn_idx_w, L0_attn_raw_delta)
    x = x + 0.5 * _L0_ffn_ref(_layernorm(x, axis=-1), L0_ffn_router_w, L0_ffn_shared_gate_w, L0_ffn_shared_up_w, L0_ffn_shared_down_w, L0_ffn_expert_gate_k, L0_ffn_expert_up_k, L0_ffn_expert_down_k)
    return x

_drawn_inputs = setup_inputs


def setup_inputs(seed=0):
    import zlib

    import numpy as np

    out = dict(_drawn_inputs(seed))
    spreads = {'L0_attn_idx_w': (1.0, 0.2)}
    factors = {'L0_attn_raw_delta': 8.0,
     'L0_ffn_router_w': 8.0,
     'L0_ffn_shared_gate_w': 6.805,
     'L0_ffn_shared_up_w': 7.08,
     'L0_ffn_shared_down_w': 6.744,
     'L0_ffn_expert_gate_k': 8.0,
     'L0_ffn_expert_up_k': 8.0,
     'L0_ffn_expert_down_k': 8.0}
    for name, (base, spread) in spreads.items():
        noise = np.random.default_rng([zlib.crc32(name.encode()), seed]).standard_normal(out[name].shape)
        drawn = base * np.exp(spread * noise) if base else spread * noise
        out[name] = jnp.asarray(drawn.astype(out[name].dtype))
    for name, factor in factors.items():
        out[name] = (out[name] * factor).astype(out[name].dtype)
    return out
```

```python
import concourse.bass as bass
from concourse import mybir
from contextlib import ExitStack

F32 = mybir.dt.float32
F32R = mybir.dt.float32r
BF16 = mybir.dt.bfloat16
FP16 = mybir.dt.float16
ALU = mybir.AluOpType
ACT = mybir.ActivationFunctionType
AX = mybir.AxisListType

B, L, D = 2, 1024, 128
NT = B * L // 128
EXPERTS, WIDE, TOPK = 64, 64, 8
CHUNK = 512
NC = B * L // CHUNK
PAIRS = EXPERTS // 2
LN_EPS = 1e-5
LOWEST = -3.0e38


def ffn_phase(nc, tag, x, x_out, w, const, banks):
    ctx = ExitStack()

    def sb(name, shape, dt):
        return ctx.enter_context(nc.sbuf_tensor(f"{name}_{tag}", shape, dt))

    def sem(name):
        return ctx.enter_context(nc.semaphore(f"{name}_{tag}"))

    with ctx:
        stat = sb("stat", [128, 4, NT], F32)
        xc = sb("xc", [128, NT, D], F32)
        sq = sb("sq", [128, NT, D], F32)
        xnT = sb("xnT", [128, NT * 128], F32)
        xhi = sb("xhi", [128, NT * 128], F32R)
        xlo = sb("xlo", [128, NT * 128], F32R)
        rw = sb("rw", [128, EXPERTS], F32)
        lg = sb("lg", [128, NT, EXPERTS], F32)
        rep = sb("rep", [128, NT, EXPERTS], F32)
        top = sb("top", [128, NT, 8], F32)
        aff = sb("aff", [128, NT, EXPERTS], F32)
        wsum = sb("wsum", [128, 2, NT], F32)
        wfull = sb("wfull", [128, NT, 2, 32], F32)
        wpart = sb("wpart", [128, NT, 2, 3, 32], BF16)
        maskT = sb("maskT", [97, 2, NT * 128], BF16)
        raw = [sb(f"raw{i}", [128, 3, 128], F32) for i in range(2)]
        whi = [sb(f"whi{i}", [128, 3, 128], F32R) for i in range(2)]
        wlo = [sb(f"wlo{i}", [128, 3, 128], F32R) for i in range(2)]
        silu = [sb(f"silu{i}", [128, CHUNK], F32) for i in range(2)]
        gated = [sb(f"gated{i}", [128, CHUNK], F32) for i in range(2)]
        act = [sb(f"act{i}", [128, CHUNK], F32) for i in range(2)]
        ahi = [sb(f"ahi{i}", [128, CHUNK], F32R) for i in range(4)]
        alo = [sb(f"alo{i}", [128, CHUNK], F32R) for i in range(4)]
        yT = sb("yT", [128, NT * 128], F32)

        acc = banks[0:4]
        gate_ps, up_ps, mask_ps = banks[4:6], banks[6], banks[7]
        LG = [banks[6], banks[7]]
        ident, identb, sel = const["ident"], const["identb"], const["sel"]

        router_loaded = sem("router_loaded")
        loaded = [sem(f"loaded{i}") for i in range(2)]
        split_done = sem("split_done")
        zeroed = sem("zeroed")
        ln = sem("ln")
        pool_turn = sem("pool_turn")
        squared = sem("squared")
        deviation = sem("deviation")
        xT_ready = sem("xT_ready")
        xT_raw = sem("xT_raw")
        xT_split = sem("xT_split")
        logits_ready = sem("logits_ready")
        logits_out = sem("logits_out")
        affinity_ready = sem("affinity_ready")
        dve_link = sem("dve_link")
        parts_ready = sem("parts_ready")
        maskT_ps = sem("maskT_ps")
        maskT_done = sem("maskT_done")
        gate_done = sem("gate_done")
        up_done = sem("up_done")
        mask_done = sem("mask_done")
        silu_done = sem("silu_done")
        gated_done = sem("gated_done")
        act_done = sem("act_done")
        ahi_done = sem("ahi_done")
        alo_done = sem("alo_done")
        down_done = sem("down_done")
        yT_done = sem("yT_done")
        y_done = sem("y_done")
        x_done = sem("x_done")

        LAG = 2

        blk = ctx.enter_context(nc.Block())

        @blk.sync
        def _(sp):
            sp.dma_start(rw[:, :], w["router"]).then_inc(router_loaded, 16)
            sp.wait_ge(zeroed, 1)
            sp.dma_start(raw[0][:, 0, 0:WIDE], w["sgate"]).then_inc(loaded[0], 16)
            sp.dma_start(raw[0][:, 1, 0:WIDE], w["sup"]).then_inc(loaded[0], 16)
            sp.dma_start(raw[0][0:WIDE, 2, :], w["sdown"]).then_inc(loaded[0], 16)

            def load(u, slot):
                if not (isinstance(u, int) and u < 2):
                    sp.wait_ge(split_done, 2 * (u - 1))
                g = w["gate"][bass.ds((u - 1) * 2, 2), :, :].rearrange("e h i -> h e i")
                v = w["up"][bass.ds((u - 1) * 2, 2), :, :].rearrange("e h i -> h e i")
                d = w["down"].rearrange("e i h -> (e i) h")[bass.ds((u - 1) * 128, 128), :]
                sp.dma_start(raw[slot][:, 0, :].rearrange("h (e i) -> h e i", e=2), g).then_inc(loaded[slot], 16)
                sp.dma_start(raw[slot][:, 1, :].rearrange("h (e i) -> h e i", e=2), v).then_inc(loaded[slot], 16)
                sp.dma_start(raw[slot][:, 2, :], d).then_inc(loaded[slot], 16)

            load(1, 1)
            load(2, 0)
            with sp.Fori(3, PAIRS, 2) as u:
                load(u, 1)
                load(u + 1, 0)

        @blk.gpsimd
        def _(pool):
            pool.memset(raw[0][:, :, :], 0.0).then_inc(zeroed, 1)

            def split(u, slot, n):
                pool.wait_ge(loaded[slot], 48 * n)
                if not (isinstance(u, int) and u < 2):
                    pool.wait_ge(down_done, 4 * (u - 1))
                pool.sem_inc(pool_turn, 1)
                pool.tensor_copy(whi[slot][:, :, :], raw[slot][:, :, :]).then_inc(split_done, 1)
                pool.wait_ge(split_done, 2 * u + 1)
                pool.tensor_tensor(wlo[slot][:, :, :], raw[slot][:, :, :], whi[slot][:, :, :].bitcast(F32),
                                   ALU.subtract).then_inc(split_done, 1)

            split(0, 0, 1)
            split(1, 1, 1)
            split(2, 0, 2)
            with pool.Fori(1, PAIRS // 2) as j:
                split(2 * j + 1, 1, j + 1)
                split(2 * j + 2, 0, j + 2)

        @blk.scalar
        def _(act_e):
            act_e.wait_ge(ln, 2)
            act_e.activation(sq[:, :, :], xc[:, :, :], ACT.Square).then_inc(squared, 1)
            act_e.wait_ge(ln, 4)
            act_e.activation(stat[:, 2, :], stat[:, 1, :], ACT.Sqrt).then_inc(deviation, 1)
            for c in range(NC):
                act_e.wait_ge(xT_ready, c + 1)
                act_e.activation(xnT[:, c * CHUNK:(c + 1) * CHUNK], gate_ps[c % 2][:, :], ACT.Copy).then_inc(xT_raw, 1)
            act_e.wait_ge(logits_out, 1)
            act_e.activation(aff[:, :, :], lg[:, :, :], ACT.Sigmoid).then_inc(affinity_ready, 1)
            for c in range(NC):
                act_e.wait_ge(maskT_ps, c + 1)
                act_e.activation(maskT[0:96, :, c * CHUNK:(c + 1) * CHUNK],
                                 gate_ps[c % 2][0:96, :].bitcast(BF16).rearrange("p (k t) -> p k t", k=2),
                                 ACT.Copy).then_inc(maskT_done, 1)

            def step(k, m):
                act_e.wait_ge(gate_done, k + 1)
                if not (isinstance(k, int) and k < 2):
                    act_e.wait_ge(gated_done, k - 1)
                act_e.activation(silu[m % 2][:, :], gate_ps[m % 2][:, :], ACT.Silu).then_inc(silu_done, 1)

            def high(k, m):
                act_e.wait_ge(act_done, k + 1)
                if not (isinstance(k, int) and k < 4):
                    act_e.wait_ge(down_done, k - 3)
                act_e.activation(ahi[m % 4][:, :], act[m % 2][:, :], ACT.Copy).then_inc(ahi_done, 1)

            step(0, 0)
            for k in range(1, 4):
                step(k, k)
                high(k - 1, k - 1)
            with act_e.Fori(0, PAIRS // 2) as j:
                for m in range(8):
                    k = 8 * j + (4 + m)
                    step(k, (4 + m) % 8)
                    high(k - 1, (3 + m) % 8)
            high(4 * PAIRS + 3, 3)
            for c in range(NC):
                act_e.wait_ge(down_done, 4 * PAIRS + c + 1)
                act_e.activation(yT[:, c * CHUNK:(c + 1) * CHUNK], acc[c][:, :], ACT.Copy, scale=0.5).then_inc(yT_done, 1)

        @blk.vector
        def _(dve):
            links = [0]

            def link(ins):
                links[0] += 1
                ins.then_inc(dve_link, 1)
                dve.wait_ge(dve_link, links[0])

            def over(ap):
                return ap.unsqueeze(2).broadcast_to([128, NT, D])

            link(dve.tensor_reduce(stat[:, 0, :], x, AX.X, ALU.add))
            link(dve.tensor_scalar(stat[:, 0, :], stat[:, 0, :], 1.0 / D, None, ALU.mult))
            dve.tensor_tensor(xc[:, :, :], x, over(stat[:, 0, :]), ALU.subtract).then_inc(ln, 2)
            dve.memset(maskT[96:97, :, :], 1.0)
            dve.wait_ge(squared, 1)
            link(dve.tensor_reduce(stat[:, 1, :], sq[:, :, :], AX.X, ALU.add))
            dve.tensor_scalar(stat[:, 1, :], stat[:, 1, :], 1.0 / D, LN_EPS, ALU.mult, ALU.add).then_inc(ln, 2)
            dve.wait_ge(deviation, 1)
            link(dve.reciprocal(stat[:, 3, :], stat[:, 2, :]))
            dve.tensor_tensor(xc[:, :, :], xc[:, :, :], over(stat[:, 3, :]), ALU.mult).then_inc(ln, 1)
            for c in range(NC):
                part = slice(c * CHUNK, (c + 1) * CHUNK)
                dve.wait_ge(xT_raw, c + 1)
                link(dve.tensor_copy(xhi[:, part], xnT[:, part]))
                dve.tensor_tensor(xlo[:, part], xnT[:, part], xhi[:, part].bitcast(F32),
                                  ALU.subtract).then_inc(xT_split, 1)
            for h in range(2):
                dve.wait_ge(logits_ready, h + 1)
                last = dve.tensor_copy(lg[:, 8 * h:8 * h + 8, :], LG[h][:, :].rearrange("p (t e) -> p t e", e=EXPERTS))
            last.then_inc(logits_out, 1)
            dve.wait_ge(logits_out, 1)
            for t in range(NT):
                last = dve.max(top[:, t, :], lg[:, t, :])
            link(last)
            for t in range(NT):
                last = dve.match_replace(rep[:, t, :], top[:, t, :], lg[:, t, :], LOWEST)
            link(last)
            link(dve.tensor_tensor(rep[:, :, :], rep[:, :, :], lg[:, :, :], ALU.is_lt))
            dve.wait_ge(affinity_ready, 1)
            link(dve.tensor_tensor(aff[:, :, :], aff[:, :, :], rep[:, :, :], ALU.mult))
            link(dve.tensor_reduce(wsum[:, 0, :], aff[:, :, :], AX.X, ALU.add))
            link(dve.tensor_scalar(wsum[:, 0, :], wsum[:, 0, :], 1e-9, None, ALU.add))
            link(dve.reciprocal(wsum[:, 1, :], wsum[:, 0, :]))
            scale = wsum[:, 1, :].unsqueeze(2).broadcast_to([128, NT, EXPERTS])
            link(dve.tensor_tensor(aff[:, :, :], aff[:, :, :], scale, ALU.mult))
            for c in range(2):
                src = aff[:, :, :].rearrange("p t (q c s) -> p c t q s", c=2, s=2)[:, c, :, :, :]
                last = dve.tensor_copy(wfull[:, :, c, :].rearrange("p t (q s) -> p t q s", s=2), src)
            link(last)
            full = wfull[:, :, :, :].rearrange("p t c e -> p (t c) e")
            part = [wpart[:, :, :, i, :].rearrange("p t c e -> p (t c) e") for i in range(3)]
            link(dve.tensor_copy(part[0], full))
            link(dve.tensor_tensor(full, full, part[0], ALU.subtract))
            link(dve.tensor_copy(part[1], full))
            link(dve.tensor_tensor(full, full, part[1], ALU.subtract))
            dve.tensor_copy(part[2], full).then_inc(parts_ready, 1)

            def gate_up(k, m):
                dve.wait_ge(silu_done, k + 1)
                dve.wait_ge(up_done, k + 1)
                if not (isinstance(k, int) and k < 2):
                    dve.wait_ge(act_done, k - 1)
                dve.tensor_tensor(gated[m % 2][:, :], silu[m % 2][:, :], up_ps[:, :], ALU.mult).then_inc(gated_done, 1)

            def weigh(k, m):
                dve.wait_ge(gated_done, k + 1)
                dve.wait_ge(mask_done, k + 1)
                if not (isinstance(k, int) and k < 2):
                    dve.wait_ge(alo_done, k - 1)
                dve.tensor_tensor(act[m % 2][:, :], gated[m % 2][:, :], mask_ps[:, :], ALU.mult).then_inc(act_done, 1)

            def low(k, m):
                dve.wait_ge(ahi_done, k + 1)
                dve.tensor_tensor(alo[m % 4][:, :], act[m % 2][:, :], ahi[m % 4][:, :].bitcast(F32),
                                  ALU.subtract).then_inc(alo_done, 1)

            gate_up(0, 0)
            weigh(0, 0)
            for k in range(1, 4):
                gate_up(k, k)
                low(k - 1, k - 1)
                weigh(k, k)
            with dve.Fori(0, PAIRS // 2) as j:
                for m in range(8):
                    k = 8 * j + (4 + m)
                    gate_up(k, (4 + m) % 8)
                    low(k - 1, (3 + m) % 8)
                    weigh(k, (4 + m) % 8)
            low(4 * PAIRS + 3, 3)
            for c in range(NC):
                dve.wait_ge(y_done, c + 1)
                dve.tensor_tensor(x_out[:, 4 * c:4 * c + 4, :], x[:, 4 * c:4 * c + 4, :],
                                  gate_ps[c % 2][:, :].rearrange("p (t d) -> p t d", t=4), ALU.add).then_inc(x_done, 1)

        @blk.tensor
        def _(pe):
            pe.wait_ge(ln, 5)
            for c in range(NC):
                if c >= 2:
                    pe.wait_ge(xT_raw, c - 1)
                for t in range(4):
                    last = pe.transpose(gate_ps[c % 2][:, t * 128:(t + 1) * 128], xc[:, 4 * c + t, :], ident)
                last.then_inc(xT_ready, 1)
            pe.wait_ge(xT_raw, NC)
            pe.wait_ge(router_loaded, 16)
            for t in range(NT):
                last = pe.matmul(LG[t // 8][:, (t % 8) * EXPERTS:(t % 8 + 1) * EXPERTS],
                                 xnT[:, t * 128:(t + 1) * 128], rw[:, :], start=True, stop=True)
                if t % 8 == 7:
                    last.then_inc(logits_ready, 1)
            pe.wait_ge(parts_ready, 1)
            pe.wait_ge(xT_split, NC)
            for c in range(NC):
                if c >= 2:
                    pe.wait_ge(maskT_done, c - 1)
                for k in range(2):
                    for t in range(4):
                        out = gate_ps[c % 2][0:96, :].bitcast(BF16)[:, (4 * k + t) * 128:(4 * k + t + 1) * 128]
                        last = pe.transpose(out, wpart[:, 4 * c + t, k, :, :].rearrange("p a e -> p (a e)"), identb)
                last.then_inc(maskT_ps, 1)
            pe.wait_ge(maskT_done, NC)

            def triple(out, i, slot, hi, lo, first, last):
                pe.matmul(out, whi[slot][:, i, :], hi, start=first, stop=False)
                pe.matmul(out, whi[slot][:, i, :], lo, start=False, stop=False)
                return pe.matmul(out, wlo[slot][:, i, :], hi, start=False, stop=last)

            def up_step(slot, c, k, m):
                cs = slice(c * CHUNK, (c + 1) * CHUNK)
                static = isinstance(k, int)
                if not (static and k < 2):
                    pe.wait_ge(silu_done, k - 1)
                triple(gate_ps[m % 2][:, :], 0, slot, xhi[:, cs], xlo[:, cs], True, True).then_inc(gate_done, 1)
                if not (static and k < 1):
                    pe.wait_ge(gated_done, k)
                triple(up_ps[:, :], 1, slot, xhi[:, cs], xlo[:, cs], True, True).then_inc(up_done, 1)

            def mask_step(q, parity, c, k):
                if not (isinstance(k, int) and k < 1):
                    pe.wait_ge(act_done, k)
                cs = slice(c * CHUNK, (c + 1) * CHUNK)
                pe.matmul(mask_ps[:, :], sel[:, bass.ds(q, 1), :].rearrange("p a m -> p (a m)"),
                          maskT[:, parity, cs], start=True, stop=True).then_inc(mask_done, 1)

            def down_step(slot, c, k, m, first=False, last=False):
                pe.wait_ge(alo_done, k + 1)
                done = triple(acc[c][:, :], 2, slot, ahi[m % 4][:, :], alo[m % 4][:, :], first, last)
                done.then_inc(down_done, 1)
                return done

            pe.wait_ge(split_done, 2)
            for c in range(4):
                up_step(0, c, c, c)
                mask_step(PAIRS // 2, 0, c, c)
                if c >= LAG:
                    down_step(0, c - LAG, c - LAG, c - LAG, first=True)

            def body(j, first=False, last=False):
                for m in range(8):
                    du, c = divmod(m, 4)
                    k = 8 * j + (4 + m)
                    if c == 0:
                        pe.wait_ge(split_done, 4 * j + (4 + 2 * du))
                    up_step(1 - du, c, k, m + 4)
                    mask_step(j, du, c, k)
                    slot = (1 - du) if c >= LAG else du
                    down_step(slot, (c - LAG) % 4, k - LAG, (m + 4 - LAG) % 8,
                              first=first and m < LAG, last=last and m >= 4 + LAG)

            body(0, first=True)
            with pe.Fori(1, PAIRS // 2 - 1) as j:
                body(j)
            body(PAIRS // 2 - 1, last=True)
            for c in (2, 3):
                down_step(0, c, 4 * PAIRS + c, c, last=True)
            for c in range(NC):
                pe.wait_ge(yT_done, c + 1)
                if c >= 2:
                    pe.wait_ge(x_done, c - 1)
                for t in range(4):
                    s = (4 * c + t) * 128
                    last = pe.transpose(gate_ps[c % 2][:, t * 128:(t + 1) * 128], yT[:, s:s + 128], ident)
                last.then_inc(y_done, 1)


HEADS, WIDTH = 8, 64
C, R = 32, 32
CQ = 64
IDX_HEADS = 4
FAR, LOCAL = 32, 64
TILES = L // 128
BLK = 16
PAIRS_B = 4
WIN = BLK + LOCAL
HEAD_KEYS = 96
SPAN = WIN + 128
GROUPS = 32
SCALE = (WIDTH + R) ** -0.5
PI = 3.14159265358979
OUT = -1.0e30
Q4 = R // 2


def width(i):
    return 128 if i == 0 else 128 * i + 64


def halves(i):
    return [(s, min(s + 512, width(i))) for s in range(0, width(i), 512)]


def plan():
    a_tasks, v_tasks = [], []
    for i in range(-2, TILES):
        n, nn = i + 1, i + 2
        if nn < TILES:
            a_tasks.append(("qi", nn))
            a_tasks += [("score", nn, s, h) for s in range(len(halves(nn))) for h in range(IDX_HEADS)]
        if 0 <= n < TILES:
            a_tasks += [("cq", n), ("qabs", n)]
        for p in range(PAIRS_B):
            if i >= 0:
                v_tasks.append(("S", i, p))
            if 0 <= n < TILES:
                v_tasks += [("gather", n, 4 * p + g) for g in range(4)]
            if i >= 0:
                a_tasks.append(("PT", i, p))
                v_tasks.append(("ctx", i, p))
            if 0 <= n < TILES:
                a_tasks += [("GT", n, 2 * p + g) for g in range(2)]
        if i >= 0:
            v_tasks.append(("out", i))
        if 0 <= n < TILES:
            a_tasks += [("QT", n, h) for h in range(2)]
    return ({k: u for u, k in enumerate(a_tasks)}, len(a_tasks), {k: u for u, k in enumerate(v_tasks)}, len(v_tasks))


def _attn_constants():
    import numpy as np
    theta = (1.0 / np.float32(10000.0) ** (2.0 * np.arange(Q4, dtype=np.float32) / R)).astype(np.float32)
    t = np.arange(L).reshape(TILES, 128).T
    angle = np.zeros((128, 2 * TILES + 1, Q4))
    angle[:, :TILES] = (t[:, :, None].astype(np.float32) * theta).astype(np.float32)
    angle[:, TILES:2 * TILES] = (t + np.maximum(t - (LOCAL - 1), 0))[:, :, None] * theta.astype(np.float64)
    rank = LOCAL + np.arange(128) % FAR
    angle[:, 2 * TILES] = (rank[:, None].astype(np.float32) * theta).astype(np.float32)
    trig = np.stack([np.cos(angle), np.sin(angle)], 2).astype(np.float32)
    p, c = np.arange(128)[:, None], np.arange(128)[None, :]
    late = np.where(c <= p, 0.0, LOWEST).astype(np.float32)
    early = np.where(c > p, OUT * (1 + c / 1024.0), LOWEST)
    early = np.where(c <= p - LOCAL, 0.0, early).astype(np.float32)
    q = p // HEADS
    w = np.arange(WIN)[None, :]
    near = np.where((w >= q + 1) & (w <= q + LOCAL), 0.0, OUT)
    far = np.where((p // 32 == p // 32) & (c // FAR == q % 4), 0.0, OUT)
    s = 128 * np.arange(TILES)[None, :] + p
    return {"trig": trig, "late": late, "early": early, "smask": np.concatenate([near, far], 1).astype(np.float32),
            "keyno": s.astype(np.float32)}



VLINKS, GLINKS = 20 * TILES, 7 * TILES


class Count:

    def __init__(self, handle, per):
        self.h, self.per = handle, per

    def wait(self, eng, b, n):
        eng.wait_ge(self.h, b * self.per + n)


def attn_loop(nc, t, x, x_out, ident, xnT, kiT, wiq, wdq, keyT, ctab, muq_dram, trig, absorb, wvo, idxw, late, early, smask,
              keyno, cpad, idx_dram, RA, RV, A_AT, A_N, V_AT, V_N):
    ctx = ExitStack()

    def sb(name, shape, dt):
        return ctx.enter_context(nc.sbuf_tensor(name, shape, dt))

    def sem(name, per):
        return Count(ctx.enter_context(nc.semaphore(name)), per)

    with ctx:
        hot = sb("hot", [128, TILES, GROUPS, 128], BF16)
        idxb = sb("idxb", [128, 128 * FAR], FP16)
        relu = [sb(f"relu{i}", [128, 512], F32) for i in range(2)]
        score = [sb(f"score{i}", [128, L], F32) for i in range(2)]
        best = sb("best", [128, 4, 8], F32)
        which = sb("which", [128, 4, 8], mybir.dt.uint16)
        idx16 = [sb(f"idx16_{i}", [128, FAR], FP16) for i in range(2)]
        G = [sb(f"G{i}", [128, GROUPS, 64], F32) for i in range(2)]
        tmp = [sb(f"tmp{i}", [128, 8, Q4], F32) for i in range(4)]
        muq = [sb(f"muq{i}", [128, HEADS, R], F32) for i in range(2)]
        QI = sb("QI", [64, IDX_HEADS, 128], F32)
        CQT = sb("CQT", [CQ, 128], F32)
        GT = sb("GT", [64, GROUPS * 128], F32)
        QN = sb("QN", [128, HEADS, 96], F32)
        QT = sb("QT", [96, 128, HEADS], F32)
        S = [sb(f"S{i}", [128, 2, SPAN], F32) for i in range(2)]
        P = [sb(f"P{i}", [128, 2, SPAN], F32) for i in range(2)]
        small = [sb(f"small{i}", [128, 4, 2], F32) for i in range(2)]
        PT = [sb(f"PT{i}", [128, 4, 128], F32) for i in range(2)]
        CT = sb("CT", [C, 128, HEADS], F32)
        cwin = [sb(f"cwin{i}", [WIN, 8, C], F32) for i in range(2)]
        chead = sb("chead", [HEAD_KEYS, C], F32)

        n_steps = sum(len(halves(i)) for i in range(TILES)) * IDX_HEADS
        steps_before = [IDX_HEADS * sum(len(halves(j)) for j in range(i)) for i in range(TILES + 1)]
        a_filled, a_emptied = sem("a_filled", A_N), sem("a_emptied", A_N)
        v_filled, v_emptied = sem("v_filled", V_N), sem("v_emptied", V_N)
        added = sem("added", n_steps)
        picked = sem("picked", TILES)
        idx_stored, idx_loaded = sem("idx_stored", 16 * TILES), sem("idx_loaded", 16 * TILES)
        hot_ready = sem("hot_ready", TILES)
        muq_loaded = [sem(f"muq_loaded{i}", 16 * TILES // 2) for i in range(2)]
        win_loaded = [sem(f"win_loaded{i}", 80 * TILES // 2) for i in range(2)]
        head_loaded = sem("head_loaded", 16)
        g_rotated = sem("g_rotated", TILES * 4)
        q_rotated = sem("q_rotated", TILES)
        biased = sem("biased", TILES * PAIRS_B)
        expd = sem("expd", TILES * PAIRS_B)
        weighed = sem("weighed", TILES * PAIRS_B)
        batch_end = sem("batch_end", 5)
        vlink = sem("vlink", VLINKS)
        glink = sem("glink", GLINKS)
        turns = {e: ctx.enter_context(nc.semaphore(f"turn_{e}")) for e in ("pe", "dve", "sp")}

        blk = ctx.enter_context(nc.Block())

        def far_pairs(i):
            return range(PAIRS_B) if i > 0 else range(LOCAL // (2 * BLK), PAIRS_B)

        def last_score(i):
            return A_AT[("score", i, len(halves(i)) - 1, IDX_HEADS - 1)]

        def close(eng, b):
            eng.sem_inc(batch_end.h, 1)
            eng.wait_ge(batch_end.h, b * 5 + 5)

        @blk.sync
        def _(sp):
            def settle():
                sp.sem_inc(turns["sp"], 1)

            with sp.Fori(0, B) as b:
                sp.dma_start(chead[:, :], cpad[bass.ds(b, 1), 64:64 + HEAD_KEYS, :]).then_inc(head_loaded.h, 16)
                for i in range(-2, TILES):
                    n = i + 1
                    if 0 <= n < TILES:
                        if n >= 2:
                            v_emptied.wait(sp, b, V_AT[("ctx", n - 2, PAIRS_B - 1)] + 1)
                            settle()
                        for m in range(WIN // BLK):
                            lo = 128 * n + BLK * m
                            sp.dma_start(cwin[n % 2][BLK * m:BLK * (m + 1), :, :],
                                         cpad[bass.ds(b, 1), lo:lo + 128, :].rearrange("a (k p) c -> p (a k) c", p=BLK)
                                         ).then_inc(win_loaded[n % 2].h, 16)
                        if n >= 2:
                            q_rotated.wait(sp, b, n - 1)
                            settle()
                        sp.dma_start(muq[n % 2][:, :, :].rearrange("p h r -> p (h r)"),
                                     muq_dram[bass.ds(b * TILES + n, 1), :, :].rearrange("a p c -> p (a c)")
                                     ).then_inc(muq_loaded[n % 2].h, 16)
                    if i + 2 < TILES:
                        m = i + 2
                        picked.wait(sp, b, m + 1)
                        settle()
                        sp.dma_start(idx_dram[m % 2, :].rearrange("(p r) -> p r", r=FAR),
                                     idx16[m % 2][:, :]).then_inc(idx_stored.h, 16)
                        idx_stored.wait(sp, b, 16 * (m + 1))
                        settle()
                        if m >= 1:
                            hot_ready.wait(sp, b, m)
                            settle()
                        sp.dma_start(idxb[:, :], idx_dram[m % 2, :].partition_broadcast(128)).then_inc(idx_loaded.h, 16)
                close(sp, b)
                settle()

        @blk.gpsimd
        def _(pool):
            with pool.Fori(0, B) as b:
                links = [0]

                def link(ins):
                    links[0] += 1
                    ins.then_inc(glink.h, 1)
                    glink.wait(pool, b, links[0])

                def rotate(dst, src, k, n):
                    co, si = (trig[:, k, j, :].unsqueeze(1).broadcast_to([128, n, Q4]) for j in range(2))
                    m1, m2 = src[:, :, 0:Q4], src[:, :, Q4:R]
                    for out, m, a in ((0, m1, co), (1, m2, si), (2, m1, si), (3, m2, co)):
                        last = pool.tensor_tensor(tmp[out][:, 0:n, :], m, a, ALU.mult)
                    link(last)
                    pool.tensor_tensor(dst[:, :, 0:Q4], tmp[0][:, 0:n, :], tmp[1][:, 0:n, :], ALU.subtract)
                    return pool.tensor_tensor(dst[:, :, Q4:R], tmp[2][:, 0:n, :], tmp[3][:, 0:n, :], ALU.add)

                for n in range(TILES):
                    muq_loaded[n % 2].wait(pool, b, 16 * (n // 2 + 1))
                    if n >= 1:
                        a_emptied.wait(pool, b, A_AT[("QT", n - 1, 1)] + 1)
                    link(rotate(QN[:, :, 32:64], muq[n % 2], n, HEADS))
                    rotate(QN[:, :, 64:96], muq[n % 2], TILES + n, HEADS).then_inc(q_rotated.h, 1)
                    q_rotated.wait(pool, b, n + 1)
                    for p in range(4):
                        v_emptied.wait(pool, b, V_AT[("gather", n, 4 * p + 3)] + 1)
                        g = G[n % 2][:, 8 * p:8 * p + 8, C:]
                        rotate(g, g, 2 * TILES, 8).then_inc(g_rotated.h, 1)
                        g_rotated.wait(pool, b, 4 * n + p + 1)
                assert links[0] == GLINKS, links[0]
                close(pool, b)

        @blk.scalar
        def _(act):
            with act.Fori(0, B) as b:
                step = [0]

                def empty(key, dst, src, func=ACT.Copy):
                    a_filled.wait(act, b, A_AT[key] + 1)
                    act.activation(dst, src, func).then_inc(a_emptied.h, 1)

                def ring(key):
                    return RA[A_AT[key] % 4]

                def scores(i):
                    for s, (lo, hi) in enumerate(halves(i)):
                        for h in range(IDX_HEADS):
                            k = step[0]
                            if k >= 2:
                                added.wait(act, b, k - 1)
                            empty(("score", i, s, h), relu[k % 2][:, 0:hi - lo], ring(("score", i, s, h))[:, 0:hi - lo],
                                  ACT.Relu)
                            step[0] += 1

                for i in range(-2, TILES):
                    n, nn = i + 1, i + 2
                    if nn < TILES:
                        key = ("qi", nn)
                        if nn >= 1:
                            a_emptied.wait(act, b, last_score(nn - 1) + 1)
                        empty(key, QI[:, :, :], ring(key)[0:64, :].rearrange("p (h t) -> p h t", h=IDX_HEADS))
                        scores(nn)
                    if 0 <= n < TILES:
                        if n >= 1:
                            a_emptied.wait(act, b, A_AT[("QT", n - 1, 1)] + 1)
                        empty(("cq", n), CQT[:, :], ring(("cq", n))[0:CQ, 0:128])
                        key = ("qabs", n)
                        empty(key, QN[:, :, 0:C], ring(key)[:, 0:256].rearrange("p (h c) -> p h c", c=C))
                    for p in range(PAIRS_B):
                        if i >= 0:
                            u = PAIRS_B * i + p
                            biased.wait(act, b, u + 1)
                            if u >= 2:
                                weighed.wait(act, b, u - 1)
                            w = SPAN if p in far_pairs(i) else HEAD_KEYS
                            for k in range(2):
                                last = act.activation(P[u % 2][:, k, 0:w], S[u % 2][:, k, 0:w], ACT.Exp, scale=SCALE,
                                                      bias=small[u % 2][:, 1, k:k + 1],
                                                      accum_out=small[u % 2][:, 2, k:k + 1])
                            last.then_inc(expd.h, 1)
                            key = ("PT", i, p)
                            a_filled.wait(act, b, A_AT[key] + 1)
                            if u >= 2:
                                v_emptied.wait(act, b, V_AT[("ctx", (u - 2) // PAIRS_B, (u - 2) % PAIRS_B)] + 1)
                            if p in far_pairs(i):
                                act.activation(PT[u % 2][0:WIN, 0:2, :],
                                               ring(key)[0:WIN, 0:256].rearrange("p (k t) -> p k t", k=2),
                                               ACT.Copy)
                                act.activation(PT[u % 2][:, 2:4, :], ring(key)[:, 256:512].rearrange(
                                    "p (k t) -> p k t", k=2), ACT.Copy).then_inc(a_emptied.h, 1)
                            else:
                                act.activation(PT[u % 2][0:HEAD_KEYS, 0:2, :],
                                               ring(key)[0:HEAD_KEYS, 0:256].rearrange("p (k t) -> p k t", k=2),
                                               ACT.Copy).then_inc(a_emptied.h, 1)
                        if 0 <= n < TILES:
                            for g in range(2):
                                q = 2 * p + g
                                if n >= 1:
                                    v_emptied.wait(act, b, V_AT[("S", i, p)] + 1)
                                empty(("GT", n, q), GT[:, q * 512:(q + 1) * 512], ring(("GT", n, q))[0:64, :])
                    if 0 <= n < TILES:
                        for h in range(2):
                            if n >= 1:
                                v_emptied.wait(act, b, V_AT[("S", i, PAIRS_B - 1)] + 1)
                            key = ("QT", n, h)
                            empty(key, QT[:, :, 4 * h:4 * h + 4],
                                  ring(key)[0:96, :].rearrange("c (h t) -> c t h", h=4))
                close(act, b)

        @blk.vector
        def _(dve):
            with dve.Fori(0, B) as b:
                links, step = [0], [0]

                def link(ins):
                    links[0] += 1
                    ins.then_inc(vlink.h, 1)
                    vlink.wait(dve, b, links[0])

                def settle():
                    dve.sem_inc(turns["dve"], 1)

                def ring(key):
                    v_filled.wait(dve, b, V_AT[key] + 1)
                    return RV[V_AT[key] % 4]

                def add_scores(i):
                    I = score[i % 2]
                    for s, (lo, hi) in enumerate(halves(i)):
                        for h in range(IDX_HEADS):
                            k = step[0]
                            a_emptied.wait(dve, b, A_AT[("score", i, s, h)] + 1)
                            r = relu[k % 2][:, 0:hi - lo]
                            if h == 0:
                                ins = dve.tensor_scalar(I[:, lo:hi], r, idxw[:, 0:1], None, ALU.mult)
                            else:
                                ins = dve.scalar_tensor_tensor(I[:, lo:hi], r, idxw[:, h:h + 1], I[:, lo:hi],
                                                               ALU.mult, ALU.add)
                            ins.then_inc(added.h, 1)
                            added.wait(dve, b, k + 1)
                            step[0] += 1
                    w = width(i)
                    link(dve.tensor_tensor(I[:, w - 128:w], I[:, w - 128:w], (late if i else early)[:, :], ALU.add))

                def pick(i, r):
                    I = score[i % 2][:, 0:width(i)]
                    settle()
                    link(dve.max(best[:, r, :], I))
                    settle()
                    link(dve.max_index(which[:, r, :], best[:, r, :], I))
                    if r < 3:
                        settle()
                        link(dve.match_replace(I, best[:, r, :], I, LOWEST * 1.1))
                    else:
                        if i >= 2:
                            idx_stored.wait(dve, b, 16 * (i - 1))
                        dve.tensor_copy(idx16[i % 2][:, :], which[:, :, :].rearrange("p a k -> p (a k)")).then_inc(
                            picked.h, 1)

                def one_hot(i):
                    idx_loaded.wait(dve, b, 16 * (i + 1))
                    if i >= 1:
                        v_filled.wait(dve, b, V_AT[("gather", i - 1, 15)] + 1)
                    for j in range(i + 1):
                        last = dve.tensor_scalar(hot[:, j, :, :].rearrange("p g q -> p (g q)"), idxb[:, :],
                                                 keyno[:, j:j + 1], None, ALU.is_equal)
                    last.then_inc(hot_ready.h, 1)

                for i in range(-2, TILES):
                    n, nn = i + 1, i + 2
                    if 0 <= n < TILES:
                        one_hot(n)
                    if nn < TILES:
                        add_scores(nn)
                    for p in range(PAIRS_B):
                        if i >= 0:
                            u = PAIRS_B * i + p
                            s, f = S[u % 2], small[u % 2]
                            far = p in far_pairs(i)
                            w = SPAN if far else HEAD_KEYS
                            ps = ring(("S", i, p))[:, 0:2 * w].rearrange("p (k c) -> p k c", k=2)
                            if u >= 2:
                                expd.wait(dve, b, u - 1)
                            if far:
                                ins = dve.tensor_tensor(s[:, :, 0:w], ps,
                                                        smask[:, :].unsqueeze(1).broadcast_to([128, 2, w]), ALU.add)
                            else:
                                ins = dve.tensor_copy(s[:, :, 0:w], ps)
                            ins.then_inc(v_emptied.h, 1)
                            v_emptied.wait(dve, b, V_AT[("S", i, p)] + 1)
                            link(dve.tensor_reduce(f[:, 0, :], s[:, :, 0:w], AX.X, ALU.max))
                            dve.tensor_scalar(f[:, 1, :], f[:, 0, :], -SCALE, None, ALU.mult).then_inc(biased.h, 1)
                        if 0 <= n < TILES:
                            for g in range(4 * p, 4 * p + 4):
                                key = ("gather", n, g)
                                ps = ring(key)[:, 0:384].rearrange("p (g a d) -> p g d a", g=2, a=3)
                                if n >= 2 and g % 4 == 0:
                                    v_emptied.wait(dve, b, V_AT[("ctx", n - 2, PAIRS_B - 1)] + 1)
                                    a_emptied.wait(dve, b, A_AT[("GT", n - 2, 7)] + 1)
                                dve.tensor_reduce(G[n % 2][:, 2 * g:2 * g + 2, 0:64], ps, AX.X, ALU.add).then_inc(
                                    v_emptied.h, 1)
                        if nn < TILES:
                            pick(nn, p)
                        if i >= 0:
                            expd.wait(dve, b, u + 1)
                            link(dve.reciprocal(f[:, 3, :], f[:, 2, :]))
                            for k in range(2):
                                ins = dve.tensor_scalar(P[u % 2][:, k, 0:w], P[u % 2][:, k, 0:w], f[:, 3, k:k + 1],
                                                        None, ALU.mult)
                            ins.then_inc(weighed.h, 1)
                            key = ("ctx", i, p)
                            ps = ring(key)[0:C, 0:256].rearrange("c (t h) -> c t h", h=HEADS)
                            if i >= 1 and p == 0:
                                v_filled.wait(dve, b, V_AT[("out", i - 1)] + 1)
                            dve.tensor_copy(CT[:, 32 * p:32 * p + 32, :], ps).then_inc(v_emptied.h, 1)
                    if i >= 0:
                        o = ring(("out", i))
                        at = bass.ds(b * TILES + i, 1)
                        dve.tensor_tensor(x_out[:, at, :].rearrange("p a d -> p (a d)"),
                                          x[:, at, :].rearrange("p a d -> p (a d)"), o[:, 0:D],
                                          ALU.add).then_inc(v_emptied.h, 1)
                assert links[0] == VLINKS, links[0]
                close(dve, b)

        @blk.tensor
        def _(pe):
            with pe.Fori(0, B) as b:
                def settle():
                    pe.sem_inc(turns["pe"], 1)

                def ra(key):
                    u = A_AT[key]
                    if u >= 4:
                        a_emptied.wait(pe, b, u - 3)
                    return RA[u % 4]

                def rv(key):
                    u = V_AT[key]
                    if u >= 4:
                        v_emptied.wait(pe, b, u - 3)
                    return RV[u % 4]

                for i in range(-2, TILES):
                    n, nn = i + 1, i + 2
                    if nn < TILES:
                        o = ra(("qi", nn))
                        tokens = xnT[:, bass.ds(b * L + 128 * nn, 128)]
                        settle()
                        for h in range(IDX_HEADS):
                            last = pe.matmul(o[0:64, h * 128:(h + 1) * 128], wiq[:, 64 * h:64 * h + 64], tokens,
                                             start=True, stop=True)
                        last.then_inc(a_filled.h, 1)
                        a_emptied.wait(pe, b, A_AT[("qi", nn)] + 1)
                        for s, (lo, hi) in enumerate(halves(nn)):
                            for h in range(IDX_HEADS):
                                o = ra(("score", nn, s, h))
                                settle()
                                pe.matmul(o[:, 0:hi - lo], QI[:, h, :], kiT[:, bass.ds(b * L + lo, hi - lo)],
                                          start=True, stop=True).then_inc(a_filled.h, 1)
                    if 0 <= n < TILES:
                        o = ra(("cq", n))
                        settle()
                        pe.matmul(o[0:CQ, 0:128], wdq[:, :], xnT[:, bass.ds(b * L + 128 * n, 128)],
                                  start=True, stop=True).then_inc(a_filled.h, 1)
                        o = ra(("qabs", n))
                        a_emptied.wait(pe, b, A_AT[("cq", n)] + 1)
                        pe.matmul(o[:, 0:256], CQT[:, :], absorb[:, :, :].rearrange("k h c -> k (h c)"),
                                  start=True, stop=True).then_inc(a_filled.h, 1)
                    for p in range(PAIRS_B):
                        u = PAIRS_B * i + p
                        far = i >= 0 and p in far_pairs(i)
                        w = SPAN if far else HEAD_KEYS
                        if i >= 0:
                            o = rv(("S", i, p))
                            if p == 0:
                                a_emptied.wait(pe, b, A_AT[("QT", i, 1)] + 1)
                            for k in range(2):
                                blk_no = 2 * p + k
                                q = QT[:, blk_no * BLK:(blk_no + 1) * BLK, :].rearrange("c t h -> c (t h)")
                                if far:
                                    lo = 128 * i + BLK * blk_no
                                    last = pe.matmul(o[:, k * w:k * w + WIN], q, keyT[:, bass.ds(b, 1), lo:lo + WIN]
                                                     .rearrange("c a s -> c (a s)"), start=True, stop=True)
                                    for g in range(4):
                                        at = (4 * blk_no + g) * 128
                                        last = pe.matmul(o[32 * g:32 * g + 32, k * w + WIN:(k + 1) * w],
                                                         q[0:64, 32 * g:32 * g + 32], GT[:, at:at + 128],
                                                         start=True, stop=True)
                                else:
                                    last = pe.matmul(o[:, k * w:(k + 1) * w], q, keyT[:, bass.ds(b, 1), 64:64 + w]
                                                     .rearrange("c a s -> c (a s)"), start=True, stop=True)
                            last.then_inc(v_filled.h, 1)
                        if 0 <= n < TILES:
                            if p == 0:
                                hot_ready.wait(pe, b, n + 1)
                            for g in range(4 * p, 4 * p + 4):
                                o = rv(("gather", n, g))
                                for k in range(2):
                                    for j in range(n + 1):
                                        last = pe.matmul(o[:, 192 * k:192 * k + 192], hot[:, j, 2 * g + k, :],
                                                         ctab[:, bass.ds(b * TILES + j, 1), :, :]
                                                         .rearrange("s a k d -> s (a k d)"),
                                                         start=(j == 0), stop=(j == n))
                                last.then_inc(v_filled.h, 1)
                        if i >= 0:
                            weighed.wait(pe, b, u + 1)
                            o = ra(("PT", i, p))
                            for k in range(2):
                                m = WIN if far else HEAD_KEYS
                                last = pe.transpose(o[0:m, 128 * k:128 * k + 128], P[u % 2][:, k, 0:m], ident)
                            if far:
                                for k in range(2):
                                    last = pe.transpose(o[:, 256 + 128 * k:384 + 128 * k], P[u % 2][:, k, WIN:SPAN],
                                                        ident)
                            last.then_inc(a_filled.h, 1)
                            o = rv(("ctx", i, p))
                            a_emptied.wait(pe, b, A_AT[("PT", i, p)] + 1)
                            if p == 0:
                                win_loaded[i % 2].wait(pe, b, 80 * (i // 2 + 1))
                                if i == 0:
                                    head_loaded.wait(pe, b, 16)
                            for k in range(2):
                                blk_no = 2 * p + k
                                part = slice(128 * k, 128 * k + 128)
                                if not far:
                                    last = pe.matmul(o[0:C, part], chead[:, :], PT[u % 2][0:HEAD_KEYS, k, :],
                                                     start=True, stop=True)
                                    continue
                                pe.matmul(o[0:C, part], cwin[i % 2][:, blk_no, :], PT[u % 2][0:WIN, k, :],
                                          start=True, stop=False)
                                for g in range(4):
                                    last = pe.matmul(o[0:C, 128 * k + 32 * g:128 * k + 32 * g + 32],
                                                     G[i % 2][:, 4 * blk_no + g, 0:C],
                                                     PT[u % 2][:, 2 + k, 32 * g:32 * g + 32],
                                                     start=False, stop=(g == 3))
                            last.then_inc(v_filled.h, 1)
                        if 0 <= n < TILES:
                            g_rotated.wait(pe, b, 4 * n + p + 1)
                            for g in range(2):
                                o = ra(("GT", n, 2 * p + g))
                                settle()
                                for k in range(4):
                                    m = 8 * p + 4 * g + k
                                    last = pe.transpose(o[0:64, 128 * k:128 * k + 128], G[n % 2][:, m, :], ident)
                                last.then_inc(a_filled.h, 1)
                    if i >= 0:
                        o = rv(("out", i))
                        v_emptied.wait(pe, b, V_AT[("ctx", i, PAIRS_B - 1)] + 1)
                        for h in range(HEADS):
                            last = pe.matmul(o[:, 0:D], CT[:, :, h], wvo[:, h, :], start=(h == 0), stop=(h == HEADS - 1))
                        last.then_inc(v_filled.h, 1)
                    if 0 <= n < TILES:
                        q_rotated.wait(pe, b, n + 1)
                        for h in range(2):
                            o = ra(("QT", n, h))
                            if h == 0:
                                a_emptied.wait(pe, b, A_AT[("qabs", n)] + 1)
                            for k in range(4):
                                last = pe.transpose(o[0:96, 128 * k:128 * k + 128], QN[:, 4 * h + k, :], ident)
                            last.then_inc(a_filled.h, 1)
                close(pe, b)


def attn_phase(nc, t, x, x_out, const, banks):
    ctx = ExitStack()

    def sb(name, shape, dt):
        return ctx.enter_context(nc.sbuf_tensor(name, shape, dt))

    def sem(name):
        return ctx.enter_context(nc.semaphore(name))

    A_AT, A_N, V_AT, V_N = plan()
    with ctx:
        ident = const["ident"]
        kiT = sb("kiT", [64, NT * 128], F32)
        xnT = sb("a_xnT", [128, NT * 128], F32)
        wiq = sb("wiq", [128, 256], F32)
        wdq = sb("wdq", [128, CQ], F32)
        keyT = sb("keyT", [96, B, 64 + L], F32)
        ctab = sb("ctab", [128, NT, 3, 64], BF16)
        trig = sb("trig", [128, 2 * TILES + 1, 2, Q4], F32)
        absorb = sb("absorb", [CQ, HEADS, C], F32)
        wvo = sb("wvo", [C, HEADS, D], F32)
        idxw = sb("idxw", [128, IDX_HEADS], F32)
        late = sb("late", [128, 128], F32)
        early = sb("early", [128, 128], F32)
        smask = sb("smask", [128, SPAN], F32)
        keyno = sb("keyno", [128, TILES], F32)
        muq_dram = nc.dram_tensor("muq_dram", (NT, 128, HEADS * R), F32, kind="Internal").ap()
        cpad = nc.dram_tensor("cpad", (B, 64 + L, C), F32, kind="Internal").ap()
        idx_dram = nc.dram_tensor("idx_dram", (2, 128 * FAR), FP16, kind="Internal").ap()
        RA, RV = [banks[0], banks[1], banks[4], banks[6]], [banks[2], banks[3], banks[5], banks[7]]

        prep = ExitStack()
        with prep:
            def sb(name, shape, dt):
                return prep.enter_context(nc.sbuf_tensor(name, shape, dt))

            def sem(name):
                return prep.enter_context(nc.semaphore(name))

            stat = sb("a_stat", [128, 4, NT], F32)
            xc = sb("a_xc", [128, NT, D], F32)
            sq = sb("a_sq", [128, NT, D], F32)
            wkv = sb("wkv", [128, C + R], F32)
            cqT = sb("cqT", [CQ, NT * 128], F32)
            wqr = sb("wqr", [CQ, HEADS * R], F32)
            wik = sb("wik", [128, 64], F32)
            wuq = sb("wuq", [CQ, 512], F32)
            wuk = sb("wuk", [C, 512], F32)
            wuv = sb("wuv", [C, 512], F32)
            wout = sb("wout", [128, 4, D], F32)
            wuqT = sb("wuqT", [128, 4, CQ], F32)
            wukT = sb("wukT", [128, 4, C], F32)
            wuvT = sb("wuvT", [128, 4, C], F32)
            delta = sb("delta", [128, 6, Q4], F32)
            base = sb("base", [128, 2 * TILES + 1, 2, Q4], F32)
            tt = sb("tt", [128, 2 * TILES + 1, Q4], F32)
            kn = sb("kn", [128, NT, C + R], F32)
            sp_a = sb("sp_a", [128, NT, R], F32)
            key3 = sb("key3", [128, NT, 96], F32)
            val = sb("val", [128, NT, 64], F32)
            rt = sb("rt", [128, NT, Q4], F32)
            qraw = [sb(f"qraw{i}", [128, 2, 256], F32) for i in range(2)]
            qsp = [sb(f"qsp{i}", [128, 2, 256], F32) for i in range(2)]

            loads = sem("a_loads")
            a_link = sem("a_link")
            v_link = sem("v_link")
            g_link = sem("g_link")
            filled = sem("p_filled")
            emptied = sem("p_emptied")
            centred = sem("a_centred")
            squared = sem("a_squared")
            varied = sem("a_varied")
            rooted = sem("a_rooted")
            normed = sem("a_normed")
            kn_soft = sem("kn_soft")
            key_ready = sem("key_ready")
            pads = sem("pads")
            cstored = sem("cstored")
            q_soft = sem("q_soft")
            muq_done = sem("muq_done")
            q_stored = [sem(f"q_stored{i}") for i in range(2)]
            quarter = sem("quarter")
            half_pi = sb("half_pi", [128, 1], F32)
            sined = sem("sined")
            NLOAD = 17

            order = [("xT", c) for c in range(NC)] + ["wuqT", "wukT", "wuvT", "absorb0", "absorb1", "wvo0", "wvo1"]
            order += [("kn", h) for h in range(2)]
            order += [("kiT", c) for c in range(NC)]
            order += [("cqT", c) for c in range(NC)] + [("qr", c) for c in range(NT // 2)]
            order += [("keyT", c) for c in range(NC)]
            at = {k: u for u, k in enumerate(order)}
            blk = prep.enter_context(nc.Block())

            @blk.sync
            def _(sp):
                for dst, src in ((wkv[:, 0:C], t["attn_W_dkv"]), (wkv[:, C:], t["attn_W_kr"]), (wdq[:, :], t["attn_W_dq"]),
                                 (wqr[:, :], t["attn_W_qr"]), (wik[:, :], t["attn_idx_wk"]), (wiq[:, :], t["attn_idx_wq"]),
                                 (wuq[:, :], t["attn_W_uq"]), (wuk[:, :], t["attn_W_uk"]), (wuv[:, :], t["attn_W_uv"]),
                                 (wout[:, :, :], t["attn_W_out"].rearrange("(k p) n -> p k n", p=128)),
                                 (idxw[:, :], t["attn_idx_w"].partition_broadcast(128)),
                                 (delta[:, 0, :], t["attn_raw_delta"].partition_broadcast(128)),
                                 (base[:, :, :, :], t["trig"]), (late[:, :], t["late"]), (early[:, :], t["early"]),
                                 (smask[:, :], t["smask"]), (keyno[:, :], t["keyno"])):
                    sp.dma_start(dst, src).then_inc(loads, 16)
                sp.wait_ge(pads, 2)
                for b in range(B):
                    sp.dma_start(cpad[b, 0:64, :], key3[0:64, b, 32:64]).then_inc(cstored, 16)
                sp.wait_ge(emptied, at[("kn", 1)] + 1)
                for b in range(B):
                    sp.dma_start(cpad[b, 64:64 + L, :].rearrange("(n p) c -> p n c", p=128),
                                 kn[:, TILES * b:TILES * (b + 1), 0:C]).then_inc(cstored, 16)
                for c in range(NT // 2):
                    sp.wait_ge(muq_done, c + 1)
                    sp.dma_start(muq_dram[2 * c:2 * c + 2, :, :].rearrange("n p c -> p n c"),
                                 qsp[c % 2][:, :, :]).then_inc(q_stored[c % 2], 16)
                sp.wait_ge(cstored, 64)
                for i in range(2):
                    sp.wait_ge(q_stored[i], 16 * (NT // 4))

            @blk.gpsimd
            def _(pool):
                pool.memset(half_pi[:, :], PI / 2).then_inc(quarter, 1)
                pool.memset(key3[:, :, 32:64], 0.0).then_inc(pads, 1)
                pool.memset(keyT[:, :, 0:64], 0.0).then_inc(pads, 1)

            @blk.scalar
            def _(act):
                links = [0]

                def link(ins):
                    links[0] += 1
                    ins.then_inc(a_link, 1)
                    act.wait_ge(a_link, links[0])

                act.wait_ge(centred, 1)
                act.activation(sq[:, :, :], xc[:, :, :], ACT.Square).then_inc(squared, 1)
                act.wait_ge(varied, 1)
                act.activation(stat[:, 2, :], stat[:, 1, :], ACT.Sqrt).then_inc(rooted, 1)

                def empty(key, dst, src):
                    act.wait_ge(filled, at[key] + 1)
                    act.activation(dst, src, ACT.Copy).then_inc(emptied, 1)

                def bank(key):
                    return banks[at[key] % 8]

                for c in range(NC):
                    empty(("xT", c), xnT[:, c * 512:(c + 1) * 512], bank(("xT", c))[:, :])
                empty("wuqT", wuqT[:, :, :], bank("wuqT")[:, 0:4 * CQ].rearrange("p (k c) -> p k c", k=4))
                empty("wukT", wukT[:, :, :], bank("wukT")[:, 0:4 * C].rearrange("p (k c) -> p k c", k=4))
                empty("wuvT", wuvT[:, :, :], bank("wuvT")[:, 0:4 * C].rearrange("p (k c) -> p k c", k=4))
                for s in range(2):
                    empty(f"absorb{s}", absorb[:, :, :].rearrange("p (j s) c -> p s j c", s=2)[:, s, :, :],
                          bank(f"absorb{s}")[0:CQ, 0:128].rearrange("p (j c) -> p j c", c=C))
                for s in range(2):
                    empty(f"wvo{s}", wvo[:, :, :].rearrange("p (j s) c -> p s j c", s=2)[:, s, :, :],
                          bank(f"wvo{s}")[0:C, :].rearrange("p (j d) -> p j d", d=D))
                for h in range(2):
                    empty(("kn", h), kn[:, 8 * h:8 * h + 8, :],
                          bank(("kn", h))[:, :].rearrange("p (n c) -> p n c", c=64))
                for c in range(NC):
                    empty(("kiT", c), kiT[:, c * 512:(c + 1) * 512], bank(("kiT", c))[0:64, :])
                for c in range(NC):
                    empty(("cqT", c), cqT[:, c * 512:(c + 1) * 512], bank(("cqT", c))[0:CQ, :])
                act.wait_ge(loads, 16 * NLOAD)
                link(act.activation(delta[:, 1, :], delta[:, 0, :], ACT.Sigmoid))
                link(act.activation(delta[:, 2, :], delta[:, 1, :], ACT.Sin, scale=-PI))
                act.wait_ge(quarter, 1)
                act.activation(delta[:, 3, :], delta[:, 1, :], ACT.Sin, scale=-PI, bias=half_pi[:, :]).then_inc(sined, 1)
                act.wait_ge(emptied, at[("kn", 1)] + 1)
                link(act.activation(sp_a[:, :, :], kn[:, :, C:], ACT.Abs))
                link(act.activation(sp_a[:, :, :], sp_a[:, :, :], ACT.Exp, scale=-1.0))
                act.activation(sp_a[:, :, :], sp_a[:, :, :], ACT.Ln, bias=1.0).then_inc(kn_soft, 1)
                for c in range(NT // 2):
                    key = ("qr", c)
                    q, s = qraw[c % 2], qsp[c % 2]
                    if c >= 2:
                        act.wait_ge(q_stored[c % 2], 16 * (c // 2))
                    empty(key, q[:, :, :], bank(key)[:, :].rearrange("p (n c) -> p n c", n=2))
                    act.wait_ge(emptied, at[key] + 1)
                    link(act.activation(s[:, :, :], q[:, :, :], ACT.Abs))
                    link(act.activation(s[:, :, :], s[:, :, :], ACT.Exp, scale=-1.0))
                    act.activation(s[:, :, :], s[:, :, :], ACT.Ln, bias=1.0).then_inc(q_soft, 1)
                for c in range(NC):
                    dst = keyT[:, c // 2, 64 + (c % 2) * 512:64 + (c % 2 + 1) * 512]
                    empty(("keyT", c), dst, bank(("keyT", c))[0:96, :])

            @blk.vector
            def _(dve):
                links = [0]

                def link(ins):
                    links[0] += 1
                    ins.then_inc(v_link, 1)
                    dve.wait_ge(v_link, links[0])

                def over(ap):
                    return ap.unsqueeze(2).broadcast_to([128, NT, D])

                link(dve.tensor_reduce(stat[:, 0, :], x[:, :, :], AX.X, ALU.add))
                link(dve.tensor_scalar(stat[:, 0, :], stat[:, 0, :], 1.0 / D, None, ALU.mult))
                dve.tensor_tensor(xc[:, :, :], x[:, :, :], over(stat[:, 0, :]), ALU.subtract).then_inc(centred, 1)
                dve.wait_ge(squared, 1)
                link(dve.tensor_reduce(stat[:, 1, :], sq[:, :, :], AX.X, ALU.add))
                dve.tensor_scalar(stat[:, 1, :], stat[:, 1, :], 1.0 / D, LN_EPS, ALU.mult, ALU.add).then_inc(varied, 1)
                dve.wait_ge(rooted, 1)
                link(dve.reciprocal(stat[:, 3, :], stat[:, 2, :]))
                dve.wait_ge(centred, 1)
                dve.tensor_tensor(xc[:, :, :], xc[:, :, :], over(stat[:, 3, :]), ALU.mult).then_inc(normed, 1)

                dve.wait_ge(loads, 16 * NLOAD)
                dve.wait_ge(sined, 1)
                sh, ch, sd, cd = (delta[:, k, :] for k in (2, 3, 4, 5))
                link(dve.tensor_tensor(sd, sh, ch, ALU.mult))
                link(dve.tensor_scalar(sd, sd, 2.0, None, ALU.mult))
                link(dve.tensor_tensor(cd, sh, sh, ALU.mult))
                link(dve.tensor_scalar(cd, cd, -2.0, 1.0, ALU.mult, ALU.add))
                n = 2 * TILES + 1

                def wide(ap):
                    return ap.unsqueeze(1).broadcast_to([128, n, Q4])

                for k, sign in ((0, ALU.subtract), (1, ALU.add)):
                    link(dve.tensor_tensor(trig[:, :, k, :], base[:, :, k, :], wide(cd), ALU.mult))
                    link(dve.tensor_tensor(tt[:, :, :], base[:, :, 1 - k, :], wide(sd), ALU.mult))
                    link(dve.tensor_tensor(trig[:, :, k, :], trig[:, :, k, :], tt[:, :, :], sign))

                dve.wait_ge(kn_soft, 1)
                for b in range(B):
                    n = slice(TILES * b, TILES * (b + 1))
                    last = dve.scalar_tensor_tensor(val[:, n, C:], kn[:, n, C:], 0.0, sp_a[:, n, :], ALU.max, ALU.add)
                link(last)
                link(dve.tensor_copy(val[:, :, 0:C], kn[:, :, 0:C]))
                dve.wait_ge(pads, 2)
                link(dve.tensor_copy(key3[:, :, 0:C], kn[:, :, 0:C]))
                for b in range(B):
                    n = slice(TILES * b, TILES * (b + 1))
                    co, si = trig[:, 0:TILES, 0, :], trig[:, 0:TILES, 1, :]
                    m1, m2 = val[:, n, C:C + Q4], val[:, n, C + Q4:]
                    for dst, a, z, op in ((slice(64, 80), co, si, ALU.subtract), (slice(80, 96), si, co, ALU.add)):
                        link(dve.tensor_tensor(key3[:, n, dst], m1, a, ALU.mult))
                        link(dve.tensor_tensor(rt[:, n, :], m2, z, ALU.mult))
                        link(dve.tensor_tensor(key3[:, n, dst], key3[:, n, dst], rt[:, n, :], op))
                dve.tensor_copy(ctab[:, :, 0, :], val[:, :, :]).then_inc(key_ready, 1)
                dve.wait_ge(key_ready, 1)
                link(dve.tensor_tensor(val[:, :, :], val[:, :, :], ctab[:, :, 0, :], ALU.subtract))
                link(dve.tensor_copy(ctab[:, :, 1, :], val[:, :, :]))
                link(dve.tensor_tensor(val[:, :, :], val[:, :, :], ctab[:, :, 1, :], ALU.subtract))
                link(dve.tensor_copy(ctab[:, :, 2, :], val[:, :, :]))
                for c in range(NT // 2):
                    dve.wait_ge(q_soft, c + 1)
                    dve.scalar_tensor_tensor(qsp[c % 2][:, :, :].rearrange("p n c -> p (n c)"),
                                             qraw[c % 2][:, :, :].rearrange("p n c -> p (n c)"), 0.0,
                                             qsp[c % 2][:, :, :].rearrange("p n c -> p (n c)"),
                                             ALU.max, ALU.add).then_inc(muq_done, 1)

            @blk.tensor
            def _(pe):
                def bank(key):
                    if at[key] >= 8:
                        pe.wait_ge(emptied, at[key] - 7)
                    return banks[at[key] % 8]

                pe.wait_ge(normed, 1)
                for c in range(NC):
                    o = bank(("xT", c))
                    for k in range(4):
                        last = pe.transpose(o[:, k * 128:(k + 1) * 128], xc[:, 4 * c + k, :], ident)
                    last.then_inc(filled, 1)
                pe.wait_ge(loads, 16 * NLOAD)
                for key, src, rows in (("wuqT", wuq, CQ), ("wukT", wuk, C), ("wuvT", wuv, C)):
                    o = bank(key)
                    for k in range(4):
                        last = pe.transpose(o[:, k * rows:(k + 1) * rows], src[:, k * 128:(k + 1) * 128],
                                            ident[0:rows, 0:rows])
                    last.then_inc(filled, 1)
                pe.wait_ge(emptied, at["wuvT"] + 1)
                for s in range(2):
                    rows = slice(64 * s, 64 * s + 64)
                    o = bank(f"absorb{s}")
                    for j in range(4):
                        last = pe.matmul(o[0:CQ, j * C:(j + 1) * C], wuqT[rows, j, :], wukT[rows, j, :],
                                         start=True, stop=True)
                    last.then_inc(filled, 1)
                for s in range(2):
                    rows = slice(64 * s, 64 * s + 64)
                    o = bank(f"wvo{s}")
                    for j in range(4):
                        last = pe.matmul(o[0:C, j * D:(j + 1) * D], wuvT[rows, j, :], wout[rows, j, :],
                                         start=True, stop=True)
                    last.then_inc(filled, 1)
                for g in range(2):
                    o = bank(("kn", g))
                    for k in range(8):
                        n = 8 * g + k
                        last = pe.matmul(o[:, k * 64:(k + 1) * 64], xnT[:, n * 128:(n + 1) * 128], wkv[:, :],
                                         start=True, stop=True)
                    last.then_inc(filled, 1)
                for c in range(NC):
                    pe.matmul(bank(("kiT", c))[0:64, :], wik[:, :], xnT[:, c * 512:(c + 1) * 512],
                              start=True, stop=True).then_inc(filled, 1)
                for c in range(NC):
                    pe.matmul(bank(("cqT", c))[0:CQ, :], wdq[:, :], xnT[:, c * 512:(c + 1) * 512],
                              start=True, stop=True).then_inc(filled, 1)
                pe.wait_ge(emptied, at[("cqT", NC - 1)] + 1)
                for c in range(NT // 2):
                    o = bank(("qr", c))
                    for k in range(2):
                        n = 2 * c + k
                        last = pe.matmul(o[:, k * 256:(k + 1) * 256], cqT[:, n * 128:(n + 1) * 128], wqr[:, :],
                                         start=True, stop=True)
                    last.then_inc(filled, 1)
                pe.wait_ge(key_ready, 1)
                for c in range(NC):
                    o = bank(("keyT", c))
                    for k in range(4):
                        last = pe.transpose(o[0:96, k * 128:(k + 1) * 128], key3[:, 4 * c + k, :], ident)
                    last.then_inc(filled, 1)
        attn_loop(nc, t, x, x_out, ident, xnT, kiT, wiq, wdq, keyT, ctab, muq_dram, trig, absorb, wvo, idxw, late, early, smask,
                  keyno, cpad, idx_dram, RA, RV, A_AT, A_N, V_AT, V_N)


def macaron_kernel(nc, t, out):
    ctx = ExitStack()
    with ctx:
        def sb(name, shape, dt):
            return ctx.enter_context(nc.sbuf_tensor(name, shape, dt))

        xs = sb("xs", [128, NT, D], F32)
        ident = sb("ident", [128, 128], F32)
        identb = sb("identb", [128, 128], BF16)
        sel = sb("sel", [97, PAIRS // 2 + 1, 128], BF16)
        banks = [ctx.enter_context(nc.psum_tensor(f"bank{i}", [128, 512], F32)) for i in range(8)]
        start_loaded = ctx.enter_context(nc.semaphore("start_loaded"))
        stored = ctx.enter_context(nc.semaphore("stored"))

        with nc.Block() as blk:
            @blk.sync
            def _(sp):
                sp.dma_start(xs[:, :, :], t["x"].rearrange("b (n p) d -> p (b n) d", p=128)).then_inc(start_loaded, 16)
                sp.dma_start(ident[:, :], t["ident"]).then_inc(start_loaded, 16)
                sp.dma_start(identb[:, :].bitcast(mybir.dt.uint16), t["identb"]).then_inc(start_loaded, 16)
                sp.dma_start(sel[:, :, :].bitcast(mybir.dt.uint16), t["sel"]).then_inc(start_loaded, 16)
                sp.wait_ge(start_loaded, 64)

        const = {"ident": ident[:, :], "identb": identb[:, :], "sel": sel}
        w = {k: t[f"ffn_{n}"] for k, n in (("router", "router_w"), ("sgate", "shared_gate_w"), ("sup", "shared_up_w"),
                                           ("sdown", "shared_down_w"), ("gate", "expert_gate_k"),
                                           ("up", "expert_up_k"), ("down", "expert_down_k"))}
        ffn_phase(nc, "f1", xs[:, :, :], xs, w, const, banks)
        attn_phase(nc, t, xs, xs, const, banks)
        ffn_phase(nc, "f2", xs[:, :, :], xs, w, const, banks)
    
        with nc.Block() as blk:
            @blk.sync
            def _(sp):
                sp.dma_start(out.rearrange("b (n p) d -> p (b n) d", p=128), xs[:, :, :]).then_inc(stored, 16)
                sp.wait_ge(stored, 16)


_FFN = ['ffn_router_w', 'ffn_shared_gate_w', 'ffn_shared_up_w', 'ffn_shared_down_w', 'ffn_expert_gate_k',
        'ffn_expert_up_k', 'ffn_expert_down_k']
_ATTN = ['attn_W_dkv', 'attn_W_uk', 'attn_W_uv', 'attn_W_dq', 'attn_W_uq', 'attn_W_qr', 'attn_W_kr', 'attn_W_out',
         'attn_idx_wq', 'attn_idx_wk', 'attn_idx_w', 'attn_raw_delta']


def _constants():
    import numpy as np
    one = 0x3F80
    c = {"ident": np.eye(128, dtype=np.float32), "identb": (np.eye(128) * one).astype(np.uint16)}
    sel = np.zeros((97, PAIRS // 2 + 1, 128), np.uint16)
    for part in range(3):
        for q in range(PAIRS // 2):
            for s in range(2):
                sel[part * 32 + 2 * q + s, q, 64 * s:64 * s + 64] = one
    sel[96, PAIRS // 2, :] = one
    c["sel"] = sel
    c.update(_attn_constants())
    return c


def kernel(**inputs):
    import numpy as _np
    import concourse.bacc as _bacc
    from concourse import mybir as _mybir
    from concourse.bass_utils import run_bass_kernel_spmd as _run

    nc = _bacc.Bacc("TRN2", target_bir_lowering=False, num_devices=1)
    arrays, t = {}, {}

    def take(name, a):
        arrays[f"in_{name}_dram"] = a
        t[name] = nc.dram_tensor(f"in_{name}_dram", a.shape, _mybir.dt.from_np(a.dtype), kind="ExternalInput").ap()

    take("x", _np.ascontiguousarray(inputs["L0_attn_x"]))
    for name in _FFN + _ATTN:
        take(name, _np.ascontiguousarray(inputs["L0_" + name]))
    for name, a in _constants().items():
        take(name, a)
    out = nc.dram_tensor("out_0_dram", (B, L, D), _mybir.dt.float32, kind="ExternalOutput").ap()
    macaron_kernel(nc, t, out)
    r = _run(nc, [arrays], core_ids=[0])
    return r.results[0]["out_0_dram"]
```

```python
import concourse.bass as bass
from concourse import mybir
from contextlib import ExitStack

F32 = mybir.dt.float32
F32R = mybir.dt.float32r
BF16 = mybir.dt.bfloat16
FP16 = mybir.dt.float16
ALU = mybir.AluOpType
ACT = mybir.ActivationFunctionType
AX = mybir.AxisListType

B, L, D = 2, 1024, 128
NT = B * L // 128
EXPERTS, WIDE, TOPK = 64, 64, 8
CHUNK = 512
NC = B * L // CHUNK
PAIRS = EXPERTS // 2
LN_EPS = 1e-5
LOWEST = -3.0e38


def ffn_phase(nc, tag, x, x_out, w, const, banks):
    ctx = ExitStack()

    def sb(name, shape, dt):
        return ctx.enter_context(nc.sbuf_tensor(f"{name}_{tag}", shape, dt))

    def sem(name):
        return ctx.enter_context(nc.semaphore(f"{name}_{tag}"))

    with ctx:
        stat = sb("stat", [128, 4, NT], F32)
        xc = sb("xc", [128, NT, D], F32)
        sq = sb("sq", [128, NT, D], F32)
        xnT = sb("xnT", [128, NT * 128], F32)
        xhi = sb("xhi", [128, NT * 128], F32R)
        xlo = sb("xlo", [128, NT * 128], F32R)
        rw = sb("rw", [128, EXPERTS], F32)
        lg = sb("lg", [128, NT, EXPERTS], F32)
        rep = sb("rep", [128, NT, EXPERTS], F32)
        top = sb("top", [128, NT, 8], F32)
        aff = sb("aff", [128, NT, EXPERTS], F32)
        wsum = sb("wsum", [128, 2, NT], F32)
        wfull = sb("wfull", [128, NT, 2, 32], F32)
        wpart = sb("wpart", [128, NT, 2, 3, 32], BF16)
        maskT = sb("maskT", [97, 2, NT * 128], BF16)
        raw = [sb(f"raw{i}", [128, 3, 128], F32) for i in range(2)]
        whi = [sb(f"whi{i}", [128, 3, 128], F32R) for i in range(2)]
        wlo = [sb(f"wlo{i}", [128, 3, 128], F32R) for i in range(2)]
        silu = [sb(f"silu{i}", [128, CHUNK], F32) for i in range(2)]
        gated = [sb(f"gated{i}", [128, CHUNK], F32) for i in range(2)]
        act = [sb(f"act{i}", [128, CHUNK], F32) for i in range(2)]
        ahi = [sb(f"ahi{i}", [128, CHUNK], F32R) for i in range(4)]
        alo = [sb(f"alo{i}", [128, CHUNK], F32R) for i in range(4)]
        yT = sb("yT", [128, NT * 128], F32)

        acc = banks[0:4]
        gate_ps, up_ps, mask_ps = banks[4:6], banks[6], banks[7]
        LG = [banks[6], banks[7]]
        ident, identb, sel = const["ident"], const["identb"], const["sel"]

        router_loaded = sem("router_loaded")
        loaded = [sem(f"loaded{i}") for i in range(2)]
        split_done = sem("split_done")
        zeroed = sem("zeroed")
        ln = sem("ln")
        pool_turn = sem("pool_turn")
        squared = sem("squared")
        deviation = sem("deviation")
        xT_ready = sem("xT_ready")
        xT_raw = sem("xT_raw")
        xT_split = sem("xT_split")
        logits_ready = sem("logits_ready")
        logits_out = sem("logits_out")
        affinity_ready = sem("affinity_ready")
        dve_link = sem("dve_link")
        parts_ready = sem("parts_ready")
        maskT_ps = sem("maskT_ps")
        maskT_done = sem("maskT_done")
        gate_done = sem("gate_done")
        up_done = sem("up_done")
        mask_done = sem("mask_done")
        silu_done = sem("silu_done")
        gated_done = sem("gated_done")
        act_done = sem("act_done")
        ahi_done = sem("ahi_done")
        alo_done = sem("alo_done")
        down_done = sem("down_done")
        yT_done = sem("yT_done")
        y_done = sem("y_done")
        x_done = sem("x_done")

        LAG = 2

        blk = ctx.enter_context(nc.Block())

        @blk.sync
        def _(sp):
            sp.dma_start(rw[:, :], w["router"]).then_inc(router_loaded, 16)
            sp.wait_ge(zeroed, 1)
            sp.dma_start(raw[0][:, 0, 0:WIDE], w["sgate"]).then_inc(loaded[0], 16)
            sp.dma_start(raw[0][:, 1, 0:WIDE], w["sup"]).then_inc(loaded[0], 16)
            sp.dma_start(raw[0][0:WIDE, 2, :], w["sdown"]).then_inc(loaded[0], 16)

            def load(u, slot):
                if not (isinstance(u, int) and u < 2):
                    sp.wait_ge(split_done, 2 * (u - 1))
                g = w["gate"][bass.ds((u - 1) * 2, 2), :, :].rearrange("e h i -> h e i")
                v = w["up"][bass.ds((u - 1) * 2, 2), :, :].rearrange("e h i -> h e i")
                d = w["down"].rearrange("e i h -> (e i) h")[bass.ds((u - 1) * 128, 128), :]
                sp.dma_start(raw[slot][:, 0, :].rearrange("h (e i) -> h e i", e=2), g).then_inc(loaded[slot], 16)
                sp.dma_start(raw[slot][:, 1, :].rearrange("h (e i) -> h e i", e=2), v).then_inc(loaded[slot], 16)
                sp.dma_start(raw[slot][:, 2, :], d).then_inc(loaded[slot], 16)

            load(1, 1)
            load(2, 0)
            with sp.Fori(3, PAIRS, 2) as u:
                load(u, 1)
                load(u + 1, 0)

        @blk.gpsimd
        def _(pool):
            pool.memset(raw[0][:, :, :], 0.0).then_inc(zeroed, 1)

            def split(u, slot, n):
                pool.wait_ge(loaded[slot], 48 * n)
                if not (isinstance(u, int) and u < 2):
                    pool.wait_ge(down_done, 4 * (u - 1))
                pool.sem_inc(pool_turn, 1)
                pool.tensor_copy(whi[slot][:, :, :], raw[slot][:, :, :]).then_inc(split_done, 1)
                pool.wait_ge(split_done, 2 * u + 1)
                pool.tensor_tensor(wlo[slot][:, :, :], raw[slot][:, :, :], whi[slot][:, :, :].bitcast(F32),
                                   ALU.subtract).then_inc(split_done, 1)

            split(0, 0, 1)
            split(1, 1, 1)
            split(2, 0, 2)
            with pool.Fori(1, PAIRS // 2) as j:
                split(2 * j + 1, 1, j + 1)
                split(2 * j + 2, 0, j + 2)

        @blk.scalar
        def _(act_e):
            act_e.wait_ge(ln, 2)
            act_e.activation(sq[:, :, :], xc[:, :, :], ACT.Square).then_inc(squared, 1)
            act_e.wait_ge(ln, 4)
            act_e.activation(stat[:, 2, :], stat[:, 1, :], ACT.Sqrt).then_inc(deviation, 1)
            for c in range(NC):
                act_e.wait_ge(xT_ready, c + 1)
                act_e.activation(xnT[:, c * CHUNK:(c + 1) * CHUNK], gate_ps[c % 2][:, :], ACT.Copy).then_inc(xT_raw, 1)
            act_e.wait_ge(logits_out, 1)
            act_e.activation(aff[:, :, :], lg[:, :, :], ACT.Sigmoid).then_inc(affinity_ready, 1)
            for c in range(NC):
                act_e.wait_ge(maskT_ps, c + 1)
                act_e.activation(maskT[0:96, :, c * CHUNK:(c + 1) * CHUNK],
                                 gate_ps[c % 2][0:96, :].bitcast(BF16).rearrange("p (k t) -> p k t", k=2),
                                 ACT.Copy).then_inc(maskT_done, 1)

            def step(k, m):
                act_e.wait_ge(gate_done, k + 1)
                if not (isinstance(k, int) and k < 2):
                    act_e.wait_ge(gated_done, k - 1)
                act_e.activation(silu[m % 2][:, :], gate_ps[m % 2][:, :], ACT.Silu).then_inc(silu_done, 1)

            def high(k, m):
                act_e.wait_ge(act_done, k + 1)
                if not (isinstance(k, int) and k < 4):
                    act_e.wait_ge(down_done, k - 3)
                act_e.activation(ahi[m % 4][:, :], act[m % 2][:, :], ACT.Copy).then_inc(ahi_done, 1)

            step(0, 0)
            for k in range(1, 4):
                step(k, k)
                high(k - 1, k - 1)
            with act_e.Fori(0, PAIRS // 2) as j:
                for m in range(8):
                    k = 8 * j + (4 + m)
                    step(k, (4 + m) % 8)
                    high(k - 1, (3 + m) % 8)
            high(4 * PAIRS + 3, 3)
            for c in range(NC):
                act_e.wait_ge(down_done, 4 * PAIRS + c + 1)
                act_e.activation(yT[:, c * CHUNK:(c + 1) * CHUNK], acc[c][:, :], ACT.Copy, scale=0.5).then_inc(yT_done, 1)

        @blk.vector
        def _(dve):
            links = [0]

            def link(ins):
                links[0] += 1
                ins.then_inc(dve_link, 1)
                dve.wait_ge(dve_link, links[0])

            def over(ap):
                return ap.unsqueeze(2).broadcast_to([128, NT, D])

            link(dve.tensor_reduce(stat[:, 0, :], x, AX.X, ALU.add))
            link(dve.tensor_scalar(stat[:, 0, :], stat[:, 0, :], 1.0 / D, None, ALU.mult))
            dve.tensor_tensor(xc[:, :, :], x, over(stat[:, 0, :]), ALU.subtract).then_inc(ln, 2)
            dve.memset(maskT[96:97, :, :], 1.0)
            dve.wait_ge(squared, 1)
            link(dve.tensor_reduce(stat[:, 1, :], sq[:, :, :], AX.X, ALU.add))
            dve.tensor_scalar(stat[:, 1, :], stat[:, 1, :], 1.0 / D, LN_EPS, ALU.mult, ALU.add).then_inc(ln, 2)
            dve.wait_ge(deviation, 1)
            link(dve.reciprocal(stat[:, 3, :], stat[:, 2, :]))
            dve.tensor_tensor(xc[:, :, :], xc[:, :, :], over(stat[:, 3, :]), ALU.mult).then_inc(ln, 1)
            for c in range(NC):
                part = slice(c * CHUNK, (c + 1) * CHUNK)
                dve.wait_ge(xT_raw, c + 1)
                link(dve.tensor_copy(xhi[:, part], xnT[:, part]))
                dve.tensor_tensor(xlo[:, part], xnT[:, part], xhi[:, part].bitcast(F32),
                                  ALU.subtract).then_inc(xT_split, 1)
            for h in range(2):
                dve.wait_ge(logits_ready, h + 1)
                last = dve.tensor_copy(lg[:, 8 * h:8 * h + 8, :], LG[h][:, :].rearrange("p (t e) -> p t e", e=EXPERTS))
            last.then_inc(logits_out, 1)
            dve.wait_ge(logits_out, 1)
            for t in range(NT):
                last = dve.max(top[:, t, :], lg[:, t, :])
            link(last)
            for t in range(NT):
                last = dve.match_replace(rep[:, t, :], top[:, t, :], lg[:, t, :], LOWEST)
            link(last)
            link(dve.tensor_tensor(rep[:, :, :], rep[:, :, :], lg[:, :, :], ALU.is_lt))
            dve.wait_ge(affinity_ready, 1)
            link(dve.tensor_tensor(aff[:, :, :], aff[:, :, :], rep[:, :, :], ALU.mult))
            link(dve.tensor_reduce(wsum[:, 0, :], aff[:, :, :], AX.X, ALU.add))
            link(dve.tensor_scalar(wsum[:, 0, :], wsum[:, 0, :], 1e-9, None, ALU.add))
            link(dve.reciprocal(wsum[:, 1, :], wsum[:, 0, :]))
            scale = wsum[:, 1, :].unsqueeze(2).broadcast_to([128, NT, EXPERTS])
            link(dve.tensor_tensor(aff[:, :, :], aff[:, :, :], scale, ALU.mult))
            for c in range(2):
                src = aff[:, :, :].rearrange("p t (q c s) -> p c t q s", c=2, s=2)[:, c, :, :, :]
                last = dve.tensor_copy(wfull[:, :, c, :].rearrange("p t (q s) -> p t q s", s=2), src)
            link(last)
            full = wfull[:, :, :, :].rearrange("p t c e -> p (t c) e")
            part = [wpart[:, :, :, i, :].rearrange("p t c e -> p (t c) e") for i in range(3)]
            link(dve.tensor_copy(part[0], full))
            link(dve.tensor_tensor(full, full, part[0], ALU.subtract))
            link(dve.tensor_copy(part[1], full))
            link(dve.tensor_tensor(full, full, part[1], ALU.subtract))
            dve.tensor_copy(part[2], full).then_inc(parts_ready, 1)

            def gate_up(k, m):
                dve.wait_ge(silu_done, k + 1)
                dve.wait_ge(up_done, k + 1)
                if not (isinstance(k, int) and k < 2):
                    dve.wait_ge(act_done, k - 1)
                dve.tensor_tensor(gated[m % 2][:, :], silu[m % 2][:, :], up_ps[:, :], ALU.mult).then_inc(gated_done, 1)

            def weigh(k, m):
                dve.wait_ge(gated_done, k + 1)
                dve.wait_ge(mask_done, k + 1)
                if not (isinstance(k, int) and k < 2):
                    dve.wait_ge(alo_done, k - 1)
                dve.tensor_tensor(act[m % 2][:, :], gated[m % 2][:, :], mask_ps[:, :], ALU.mult).then_inc(act_done, 1)

            def low(k, m):
                dve.wait_ge(ahi_done, k + 1)
                dve.tensor_tensor(alo[m % 4][:, :], act[m % 2][:, :], ahi[m % 4][:, :].bitcast(F32),
                                  ALU.subtract).then_inc(alo_done, 1)

            gate_up(0, 0)
            weigh(0, 0)
            for k in range(1, 4):
                gate_up(k, k)
                low(k - 1, k - 1)
                weigh(k, k)
            with dve.Fori(0, PAIRS // 2) as j:
                for m in range(8):
                    k = 8 * j + (4 + m)
                    gate_up(k, (4 + m) % 8)
                    low(k - 1, (3 + m) % 8)
                    weigh(k, (4 + m) % 8)
            low(4 * PAIRS + 3, 3)
            for c in range(NC):
                dve.wait_ge(y_done, c + 1)
                dve.tensor_tensor(x_out[:, 4 * c:4 * c + 4, :], x[:, 4 * c:4 * c + 4, :],
                                  gate_ps[c % 2][:, :].rearrange("p (t d) -> p t d", t=4), ALU.add).then_inc(x_done, 1)

        @blk.tensor
        def _(pe):
            pe.wait_ge(ln, 5)
            for c in range(NC):
                if c >= 2:
                    pe.wait_ge(xT_raw, c - 1)
                for t in range(4):
                    last = pe.transpose(gate_ps[c % 2][:, t * 128:(t + 1) * 128], xc[:, 4 * c + t, :], ident)
                last.then_inc(xT_ready, 1)
            pe.wait_ge(xT_raw, NC)
            pe.wait_ge(router_loaded, 16)
            for t in range(NT):
                last = pe.matmul(LG[t // 8][:, (t % 8) * EXPERTS:(t % 8 + 1) * EXPERTS],
                                 xnT[:, t * 128:(t + 1) * 128], rw[:, :], start=True, stop=True)
                if t % 8 == 7:
                    last.then_inc(logits_ready, 1)
            pe.wait_ge(parts_ready, 1)
            pe.wait_ge(xT_split, NC)
            for c in range(NC):
                if c >= 2:
                    pe.wait_ge(maskT_done, c - 1)
                for k in range(2):
                    for t in range(4):
                        out = gate_ps[c % 2][0:96, :].bitcast(BF16)[:, (4 * k + t) * 128:(4 * k + t + 1) * 128]
                        last = pe.transpose(out, wpart[:, 4 * c + t, k, :, :].rearrange("p a e -> p (a e)"), identb)
                last.then_inc(maskT_ps, 1)
            pe.wait_ge(maskT_done, NC)

            def triple(out, i, slot, hi, lo, first, last):
                pe.matmul(out, whi[slot][:, i, :], hi, start=first, stop=False)
                pe.matmul(out, whi[slot][:, i, :], lo, start=False, stop=False)
                return pe.matmul(out, wlo[slot][:, i, :], hi, start=False, stop=last)

            def up_step(slot, c, k, m):
                cs = slice(c * CHUNK, (c + 1) * CHUNK)
                static = isinstance(k, int)
                if not (static and k < 2):
                    pe.wait_ge(silu_done, k - 1)
                triple(gate_ps[m % 2][:, :], 0, slot, xhi[:, cs], xlo[:, cs], True, True).then_inc(gate_done, 1)
                if not (static and k < 1):
                    pe.wait_ge(gated_done, k)
                triple(up_ps[:, :], 1, slot, xhi[:, cs], xlo[:, cs], True, True).then_inc(up_done, 1)

            def mask_step(q, parity, c, k):
                if not (isinstance(k, int) and k < 1):
                    pe.wait_ge(act_done, k)
                cs = slice(c * CHUNK, (c + 1) * CHUNK)
                pe.matmul(mask_ps[:, :], sel[:, bass.ds(q, 1), :].rearrange("p a m -> p (a m)"),
                          maskT[:, parity, cs], start=True, stop=True).then_inc(mask_done, 1)

            def down_step(slot, c, k, m, first=False, last=False):
                pe.wait_ge(alo_done, k + 1)
                done = triple(acc[c][:, :], 2, slot, ahi[m % 4][:, :], alo[m % 4][:, :], first, last)
                done.then_inc(down_done, 1)
                return done

            pe.wait_ge(split_done, 2)
            for c in range(4):
                up_step(0, c, c, c)
                mask_step(PAIRS // 2, 0, c, c)
                if c >= LAG:
                    down_step(0, c - LAG, c - LAG, c - LAG, first=True)

            def body(j, first=False, last=False):
                for m in range(8):
                    du, c = divmod(m, 4)
                    k = 8 * j + (4 + m)
                    if c == 0:
                        pe.wait_ge(split_done, 4 * j + (4 + 2 * du))
                    up_step(1 - du, c, k, m + 4)
                    mask_step(j, du, c, k)
                    slot = (1 - du) if c >= LAG else du
                    down_step(slot, (c - LAG) % 4, k - LAG, (m + 4 - LAG) % 8,
                              first=first and m < LAG, last=last and m >= 4 + LAG)

            body(0, first=True)
            with pe.Fori(1, PAIRS // 2 - 1) as j:
                body(j)
            body(PAIRS // 2 - 1, last=True)
            for c in (2, 3):
                down_step(0, c, 4 * PAIRS + c, c, last=True)
            for c in range(NC):
                pe.wait_ge(yT_done, c + 1)
                if c >= 2:
                    pe.wait_ge(x_done, c - 1)
                for t in range(4):
                    s = (4 * c + t) * 128
                    last = pe.transpose(gate_ps[c % 2][:, t * 128:(t + 1) * 128], yT[:, s:s + 128], ident)
                last.then_inc(y_done, 1)


HEADS, WIDTH = 8, 64
C, R = 32, 32
CQ = 64
IDX_HEADS = 4
FAR, LOCAL = 32, 64
TILES = L // 128
BLK = 16
PAIRS_B = 4
WIN = BLK + LOCAL
HEAD_KEYS = 96
SPAN = WIN + 128
GROUPS = 32
SCALE = (WIDTH + R) ** -0.5
PI = 3.14159265358979
OUT = -1.0e30
Q4 = R // 2


def place(i):
    return i // TILES, i % TILES


def width(i):
    k = i % TILES
    return 128 if k == 0 else 128 * k + 64


def halves(i):
    return [(s, min(s + 512, width(i))) for s in range(0, width(i), 512)]


def chunks(n):
    return range(4) if n % TILES else range(LOCAL // 32, 4)


def key_tiles(n, p):
    return range(n % TILES + (p >= 2))


def turned(i, p):
    tile, chunk = (i, 3) if p == 0 else (i + 1, p - 2)
    return [(tile, chunk)] if 0 <= tile < NT and chunk in chunks(tile) else []


def attended(i, p):
    tile, pair = (i - 1, 3) if p == 0 else (i, p - 2)
    return [(tile, pair)] if tile >= 0 and pair >= 0 else []


def plan():
    a_tasks, v_tasks, c_tasks = [], [], []
    for i in range(-4, NT):
        n, m = i + 1, i + 4
        for p in range(5):
            if i >= 0 and p < 4:
                a_tasks.append(("S", i, p))
            for tile, pair in attended(i, p):
                a_tasks.append(("ctx", tile, pair))
            if 0 <= n < NT and p in chunks(n):
                v_tasks += [("gather", n, 2 * p + g) for g in range(2)]
                c_tasks.append((n, p))
            if i >= 1 and p == 0:
                v_tasks.append(("out", i - 1))
            if p == 4 and 0 <= n < NT:
                a_tasks.append(("cq", n))
            if p == 4 and m < NT:
                a_tasks.append(("qi", m))
            if p == 4 and 0 <= n < NT:
                a_tasks.append(("qabs", n))
            if p == 4 and m < NT:
                a_tasks += [("score", m, s, h) for s in range(len(halves(m))) for h in range(IDX_HEADS)]
            if p == 4 and 0 <= n < NT:
                a_tasks += [("QT", n, h) for h in range(2)]
            if i >= 0 and p >= 1:
                a_tasks.append(("PT", i, p - 1))
            for tile, chunk in turned(i, p):
                a_tasks += [("GT", tile, 2 * chunk + g) for g in range(2)]
    a_tasks.append(("ctx", NT - 1, PAIRS_B - 1))
    v_tasks.append(("out", NT - 1))
    return ({k: u for u, k in enumerate(a_tasks)}, len(a_tasks), {k: u for u, k in enumerate(v_tasks)}, len(v_tasks),
            {k: u for u, k in enumerate(c_tasks)}, len(c_tasks))


def _attn_constants():
    import numpy as np
    theta = (1.0 / np.float32(10000.0) ** (2.0 * np.arange(Q4, dtype=np.float32) / R)).astype(np.float32)
    t = np.arange(L).reshape(TILES, 128).T
    angle = np.zeros((128, 2 * TILES + 1, Q4))
    angle[:, :TILES] = (t[:, :, None].astype(np.float32) * theta).astype(np.float32)
    angle[:, TILES:2 * TILES] = (t + np.maximum(t - (LOCAL - 1), 0))[:, :, None] * theta.astype(np.float64)
    rank = LOCAL + np.arange(128) % FAR
    angle[:, 2 * TILES] = (rank[:, None].astype(np.float32) * theta).astype(np.float32)
    trig = np.stack([np.cos(angle), np.sin(angle)], 2).astype(np.float32)
    p, c = np.arange(128)[:, None], np.arange(128)[None, :]
    late = np.where(c <= p, 0.0, LOWEST).astype(np.float32)
    early = np.where(c > p, OUT * (1 + c / 1024.0), LOWEST)
    early = np.where(c <= p - LOCAL, 0.0, early).astype(np.float32)
    q = p // HEADS
    w = np.arange(WIN)[None, :]
    near = np.where((w >= q + 1) & (w <= q + LOCAL), 0.0, OUT)
    far = np.where((p // 32 == p // 32) & (c // FAR == q % 4), 0.0, OUT)
    s = 128 * np.arange(TILES)[None, :] + p
    return {"trig": trig, "late": late, "early": early, "smask": (np.concatenate([near, far], 1).astype(np.float32).view(np.uint32) >> 16).astype(np.uint16),
            "keyno": s.astype(np.float32)}



def attn_loop(nc, t, x, x_out, ident, identb, xnT, kiT, wiq, wdq, keyT, ctab, muq_dram, trig, absorb, wvo, expo, idxw, late, early, smask,
              keyno, cpad, idx_dram, RA, RV, A_AT, A_N, V_AT, V_N, C_AT, C_N):
    ctx = ExitStack()

    def sb(name, shape, dt):
        return ctx.enter_context(nc.sbuf_tensor(name, shape, dt))

    def sem(name):
        return ctx.enter_context(nc.semaphore(name))

    with ctx:
        hot = sb("hot", [128, TILES, GROUPS, 128], FP16)
        idxb = sb("idxb", [128, 128 * FAR], FP16)
        relu = [sb(f"relu{i}", [128, 512], F32) for i in range(2)]
        score = [sb(f"score{i}", [128, L], F32) for i in range(2)]
        best = sb("best", [128, 4, 8], F32)
        which = sb("which", [128, 4, 8], mybir.dt.uint16)
        idx16 = [sb(f"idx16_{i}", [128, FAR], FP16) for i in range(2)]
        G = [sb(f"G{i}", [128, GROUPS, 64], F32) for i in range(2)]
        tmp = [sb(f"tmp{i}", [128, 8, Q4], F32) for i in range(4)]
        muq = [sb(f"muq{i}", [128, HEADS, R], F32) for i in range(2)]
        QI = sb("QI", [64, IDX_HEADS, 128], F32)
        CQT = sb("CQT", [CQ, 128], F32)
        GT = sb("GT", [64, GROUPS * 128], F32)
        QN = sb("QN", [128, HEADS, 96], F32)
        QT = sb("QT", [96, 128, HEADS], F32)
        diag = [sb(f"diag{i}", [128, 2, 128], F32) for i in range(2)]
        P = [sb(f"P{i}", [128, 2, SPAN], F32) for i in range(2)]
        small = [sb(f"small{i}", [128, 4, 2], F32) for i in range(2)]
        PT = [sb(f"PT{i}", [128, 4, 128], F32) for i in range(2)]
        CT = sb("CT", [C, 128, HEADS], F32)
        cwin = [sb(f"cwin{i}", [WIN, 8, C], F32) for i in range(2)]
        chead = sb("chead", [HEAD_KEYS, C], F32)

        a_filled, a_emptied = sem("a_filled"), sem("a_emptied")
        v_filled, v_emptied = sem("v_filled"), sem("v_emptied")
        added = sem("added")
        picked = sem("picked")
        idx_stored = sem("idx_stored")
        idx_loaded = [sem(f"idx_loaded{p}") for p in range(4)]
        hot_ready = sem("hot_ready")
        muq_loaded = [sem(f"muq_loaded{i}") for i in range(2)]
        win_loaded = [sem(f"win_loaded{i}") for i in range(2)]
        head_loaded = sem("head_loaded")
        g_rotated = sem("g_rotated")
        q_rotated = sem("q_rotated")
        biased = sem("biased")
        inverted = sem("inverted")
        diag_ready = sem("diag_ready")
        vlink = sem("vlink")
        glink = sem("glink")

        blk = ctx.enter_context(nc.Block())

        def far_pairs(i):
            return range(PAIRS_B) if i % TILES else range(LOCAL // (2 * BLK), PAIRS_B)

        def step_place(u):
            return u // PAIRS_B, u % PAIRS_B

        def last_score(i):
            return A_AT[("score", i, len(halves(i)) - 1, IDX_HEADS - 1)]

        @blk.sync
        def _(sp):
            for i in range(-4, NT):
                n = i + 1
                if 0 <= n < NT:
                    if n >= 2:
                        sp.wait_ge(a_emptied, A_AT[("ctx", n - 2, PAIRS_B - 1)] + 1)
                    b, k = place(n)
                    if k == 0:
                        if b:
                            sp.wait_ge(a_emptied, A_AT[("ctx", n - TILES, PAIRS_B - 1)] + 1)
                        sp.dma_start(chead[:, :], cpad[b, 64:64 + HEAD_KEYS, :]).then_inc(head_loaded, 16)
                    for m in range(WIN // BLK):
                        lo = 128 * k + BLK * m
                        sp.dma_start(cwin[n % 2][BLK * m:BLK * (m + 1), :, :],
                                     cpad[b, lo:lo + 128, :].rearrange("(q p) c -> p q c", p=BLK)
                                     ).then_inc(win_loaded[n % 2], 16)
                    if n >= 2:
                        sp.wait_ge(q_rotated, 2 * (n - 1))
                    sp.dma_start(muq[n % 2][:, :, :].rearrange("p h r -> p (h r)"),
                                 muq_dram[n, :, :]
                                 ).then_inc(muq_loaded[n % 2], 16)
                if 0 <= i + 3 < NT:
                    m = i + 3
                    sp.wait_ge(picked, m + 1)
                    sp.dma_start(idx_dram[m % 2, :].rearrange("(p r) -> p r", r=FAR),
                                 idx16[m % 2][:, :]).then_inc(idx_stored, 16)
                    sp.wait_ge(idx_stored, 16 * (m + 1))
                    for p in chunks(m):
                        if m >= 1:
                            last = m - 1 if p in chunks(m - 1) else m - 2
                            if last >= 0:
                                sp.wait_ge(hot_ready, C_AT[(last, p)] + 1)
                        part = slice(1024 * p, 1024 * (p + 1))
                        sp.dma_start(idxb[:, part], idx_dram[m % 2, part].partition_broadcast(128)).then_inc(
                            idx_loaded[p], 16)

        @blk.gpsimd
        def _(pool):
            links = [0]

            def link(ins):
                links[0] += 1
                ins.then_inc(glink, 1)
                pool.wait_ge(glink, links[0])

            def rotate(dst, src, k, n):
                co, si = (trig[:, k, j, :].unsqueeze(1).broadcast_to([128, n, Q4]) for j in range(2))
                m1, m2 = src[:, :, 0:Q4], src[:, :, Q4:R]
                for out, m, a in ((0, m1, co), (1, m2, si), (2, m1, si), (3, m2, co)):
                    last = pool.tensor_tensor(tmp[out][:, 0:n, :], m, a, ALU.mult)
                link(last)
                pool.tensor_tensor(dst[:, :, 0:Q4], tmp[0][:, 0:n, :], tmp[1][:, 0:n, :], ALU.subtract)
                return pool.tensor_tensor(dst[:, :, Q4:R], tmp[2][:, 0:n, :], tmp[3][:, 0:n, :], ALU.add)

            def queries(n, k):
                if k == 0:
                    pool.wait_ge(muq_loaded[n % 2], 16 * (n // 2 + 1))
                    if n >= 1:
                        pool.wait_ge(a_emptied, A_AT[("QT", n - 1, 1)] + 1)
                dst = QN[:, :, 32 + 32 * k:64 + 32 * k]
                rotate(dst, muq[n % 2], TILES * k + n % TILES, HEADS).then_inc(q_rotated, 1)
                pool.wait_ge(q_rotated, 2 * n + k + 1)

            def far_keys(n, p):
                pool.wait_ge(v_emptied, V_AT[("gather", n, 2 * p + 1)] + 1)
                g = G[n % 2][:, 8 * p:8 * p + 8, C:]
                rotate(g, g, 2 * TILES, 8).then_inc(g_rotated, 1)
                pool.wait_ge(g_rotated, C_AT[(n, p)] + 1)

            def divisors(i, p):
                u = PAIRS_B * i + p
                pool.wait_ge(inverted, u + 1)
                if u >= 2:
                    pool.wait_ge(a_filled, A_AT[("PT", *step_place(u - 2))] + 1)
                pool.tensor_tensor(diag[u % 2][:, :, :], ident.unsqueeze(1).broadcast_to([128, 2, 128]),
                                   small[u % 2][:, 3, :].unsqueeze(2).broadcast_to([128, 2, 128]),
                                   ALU.mult).then_inc(diag_ready, 1)

            for i in range(-1, NT):
                n = i + 1
                for p in range(5):
                    if i >= 0 and p < 4:
                        divisors(i, p)
                    if n < NT and p in chunks(n):
                        far_keys(n, p)
                    if n < NT and p in (1, 2):
                        queries(n, p - 1)

        @blk.scalar
        def _(act):
            step = [0]

            def empty(key, dst, src, func=ACT.Copy):
                act.wait_ge(a_filled, A_AT[key] + 1)
                act.activation(dst, src, func).then_inc(a_emptied, 1)

            def ring(key):
                return RA[A_AT[key] % 4]

            def scores(i):
                for s, (lo, hi) in enumerate(halves(i)):
                    for h in range(IDX_HEADS):
                        k = step[0]
                        if k >= 2:
                            act.wait_ge(added, k - 1)
                        empty(("score", i, s, h), relu[k % 2][:, 0:hi - lo], ring(("score", i, s, h))[:, 0:hi - lo],
                              ACT.Relu)
                        step[0] += 1

            def exps(i, p):
                u = PAIRS_B * i + p
                act.wait_ge(biased, u + 1)
                w = SPAN if p in far_pairs(i) else HEAD_KEYS
                for k in range(2):
                    last = act.activation(P[u % 2][:, k, 0:w], ring(("S", i, p))[:, k * w:(k + 1) * w], ACT.Exp,
                                          scale=expo[:, 0:1], bias=small[u % 2][:, 1, k:k + 1],
                                          accum_out=small[u % 2][:, 2, k:k + 1])
                last.then_inc(a_emptied, 1)

            def weights_out(i, p):
                u = PAIRS_B * i + p
                key = ("PT", i, p)
                act.wait_ge(a_filled, A_AT[key] + 1)
                if u >= 2:
                    prior = (u - 2) // PAIRS_B, (u - 2) % PAIRS_B
                    act.wait_ge(a_emptied, A_AT[("ctx", *prior)] + 1)
                rows = WIN if p in far_pairs(i) else HEAD_KEYS
                last = act.activation(PT[u % 2][0:rows, 0:2, :],
                                      ring(key)[0:rows, 0:256].rearrange("p (k t) -> p k t", k=2), ACT.Copy)
                if p in far_pairs(i):
                    last = act.activation(PT[u % 2][:, 2:4, :],
                                          ring(key)[:, 256:512].rearrange("p (k t) -> p k t", k=2), ACT.Copy)
                last.then_inc(a_emptied, 1)

            def context_out(i, p):
                if i >= 1 and p == 0:
                    act.wait_ge(v_emptied, V_AT[("out", i - 1)] + 1)
                key = ("ctx", i, p)
                empty(key, CT[:, 32 * p:32 * p + 32, :], ring(key)[0:C, 0:256].rearrange("c (t h) -> c t h", h=HEADS))

            for i in range(-4, NT):
                n, m = i + 1, i + 4
                for p in range(5):
                    if i >= 0 and p < 4:
                        exps(i, p)
                    for tile, pair in attended(i, p):
                        context_out(tile, pair)
                    if p == 4 and 0 <= n < NT:
                        if n >= 1:
                            act.wait_ge(a_emptied, A_AT[("QT", n - 1, 1)] + 1)
                        empty(("cq", n), CQT[:, :], ring(("cq", n))[0:CQ, 0:128])
                    if p == 4 and m < NT:
                        key = ("qi", m)
                        if m >= 1:
                            act.wait_ge(a_emptied, last_score(m - 1) + 1)
                        empty(key, QI[:, :, :], ring(key)[0:64, :].rearrange("p (h t) -> p h t", h=IDX_HEADS))
                    if p == 4 and 0 <= n < NT:
                        key = ("qabs", n)
                        empty(key, QN[:, :, 0:C], ring(key)[:, 0:256].rearrange("p (h c) -> p h c", c=C))
                    if p == 4 and m < NT:
                        scores(m)
                    if p == 4 and 0 <= n < NT:
                        for h in range(2):
                            key = ("QT", n, h)
                            empty(key, QT[:, :, 4 * h:4 * h + 4],
                                  ring(key)[0:96, :].rearrange("c (h t) -> c t h", h=4))
                    if i >= 0 and p >= 1:
                        weights_out(i, p - 1)
                    for tile, chunk in turned(i, p):
                        for q in (2 * chunk, 2 * chunk + 1):
                            empty(("GT", tile, q), GT[:, q * 512:(q + 1) * 512], ring(("GT", tile, q))[0:64, :])
            context_out(NT - 1, PAIRS_B - 1)

        @blk.vector
        def _(dve):
            links, step = [0], [0]

            def link(ins):
                links[0] += 1
                ins.then_inc(vlink, 1)
                dve.wait_ge(vlink, links[0])

            def ring(key):
                dve.wait_ge(v_filled, V_AT[key] + 1)
                return RV[V_AT[key] % 4]

            def add_scores(i):
                I = score[i % 2]
                for s, (lo, hi) in enumerate(halves(i)):
                    for h in range(IDX_HEADS):
                        k = step[0]
                        dve.wait_ge(a_emptied, A_AT[("score", i, s, h)] + 1)
                        r = relu[k % 2][:, 0:hi - lo]
                        if h == 0:
                            ins = dve.tensor_scalar(I[:, lo:hi], r, idxw[:, 0:1], None, ALU.mult)
                        else:
                            ins = dve.scalar_tensor_tensor(I[:, lo:hi], r, idxw[:, h:h + 1], I[:, lo:hi],
                                                           ALU.mult, ALU.add)
                        ins.then_inc(added, 1)
                        dve.wait_ge(added, k + 1)
                        step[0] += 1
                w = width(i)
                link(dve.tensor_tensor(I[:, w - 128:w], I[:, w - 128:w], (late if i % TILES else early)[:, :], ALU.add))

            def pick(i, r, part):
                I = score[i % 2][:, 0:width(i)]
                if part == 0:
                    link(dve.max(best[:, r, :], I))
                elif part == 1:
                    link(dve.max_index(which[:, r, :], best[:, r, :], I))
                elif part == 2 and r < 3:
                    link(dve.match_replace(I, best[:, r, :], I, LOWEST * 1.1))
                elif part == 2:
                    if i >= 2:
                        dve.wait_ge(idx_stored, 16 * (i - 1))
                    dve.tensor_copy(idx16[i % 2][:, :], which[:, :, :].rearrange("p a k -> p (a k)")).then_inc(
                        picked, 1)

            def one_hot(i, p, part):
                tiles = [j for j in key_tiles(i, p) if j // 2 == part]
                if part == 0:
                    dve.wait_ge(idx_loaded[p], 16 * sum(p in chunks(j) for j in range(i + 1)))
                for j in tiles:
                    ins = dve.tensor_scalar(hot[:, j, 8 * p:8 * p + 8, :].rearrange("p g q -> p (g q)"),
                                            idxb[:, 1024 * p:1024 * (p + 1)], keyno[:, j:j + 1], None,
                                            ALU.is_equal)
                    if j == key_tiles(i, p)[-1]:
                        ins.then_inc(hot_ready, 1)

            def biases(i, p):
                u = PAIRS_B * i + p
                f = small[u % 2]
                w = SPAN if p in far_pairs(i) else HEAD_KEYS
                key = ("S", i, p)
                dve.wait_ge(a_filled, A_AT[key] + 1)
                if u >= 2:
                    dve.wait_ge(a_emptied, A_AT[("S", *step_place(u - 2))] + 1)
                link(dve.tensor_reduce(f[:, 0, :], RA[A_AT[key] % 4][:, 0:2 * w].rearrange("p (k c) -> p k c", k=2),
                                       AX.X, ALU.max))
                dve.tensor_scalar(f[:, 1, :], f[:, 0, :], expo[:, 1:2], None, ALU.mult).then_inc(biased, 1)

            def invert(i, p):
                u = PAIRS_B * i + p
                dve.wait_ge(a_emptied, A_AT[("S", i, p)] + 1)
                if u >= 2:
                    dve.wait_ge(diag_ready, u - 1)
                dve.reciprocal(small[u % 2][:, 3, :], small[u % 2][:, 2, :]).then_inc(inverted, 1)

            def out(i):
                o = ring(("out", i))
                dve.tensor_tensor(x_out[:, i, :], x[:, i, :], o[:, 0:D], ALU.add).then_inc(v_emptied, 1)

            for i in range(-4, NT):
                n, nn, nnn, m = i + 1, i + 2, i + 3, i + 4
                for p in range(5):
                    if i >= 0 and p < 4:
                        biases(i, p)
                    for g in range(4):
                        if 0 <= n < NT and p in chunks(n) and g % 2:
                            key = ("gather", n, 2 * p + g // 2)
                            ps = ring(key)[:, :].rearrange("p (g a d) -> p g d a", g=4, a=2)
                            if n >= 2 and g == 1:
                                dve.wait_ge(a_emptied, A_AT[("ctx", n - 2, PAIRS_B - 1)] + 1)
                            four = slice(8 * p + 2 * g - 2, 8 * p + 2 * g + 2)
                            dve.tensor_reduce(G[n % 2][:, four, :], ps, AX.X, ALU.add).then_inc(v_emptied, 1)
                        if 0 <= nn < NT and p - 1 in chunks(nn):
                            one_hot(nn, p - 1, g)
                        if 0 <= nnn < NT and p < 4:
                            pick(nnn, p, g)
                        if i >= 0 and p < 4 and g == 1:
                            invert(i, p)
                    if i >= 1 and p == 0:
                        out(i - 1)
                    if p == 4 and m < NT:
                        add_scores(m)
            out(NT - 1)

        @blk.tensor
        def _(pe):
            def ra(key, after=None):
                u = A_AT[key]
                need = max(u - 3, A_AT[after] + 1 if after else 0)
                if need > 0:
                    pe.wait_ge(a_emptied, need)
                return RA[u % 4]

            def rv(key, after=None):
                u = V_AT[key]
                need = max(u - 3, V_AT[after] + 1 if after else 0)
                if need > 0:
                    pe.wait_ge(v_emptied, need)
                return RV[u % 4]

            def index_queries(i):
                o = ra(("qi", i))
                tokens = xnT[:, 128 * i:128 * i + 128]
                for h in range(IDX_HEADS):
                    last = pe.matmul(o[0:64, h * 128:(h + 1) * 128], wiq[:, 64 * h:64 * h + 64], tokens,
                                     start=True, stop=True)
                last.then_inc(a_filled, 1)

            def index_scores(i):
                at = L * place(i)[0]
                for s, (lo, hi) in enumerate(halves(i)):
                    for h in range(IDX_HEADS):
                        o = ra(("score", i, s, h), ("qi", i))
                        pe.matmul(o[:, 0:hi - lo], QI[:, h, :], kiT[:, at + lo:at + hi],
                                  start=True, stop=True).then_inc(a_filled, 1)

            def queries(n):
                o = ra(("cq", n))
                pe.matmul(o[0:CQ, 0:128], wdq[:, :], xnT[:, 128 * n:128 * n + 128],
                          start=True, stop=True).then_inc(a_filled, 1)

            def absorbed(n):
                o = ra(("qabs", n), ("cq", n))
                pe.matmul(o[:, 0:256], CQT[:, :], absorb[:, :, :].rearrange("k h c -> k (h c)"),
                          start=True, stop=True).then_inc(a_filled, 1)

            def scores(i, p):
                far = p in far_pairs(i)
                w = SPAN if far else HEAD_KEYS
                b, tile = place(i)
                o = ra(("S", i, p), ("GT", i, 2 * p + 1) if p >= 2 else ("QT", i, 1))
                for k in range(2):
                    blk_no = 2 * p + k
                    q = QT[:, blk_no * BLK:(blk_no + 1) * BLK, :].rearrange("c t h -> c (t h)")
                    if far:
                        lo = 128 * tile + BLK * blk_no
                        pe.matmul(o[:, k * w:(k + 1) * w], identb, smask[:, :], start=True, stop=False)
                        pe.matmul(o[:, k * w:k * w + WIN], q, keyT[:, b, lo:lo + WIN], start=False, stop=False)
                        for g in range(4):
                            at = (4 * blk_no + g) * 128
                            last = pe.matmul(o[32 * g:32 * g + 32, k * w + WIN:(k + 1) * w],
                                             q[0:64, 32 * g:32 * g + 32], GT[:, at:at + 128],
                                             start=False, stop=True)
                    else:
                        last = pe.matmul(o[:, k * w:(k + 1) * w], q, keyT[:, b, 64:64 + w], start=True, stop=True)
                last.then_inc(a_filled, 1)

            def gather(n, p):
                pe.wait_ge(hot_ready, C_AT[(n, p)] + 1)
                tiles = key_tiles(n, p)
                first = TILES * place(n)[0]
                for g in range(2 * p, 2 * p + 2):
                    o = rv(("gather", n, g))
                    for k in range(4):
                        for j in tiles:
                            last = pe.matmul(o[:, 128 * k:128 * k + 128], hot[:, j, 4 * g + k, :],
                                             ctab[:, first + j, :, :].rearrange("s k d -> s (k d)"),
                                             start=(j == 0), stop=(j == tiles[-1]))
                    last.then_inc(v_filled, 1)

            def weights_turned(i, p):
                u = PAIRS_B * i + p
                pe.wait_ge(diag_ready, u + 1)
                o = ra(("PT", i, p))
                far = p in far_pairs(i)
                w = WIN if far else HEAD_KEYS
                for k in range(2):
                    last = pe.matmul(o[0:w, 128 * k:128 * k + 128], P[u % 2][:, k, 0:w], diag[u % 2][:, k, :],
                                     start=True, stop=True)
                if far:
                    for k in range(2):
                        last = pe.matmul(o[:, 256 + 128 * k:384 + 128 * k], P[u % 2][:, k, WIN:SPAN],
                                         diag[u % 2][:, k, :], start=True, stop=True)
                last.then_inc(a_filled, 1)

            def gathered_turned(n, p):
                pe.wait_ge(g_rotated, C_AT[(n, p)] + 1)
                for g in range(2):
                    o = ra(("GT", n, 2 * p + g))
                    for k in range(4):
                        last = pe.transpose(o[0:64, 128 * k:128 * k + 128], G[n % 2][:, 8 * p + 4 * g + k, :], ident)
                    last.then_inc(a_filled, 1)

            def attend(i, p):
                u = PAIRS_B * i + p
                o = ra(("ctx", i, p), ("PT", i, p))
                if p == 0:
                    pe.wait_ge(win_loaded[i % 2], 80 * (i // 2 + 1))
                    if i % TILES == 0:
                        pe.wait_ge(head_loaded, 16 * (i // TILES + 1))
                for k in range(2):
                    blk_no = 2 * p + k
                    part = slice(128 * k, 128 * k + 128)
                    if p not in far_pairs(i):
                        last = pe.matmul(o[0:C, part], chead[:, :], PT[u % 2][0:HEAD_KEYS, k, :],
                                         start=True, stop=True)
                        continue
                    pe.matmul(o[0:C, part], cwin[i % 2][:, blk_no, :], PT[u % 2][0:WIN, k, :],
                              start=True, stop=False)
                    for g in range(4):
                        last = pe.matmul(o[0:C, 128 * k + 32 * g:128 * k + 32 * g + 32],
                                         G[i % 2][:, 4 * blk_no + g, 0:C], PT[u % 2][:, 2 + k, 32 * g:32 * g + 32],
                                         start=False, stop=(g == 3))
                last.then_inc(a_filled, 1)

            def queries_turned(n):
                pe.wait_ge(q_rotated, 2 * n + 2)
                for h in range(2):
                    o = ra(("QT", n, h), ("qabs", n))
                    for k in range(4):
                        last = pe.transpose(o[0:96, 128 * k:128 * k + 128], QN[:, 4 * h + k, :], ident)
                    last.then_inc(a_filled, 1)

            def out(i):
                o = rv(("out", i))
                pe.wait_ge(a_emptied, A_AT[("ctx", i, PAIRS_B - 1)] + 1)
                for h in range(HEADS):
                    last = pe.matmul(o[:, 0:D], CT[:, :, h], wvo[:, h, :], start=(h == 0), stop=(h == HEADS - 1))
                last.then_inc(v_filled, 1)

            for i in range(-4, NT):
                n, m = i + 1, i + 4
                for p in range(5):
                    if i >= 0 and p < 4:
                        scores(i, p)
                    for tile, pair in attended(i, p):
                        attend(tile, pair)
                    if 0 <= n < NT and p in chunks(n):
                        gather(n, p)
                    if i >= 1 and p == 0:
                        out(i - 1)
                    if p == 4 and 0 <= n < NT:
                        queries(n)
                    if p == 4 and m < NT:
                        index_queries(m)
                    if p == 4 and 0 <= n < NT:
                        absorbed(n)
                    if p == 4 and m < NT:
                        index_scores(m)
                    if p == 4 and 0 <= n < NT:
                        queries_turned(n)
                    if i >= 0 and p >= 1:
                        weights_turned(i, p - 1)
                    for tile, chunk in turned(i, p):
                        gathered_turned(tile, chunk)
            attend(NT - 1, PAIRS_B - 1)
            out(NT - 1)


def attn_phase(nc, t, x, x_out, const, banks):
    ctx = ExitStack()

    def sb(name, shape, dt):
        return ctx.enter_context(nc.sbuf_tensor(name, shape, dt))

    def sem(name):
        return ctx.enter_context(nc.semaphore(name))

    A_AT, A_N, V_AT, V_N, C_AT, C_N = plan()
    with ctx:
        ident, identb = const["ident"], const["identb"]
        kiT = sb("kiT", [64, NT * 128], F32)
        xnT = sb("a_xnT", [128, NT * 128], F32)
        wiq = sb("wiq", [128, 256], F32)
        wdq = sb("wdq", [128, CQ], F32)
        keyT = sb("keyT", [96, B, 64 + L], F32)
        ctab = sb("ctab", [128, NT, 2, 64], FP16)
        expo = sb("expo", [128, 2], F32)
        trig = sb("trig", [128, 2 * TILES + 1, 2, Q4], F32)
        absorb = sb("absorb", [CQ, HEADS, C], F32)
        wvo = sb("wvo", [C, HEADS, D], F32)
        idxw = sb("idxw", [128, IDX_HEADS], F32)
        late = sb("late", [128, 128], F32)
        early = sb("early", [128, 128], F32)
        smask = sb("smask", [128, SPAN], BF16)
        keyno = sb("keyno", [128, TILES], F32)
        muq_dram = nc.dram_tensor("muq_dram", (NT, 128, HEADS * R), F32, kind="Internal").ap()
        cpad = nc.dram_tensor("cpad", (B, 64 + L, C), F32, kind="Internal").ap()
        idx_dram = nc.dram_tensor("idx_dram", (2, 128 * FAR), FP16, kind="Internal").ap()
        RA, RV = [banks[0], banks[1], banks[4], banks[6]], [banks[2], banks[3], banks[5], banks[7]]

        prep = ExitStack()
        with prep:
            def sb(name, shape, dt):
                return prep.enter_context(nc.sbuf_tensor(name, shape, dt))

            def sem(name):
                return prep.enter_context(nc.semaphore(name))

            stat = sb("a_stat", [128, 4, NT], F32)
            xc = sb("a_xc", [128, NT, D], F32)
            sq = sb("a_sq", [128, NT, D], F32)
            wkv = sb("wkv", [128, C + R], F32)
            cqT = sb("cqT", [CQ, NT * 128], F32)
            wqr = sb("wqr", [CQ, HEADS * R], F32)
            wik = sb("wik", [128, 64], F32)
            wuq = sb("wuq", [CQ, 512], F32)
            wuk = sb("wuk", [C, 512], F32)
            wuv = sb("wuv", [C, 512], F32)
            wout = sb("wout", [128, 4, D], F32)
            wuqT = sb("wuqT", [128, 4, CQ], F32)
            wukT = sb("wukT", [128, 4, C], F32)
            wuvT = sb("wuvT", [128, 4, C], F32)
            delta = sb("delta", [128, 6, Q4], F32)
            base = sb("base", [128, 2 * TILES + 1, 2, Q4], F32)
            tt = sb("tt", [128, 2 * TILES + 1, Q4], F32)
            peak = sb("peak", [128, 4], F32)
            peak_all = sb("peak_all", [1, 1], F32)
            ones = sb("a_ones", [1, 128], F32)
            kn = sb("kn", [128, NT, C + R], F32)
            sp_a = sb("sp_a", [128, NT, R], F32)
            key3 = sb("key3", [128, NT, 96], F32)
            val = sb("val", [128, NT, 64], F32)
            rt = sb("rt", [128, NT, Q4], F32)
            qsp = sb("qsp", [128, NT, HEADS * R], F32)

            loads = sem("a_loads")
            a_link = sem("a_link")
            v_link = sem("v_link")
            filled = sem("p_filled")
            emptied = sem("p_emptied")
            centred = sem("a_centred")
            squared = sem("a_squared")
            varied = sem("a_varied")
            rooted = sem("a_rooted")
            normed = sem("a_normed")
            kn_soft = sem("kn_soft")
            key_ready = sem("key_ready")
            key_filled = sem("key_filled")
            pads = sem("pads")
            cstored = sem("cstored")
            scaled = sem("scaled")
            peak_step = sem("peak_step")
            peak_made = sem("peak_made")
            wvo_scaled = sem("wvo_scaled")
            q_filled = sem("q_filled")
            q_abs = sem("q_abs")
            q_soft = sem("q_soft")
            muq_done = sem("muq_done")
            q_stored = sem("q_stored")
            quarter = sem("quarter")
            half_pi = sb("half_pi", [128, 1], F32)
            sined = sem("sined")
            NLOAD = 17

            order = ["wuqT", "wukT", "wuvT", "absorb0", "absorb1", "wvo0", "wvo1"] + [("xT", c) for c in range(NC)]
            order += [("kn", h) for h in range(2)] + [("cqT", c) for c in range(NC)] + [("kiT", c) for c in range(NC)]
            at = {k: u for u, k in enumerate(order)}
            blk = prep.enter_context(nc.Block())

            @blk.sync
            def _(sp):
                for dst, src in ((wkv[:, 0:C], t["attn_W_dkv"]), (wkv[:, C:], t["attn_W_kr"]), (wdq[:, :], t["attn_W_dq"]),
                                 (wqr[:, :], t["attn_W_qr"]), (wik[:, :], t["attn_idx_wk"]), (wiq[:, :], t["attn_idx_wq"]),
                                 (wuq[:, :], t["attn_W_uq"]), (wuk[:, :], t["attn_W_uk"]), (wuv[:, :], t["attn_W_uv"]),
                                 (wout[:, :, :], t["attn_W_out"].rearrange("(k p) n -> p k n", p=128)),
                                 (idxw[:, :], t["attn_idx_w"].partition_broadcast(128)),
                                 (delta[:, 0, :], t["attn_raw_delta"].partition_broadcast(128)),
                                 (base[:, :, :, :], t["trig"]), (late[:, :], t["late"]), (early[:, :], t["early"]),
                                 (smask[:, :].bitcast(mybir.dt.uint16), t["smask"]), (keyno[:, :], t["keyno"])):
                    sp.dma_start(dst, src).then_inc(loads, 16)
                sp.wait_ge(pads, 3)
                for b in range(B):
                    sp.dma_start(cpad[b, 0:64, :], key3[0:64, b, 32:64]).then_inc(cstored, 16)
                sp.wait_ge(scaled, 1)
                for b in range(B):
                    sp.dma_start(cpad[b, 64:64 + L, :].rearrange("(n p) c -> p n c", p=128),
                                 val[:, TILES * b:TILES * (b + 1), 0:C]).then_inc(cstored, 16)
                for c in range(4):
                    sp.wait_ge(muq_done, 2 * c + 2)
                    sp.dma_start(muq_dram[4 * c:4 * c + 4, :, :].rearrange("n p c -> p n c"),
                                 qsp[:, 4 * c:4 * c + 4, :]).then_inc(q_stored, 16)
                sp.wait_ge(cstored, 64)
                sp.wait_ge(q_stored, 64)

            @blk.gpsimd
            def _(pool):
                pool.memset(half_pi[:, :], PI / 2).then_inc(quarter, 1)
                pool.memset(ones[:, :], 1.0).then_inc(pads, 1)
                pool.memset(key3[:, :, 32:64], 0.0).then_inc(pads, 1)
                pool.memset(keyT[:, :, 0:64], 0.0).then_inc(pads, 1)

            @blk.scalar
            def _(act):
                links = [0]

                def link(ins):
                    links[0] += 1
                    ins.then_inc(a_link, 1)
                    act.wait_ge(a_link, links[0])

                act.wait_ge(loads, 16 * NLOAD)
                link(act.activation(delta[:, 1, :], delta[:, 0, :], ACT.Sigmoid))
                link(act.activation(delta[:, 2, :], delta[:, 1, :], ACT.Sin, scale=-PI))
                act.wait_ge(quarter, 1)
                act.activation(delta[:, 3, :], delta[:, 1, :], ACT.Sin, scale=-PI, bias=half_pi[:, :]).then_inc(sined, 1)
                act.wait_ge(centred, 1)
                act.activation(sq[:, :, :], xc[:, :, :], ACT.Square).then_inc(squared, 1)
                act.wait_ge(varied, 1)
                act.activation(stat[:, 2, :], stat[:, 1, :], ACT.Sqrt).then_inc(rooted, 1)

                def empty(key, dst, src):
                    act.wait_ge(filled, at[key] + 1)
                    act.activation(dst, src, ACT.Copy).then_inc(emptied, 1)

                def bank(key):
                    return banks[at[key] % 8]

                empty("wuqT", wuqT[:, :, :], bank("wuqT")[:, 0:4 * CQ].rearrange("p (k c) -> p k c", k=4))
                empty("wukT", wukT[:, :, :], bank("wukT")[:, 0:4 * C].rearrange("p (k c) -> p k c", k=4))
                empty("wuvT", wuvT[:, :, :], bank("wuvT")[:, 0:4 * C].rearrange("p (k c) -> p k c", k=4))
                for s in range(2):
                    empty(f"absorb{s}", absorb[:, :, :].rearrange("p (j s) c -> p s j c", s=2)[:, s, :, :],
                          bank(f"absorb{s}")[0:CQ, 0:128].rearrange("p (j c) -> p j c", c=C))
                for s in range(2):
                    empty(f"wvo{s}", wvo[:, :, :].rearrange("p (j s) c -> p s j c", s=2)[:, s, :, :],
                          bank(f"wvo{s}")[0:C, :].rearrange("p (j d) -> p j d", d=D))
                for c in range(NC):
                    empty(("xT", c), xnT[:, c * 512:(c + 1) * 512], bank(("xT", c))[:, :])
                for h in range(2):
                    empty(("kn", h), kn[:, 8 * h:8 * h + 8, :],
                          bank(("kn", h))[:, :].rearrange("p (n c) -> p n c", c=64))
                act.wait_ge(emptied, at[("kn", 1)] + 1)
                link(act.activation(sp_a[:, :, :], kn[:, :, C:], ACT.Abs))
                link(act.activation(sp_a[:, :, :], sp_a[:, :, :], ACT.Exp, scale=-1.0))
                act.activation(sp_a[:, :, :], sp_a[:, :, :], ACT.Ln, bias=1.0).then_inc(kn_soft, 1)
                for c in range(NC):
                    empty(("cqT", c), cqT[:, c * 512:(c + 1) * 512], bank(("cqT", c))[0:CQ, :])
                for c in range(NC):
                    empty(("kiT", c), kiT[:, c * 512:(c + 1) * 512], bank(("kiT", c))[0:64, :])
                for c in range(NT // 2):
                    act.wait_ge(q_filled, c + 1)
                    act.activation(qsp[:, 2 * c:2 * c + 2, :], banks[c][:, :].rearrange("p (n c) -> p n c", n=2),
                                   ACT.Abs).then_inc(q_abs, 1)
                act.wait_ge(q_abs, NT // 2)
                link(act.activation(qsp[:, :, :], qsp[:, :, :], ACT.Exp, scale=-1.0))
                for c in range(NT // 2):
                    two = qsp[:, 2 * c:2 * c + 2, :]
                    act.activation(two, two, ACT.Ln, bias=1.0).then_inc(q_soft, 1)
                for c in range(NC):
                    dst = keyT[:, c // 2, 64 + (c % 2) * 512:64 + (c % 2 + 1) * 512]
                    act.wait_ge(key_filled, c + 1)
                    act.activation(dst, banks[c][0:96, :], ACT.Copy)

            @blk.vector
            def _(dve):
                links = [0]

                def link(ins):
                    links[0] += 1
                    ins.then_inc(v_link, 1)
                    dve.wait_ge(v_link, links[0])

                def over(ap):
                    return ap.unsqueeze(2).broadcast_to([128, NT, D])

                link(dve.tensor_reduce(stat[:, 0, :], x[:, :, :], AX.X, ALU.add))
                link(dve.tensor_scalar(stat[:, 0, :], stat[:, 0, :], 1.0 / D, None, ALU.mult))
                dve.tensor_tensor(xc[:, :, :], x[:, :, :], over(stat[:, 0, :]), ALU.subtract).then_inc(centred, 1)
                dve.wait_ge(squared, 1)
                link(dve.tensor_reduce(stat[:, 1, :], sq[:, :, :], AX.X, ALU.add))
                dve.tensor_scalar(stat[:, 1, :], stat[:, 1, :], 1.0 / D, LN_EPS, ALU.mult, ALU.add).then_inc(varied, 1)
                dve.wait_ge(rooted, 1)
                link(dve.reciprocal(stat[:, 3, :], stat[:, 2, :]))
                dve.wait_ge(centred, 1)
                dve.tensor_tensor(xc[:, :, :], xc[:, :, :], over(stat[:, 3, :]), ALU.mult).then_inc(normed, 1)

                dve.wait_ge(loads, 16 * NLOAD)
                dve.wait_ge(sined, 1)
                sh, ch, sd, cd = (delta[:, k, :] for k in (2, 3, 4, 5))
                link(dve.tensor_tensor(sd, sh, ch, ALU.mult))
                link(dve.tensor_scalar(sd, sd, 2.0, None, ALU.mult))
                link(dve.tensor_tensor(cd, sh, sh, ALU.mult))
                link(dve.tensor_scalar(cd, cd, -2.0, 1.0, ALU.mult, ALU.add))
                n = 2 * TILES + 1

                def wide(ap):
                    return ap.unsqueeze(1).broadcast_to([128, n, Q4])

                for k, sign in ((0, ALU.subtract), (1, ALU.add)):
                    link(dve.tensor_tensor(trig[:, :, k, :], base[:, :, k, :], wide(cd), ALU.mult))
                    link(dve.tensor_tensor(tt[:, :, :], base[:, :, 1 - k, :], wide(sd), ALU.mult))
                    link(dve.tensor_tensor(trig[:, :, k, :], trig[:, :, k, :], tt[:, :, :], sign))

                dve.wait_ge(kn_soft, 1)
                dve.scalar_tensor_tensor(val[:, :, C:], kn[:, :, C:], 0.0, sp_a[:, :, :], ALU.max, ALU.add)
                link(dve.tensor_copy(val[:, :, 0:C], kn[:, :, 0:C]))
                dve.tensor_reduce(peak[:, 0:1], val[:, :, :].rearrange("p n c -> p (n c)"), AX.X, ALU.max,
                                  apply_absolute_value=True).then_inc(peak_made, 1)
                dve.wait_ge(peak_step, 1)
                dve.tensor_reduce(peak_all[:, :], banks[7][0:1, 0:128], AX.X, ALU.max).then_inc(peak_made, 1)
                dve.wait_ge(peak_step, 2)
                link(dve.tensor_scalar(peak[:, 1:2], banks[7][:, 128:129], 2.0 ** -100, None, ALU.max))
                link(dve.tensor_scalar(peak[:, 2:3].bitcast(mybir.dt.int32), peak[:, 1:2].bitcast(mybir.dt.int32),
                                       0x7F800000, None, ALU.bitwise_and))
                link(dve.reciprocal(peak[:, 3:4], peak[:, 2:3]))
                dve.tensor_scalar(peak[:, 3:4], peak[:, 3:4], 2.0 ** 14, None, ALU.mult)
                dve.tensor_scalar(peak[:, 2:3], peak[:, 2:3], 2.0 ** -14, None, ALU.mult).then_inc(peak_made, 1)
                dve.wait_ge(peak_made, 3)
                link(dve.tensor_scalar(expo[:, 0:1], peak[:, 2:3], SCALE, None, ALU.mult))
                dve.tensor_scalar(expo[:, 1:2], peak[:, 2:3], -SCALE, None, ALU.mult)
                dve.tensor_scalar(val[:, :, :], val[:, :, :], peak[:, 3:4], None, ALU.mult).then_inc(scaled, 1)
                dve.wait_ge(scaled, 1)
                dve.wait_ge(emptied, at["wvo1"] + 1)
                dve.tensor_scalar(wvo[:, :, :], wvo[:, :, :], peak[0:C, 2:3], None, ALU.mult)
                dve.wait_ge(pads, 3)
                link(dve.tensor_copy(key3[:, :, 0:C], val[:, :, 0:C]))
                for b in range(B):
                    n = slice(TILES * b, TILES * (b + 1))
                    co, si = trig[:, 0:TILES, 0, :], trig[:, 0:TILES, 1, :]
                    m1, m2 = val[:, n, C:C + Q4], val[:, n, C + Q4:]
                    for dst, a, z, op in ((slice(64, 80), co, si, ALU.subtract), (slice(80, 96), si, co, ALU.add)):
                        link(dve.tensor_tensor(key3[:, n, dst], m1, a, ALU.mult))
                        link(dve.tensor_tensor(rt[:, n, :], m2, z, ALU.mult))
                        last = dve.tensor_tensor(key3[:, n, dst], key3[:, n, dst], rt[:, n, :], op)
                        if b == 0 or op == ALU.subtract:
                            link(last)
                last.then_inc(key_ready, 1)
                link(dve.tensor_copy(ctab[:, :, 0, :], val[:, :, :]))
                link(dve.tensor_tensor(kn[:, :, :], val[:, :, :], ctab[:, :, 0, :], ALU.subtract))
                link(dve.tensor_copy(ctab[:, :, 1, :], kn[:, :, :]))
                for c in range(NT // 2):
                    dve.wait_ge(q_soft, c + 1)
                    two = qsp[:, 2 * c:2 * c + 2, :].rearrange("p n c -> p (n c)")
                    dve.scalar_tensor_tensor(two, banks[c][:, :], 0.0, two, ALU.max, ALU.add).then_inc(muq_done, 1)

            @blk.tensor
            def _(pe):
                def bank(key):
                    if at[key] >= 8:
                        pe.wait_ge(emptied, at[key] - 7)
                    return banks[at[key] % 8]

                pe.wait_ge(loads, 16 * NLOAD)
                for key, src, rows in (("wuqT", wuq, CQ), ("wukT", wuk, C), ("wuvT", wuv, C)):
                    o = bank(key)
                    for k in range(4):
                        last = pe.transpose(o[:, k * rows:(k + 1) * rows], src[:, k * 128:(k + 1) * 128],
                                            ident[0:rows, 0:rows])
                    last.then_inc(filled, 1)
                pe.wait_ge(emptied, at["wuvT"] + 1)
                for s in range(2):
                    rows = slice(64 * s, 64 * s + 64)
                    o = bank(f"absorb{s}")
                    for j in range(4):
                        last = pe.matmul(o[0:CQ, j * C:(j + 1) * C], wuqT[rows, j, :], wukT[rows, j, :],
                                         start=True, stop=True)
                    last.then_inc(filled, 1)
                for s in range(2):
                    rows = slice(64 * s, 64 * s + 64)
                    o = bank(f"wvo{s}")
                    for j in range(4):
                        last = pe.matmul(o[0:C, j * D:(j + 1) * D], wuvT[rows, j, :], wout[rows, j, :],
                                         start=True, stop=True)
                    last.then_inc(filled, 1)
                pe.wait_ge(normed, 1)
                for c in range(NC):
                    o = bank(("xT", c))
                    for k in range(4):
                        last = pe.transpose(o[:, k * 128:(k + 1) * 128], xc[:, 4 * c + k, :], ident)
                    last.then_inc(filled, 1)
                for g in range(2):
                    o = bank(("kn", g))
                    pe.wait_ge(emptied, at[("xT", 2 * g + 1)] + 1)
                    for k in range(8):
                        n = 8 * g + k
                        last = pe.matmul(o[:, k * 64:(k + 1) * 64], xnT[:, n * 128:(n + 1) * 128], wkv[:, :],
                                         start=True, stop=True)
                    last.then_inc(filled, 1)
                for c in range(NC):
                    pe.matmul(bank(("cqT", c))[0:CQ, :], wdq[:, :], xnT[:, c * 512:(c + 1) * 512],
                              start=True, stop=True).then_inc(filled, 1)
                for c in range(NC):
                    pe.matmul(bank(("kiT", c))[0:64, :], wik[:, :], xnT[:, c * 512:(c + 1) * 512],
                              start=True, stop=True).then_inc(filled, 1)
                pe.wait_ge(emptied, at[("kiT", NC - 1)] + 1)
                for c in range(NT // 2):
                    if c == 5:
                        pe.wait_ge(peak_made, 1)
                        pe.transpose(banks[7][0:1, 0:128], peak[:, 0:1], ident).then_inc(peak_step, 1)
                    if c == 7:
                        pe.wait_ge(pads, 3)
                        pe.wait_ge(peak_made, 2)
                        pe.matmul(banks[7][:, 128:129], ones[:, :], peak_all[:, :], start=True,
                                  stop=True).then_inc(peak_step, 1)
                        pe.wait_ge(peak_made, 3)
                    for k in range(2):
                        n = 2 * c + k
                        last = pe.matmul(banks[c][:, k * 256:(k + 1) * 256], cqT[:, n * 128:(n + 1) * 128], wqr[:, :],
                                         start=True, stop=True)
                    last.then_inc(q_filled, 1)
                pe.wait_ge(key_ready, 1)
                for c in range(NC):
                    pe.wait_ge(muq_done, c + 1)
                    for k in range(4):
                        last = pe.transpose(banks[c][0:96, k * 128:(k + 1) * 128], key3[:, 4 * c + k, :], ident)
                    last.then_inc(key_filled, 1)
        attn_loop(nc, t, x, x_out, ident, identb, xnT, kiT, wiq, wdq, keyT, ctab, muq_dram, trig, absorb, wvo, expo, idxw, late, early, smask,
                  keyno, cpad, idx_dram, RA, RV, A_AT, A_N, V_AT, V_N, C_AT, C_N)


def macaron_kernel(nc, t, out):
    ctx = ExitStack()
    with ctx:
        def sb(name, shape, dt):
            return ctx.enter_context(nc.sbuf_tensor(name, shape, dt))

        xs = sb("xs", [128, NT, D], F32)
        ident = sb("ident", [128, 128], F32)
        identb = sb("identb", [128, 128], BF16)
        sel = sb("sel", [97, PAIRS // 2 + 1, 128], BF16)
        banks = [ctx.enter_context(nc.psum_tensor(f"bank{i}", [128, 512], F32)) for i in range(8)]
        start_loaded = ctx.enter_context(nc.semaphore("start_loaded"))
        stored = ctx.enter_context(nc.semaphore("stored"))

        with nc.Block() as blk:
            @blk.sync
            def _(sp):
                sp.dma_start(xs[:, :, :], t["x"].rearrange("b (n p) d -> p (b n) d", p=128)).then_inc(start_loaded, 16)
                sp.dma_start(ident[:, :], t["ident"]).then_inc(start_loaded, 16)
                sp.dma_start(identb[:, :].bitcast(mybir.dt.uint16), t["identb"]).then_inc(start_loaded, 16)
                sp.dma_start(sel[:, :, :].bitcast(mybir.dt.uint16), t["sel"]).then_inc(start_loaded, 16)
                sp.wait_ge(start_loaded, 64)

        const = {"ident": ident[:, :], "identb": identb[:, :], "sel": sel}
        w = {k: t[f"ffn_{n}"] for k, n in (("router", "router_w"), ("sgate", "shared_gate_w"), ("sup", "shared_up_w"),
                                           ("sdown", "shared_down_w"), ("gate", "expert_gate_k"),
                                           ("up", "expert_up_k"), ("down", "expert_down_k"))}
        ffn_phase(nc, "f1", xs[:, :, :], xs, w, const, banks)
        attn_phase(nc, t, xs, xs, const, banks)
        ffn_phase(nc, "f2", xs[:, :, :], xs, w, const, banks)
    
        with nc.Block() as blk:
            @blk.sync
            def _(sp):
                sp.dma_start(out.rearrange("b (n p) d -> p (b n) d", p=128), xs[:, :, :]).then_inc(stored, 16)
                sp.wait_ge(stored, 16)


_FFN = ['ffn_router_w', 'ffn_shared_gate_w', 'ffn_shared_up_w', 'ffn_shared_down_w', 'ffn_expert_gate_k',
        'ffn_expert_up_k', 'ffn_expert_down_k']
_ATTN = ['attn_W_dkv', 'attn_W_uk', 'attn_W_uv', 'attn_W_dq', 'attn_W_uq', 'attn_W_qr', 'attn_W_kr', 'attn_W_out',
         'attn_idx_wq', 'attn_idx_wk', 'attn_idx_w', 'attn_raw_delta']


def _constants():
    import numpy as np
    one = 0x3F80
    c = {"ident": np.eye(128, dtype=np.float32), "identb": (np.eye(128) * one).astype(np.uint16)}
    sel = np.zeros((97, PAIRS // 2 + 1, 128), np.uint16)
    for part in range(3):
        for q in range(PAIRS // 2):
            for s in range(2):
                sel[part * 32 + 2 * q + s, q, 64 * s:64 * s + 64] = one
    sel[96, PAIRS // 2, :] = one
    c["sel"] = sel
    c.update(_attn_constants())
    return c


def kernel(**inputs):
    import numpy as _np
    import concourse.bacc as _bacc
    from concourse import mybir as _mybir
    from concourse.bass_utils import run_bass_kernel_spmd as _run

    nc = _bacc.Bacc("TRN2", target_bir_lowering=False, num_devices=1)
    arrays, t = {}, {}

    def take(name, a):
        arrays[f"in_{name}_dram"] = a
        t[name] = nc.dram_tensor(f"in_{name}_dram", a.shape, _mybir.dt.from_np(a.dtype), kind="ExternalInput").ap()

    take("x", _np.ascontiguousarray(inputs["L0_attn_x"]))
    for name in _FFN + _ATTN:
        take(name, _np.ascontiguousarray(inputs["L0_" + name]))
    for name, a in _constants().items():
        take(name, a)
    out = nc.dram_tensor("out_0_dram", (B, L, D), _mybir.dt.float32, kind="ExternalOutput").ap()
    macaron_kernel(nc, t, out)
    r = _run(nc, [arrays], core_ids=[0])
    return r.results[0]["out_0_dram"]
```

```python
import concourse.bass as bass
from concourse import mybir
from contextlib import ExitStack

F32 = mybir.dt.float32
F32R = mybir.dt.float32r
BF16 = mybir.dt.bfloat16
FP16 = mybir.dt.float16
ALU = mybir.AluOpType
ACT = mybir.ActivationFunctionType
AX = mybir.AxisListType

B, L, D = 2, 1024, 128
NT = B * L // 128
EXPERTS, WIDE, TOPK = 64, 64, 8
CHUNK = 512
NC = B * L // CHUNK
PAIRS = EXPERTS // 2
LN_EPS = 1e-5
LOWEST = -3.0e38


def ln_statistics(dve, link, x, stats, moments, g, varied):
    for t in range(4 * g, 4 * g + 4):
        last = dve.bn_stats(stats[:, t, :], x[:, t, :])
    link(last)
    for t in range(4 * g, 4 * g + 4):
        last = dve.bn_aggr(moments[:, t, 0:2], stats[:, t, :])
    link(last)
    four = moments[:, 4 * g:4 * g + 4, :]
    dve.tensor_scalar(four[:, :, 2], four[:, :, 1], LN_EPS, None, ALU.add).then_inc(varied, 1)


def ln_apply(dve, link, x, xn, moments, g, rooted, normed):
    dve.wait_ge(rooted, g + 1)
    four = moments[:, 4 * g:4 * g + 4, :]
    link(dve.reciprocal(four[:, :, 4], four[:, :, 3]))
    for t in range(4 * g, 4 * g + 4):
        last = dve.tensor_scalar(xn[:, t, :], x[:, t, :], moments[:, t, 0:1], moments[:, t, 4:5],
                                 ALU.subtract, ALU.mult)
    last.then_inc(normed, 1)


def ln_root(act, moments, varied, rooted, g):
    four = moments[:, 4 * g:4 * g + 4, :]
    act.wait_ge(varied, g + 1)
    act.activation(four[:, :, 3], four[:, :, 2], ACT.Sqrt).then_inc(rooted, 1)


def ffn_phase(nc, tag, x, x_out, w, const, banks):
    ctx = ExitStack()

    def sb(name, shape, dt):
        return ctx.enter_context(nc.sbuf_tensor(f"{name}_{tag}", shape, dt))

    def sem(name):
        return ctx.enter_context(nc.semaphore(f"{name}_{tag}"))

    with ctx:
        stats = sb("stats", [128, NT, 6], F32)
        moments = sb("moments", [128, NT, 5], F32)
        xn = sb("xn", [128, NT, D], F32)
        xnT = sb("xnT", [128, NT * 128], F32)
        xhi = sb("xhi", [128, NT * 128], F32R)
        xlo = sb("xlo", [128, NT * 128], F32R)
        rw = sb("rw", [128, EXPERTS], F32)
        lg = sb("lg", [128, NT, EXPERTS], F32)
        rep = sb("rep", [128, NT, EXPERTS], F32)
        top = sb("top", [128, NT, 8], F32)
        aff = sb("aff", [128, NT, EXPERTS], F32)
        wsum = sb("wsum", [128, 2, NT], F32)
        wpart = sb("wpart", [128, NT, 2, 3, 32], BF16)
        maskT = sb("maskT", [96, 2, NT * 128], BF16)
        ones = sb("ones", [1, CHUNK], BF16)
        raw = [sb(f"raw{i}", [128, 3, 128], F32) for i in range(2)]
        whi = [sb(f"whi{i}", [128, 3, 128], F32R) for i in range(2)]
        wlo = [sb(f"wlo{i}", [128, 3, 128], F32R) for i in range(2)]
        silu = [sb(f"silu{i}", [128, CHUNK], F32) for i in range(2)]
        gated = [sb(f"gated{i}", [128, CHUNK], F32) for i in range(2)]
        act = [sb(f"act{i}", [128, CHUNK], F32) for i in range(2)]
        ahi = [sb(f"ahi{i}", [128, CHUNK], F32R) for i in range(4)]
        alo = [sb(f"alo{i}", [128, CHUNK], F32R) for i in range(4)]
        yT = sb("yT", [128, NT * 128], F32)

        acc = banks[0:4]
        gate_ps, up_ps, mask_ps = banks[4:6], banks[6], banks[7]
        LG = [banks[6], banks[7]]
        ident, identb, sel = const["ident"], const["identb"], const["sel"]

        router_loaded = sem("router_loaded")
        loaded = [sem(f"loaded{i}") for i in range(2)]
        split_done = sem("split_done")
        zeroed = sem("zeroed")
        varied = sem("varied")
        rooted = sem("rooted")
        normed = sem("normed")
        pool_turn = sem("pool_turn")
        xT_ready = sem("xT_ready")
        xT_raw = sem("xT_raw")
        xT_high = sem("xT_high")
        xT_split = sem("xT_split")
        logits_ready = sem("logits_ready")
        logits_out = sem("logits_out")
        affinity_ready = sem("affinity_ready")
        dve_link = sem("dve_link")
        sums_ready = sem("sums_ready")
        weights_ready = sem("weights_ready")
        part_made = sem("part_made")
        rest_made = sem("rest_made")
        parts_ready = sem("parts_ready")
        maskT_ps = sem("maskT_ps")
        maskT_done = sem("maskT_done")
        gate_done = sem("gate_done")
        up_done = sem("up_done")
        mask_done = sem("mask_done")
        silu_done = sem("silu_done")
        gated_done = sem("gated_done")
        act_done = sem("act_done")
        ahi_done = sem("ahi_done")
        alo_done = sem("alo_done")
        down_done = sem("down_done")
        yT_done = sem("yT_done")
        y_done = sem("y_done")
        x_done = sem("x_done")

        LAG = 3

        blk = ctx.enter_context(nc.Block())

        @blk.sync
        def _(sp):
            sp.dma_start(rw[:, :], w["router"]).then_inc(router_loaded, 16)
            sp.wait_ge(zeroed, 1)
            sp.dma_start(raw[0][:, 0, 0:WIDE], w["sgate"]).then_inc(loaded[0], 16)
            sp.dma_start(raw[0][:, 1, 0:WIDE], w["sup"]).then_inc(loaded[0], 16)
            sp.dma_start(raw[0][0:WIDE, 2, :], w["sdown"]).then_inc(loaded[0], 16)

            def load(u, slot, e):
                if not (isinstance(u, int) and u < 2):
                    sp.wait_ge(split_done, 4 * (u - 1))
                g = w["gate"][bass.ds(e, 2), :, :].rearrange("e h i -> h e i")
                v = w["up"][bass.ds(e, 2), :, :].rearrange("e h i -> h e i")
                d = w["down"].rearrange("e i h -> (e i) h")[bass.ds(e * WIDE, 2 * WIDE), :]
                sp.dma_start(raw[slot][:, 0, :].rearrange("h (e i) -> h e i", e=2), g).then_inc(loaded[slot], 16)
                sp.dma_start(raw[slot][:, 1, :].rearrange("h (e i) -> h e i", e=2), v).then_inc(loaded[slot], 16)
                sp.dma_start(raw[slot][:, 2, :], d).then_inc(loaded[slot], 16)

            load(1, 1, 0)
            load(2, 0, PAIRS)
            with sp.Fori(3, PAIRS, 2) as u:
                load(u, 1, u - 1)
                load(u + 1, 0, u + (PAIRS - 1))

        @blk.gpsimd
        def _(pool):
            pool.memset(raw[0][:, :, :], 0.0).then_inc(zeroed, 1)
            pool.memset(ones[:, :], 1.0).then_inc(zeroed, 1)

            def split(u, slot, n):
                pool.wait_ge(loaded[slot], 48 * n)
                for part, used, step in ((slice(0, 2), up_done, 0), (slice(2, 3), down_done, 2)):
                    if not (isinstance(u, int) and u < 2):
                        pool.wait_ge(used, 4 * (u - 1))
                    pool.sem_inc(pool_turn, 1)
                    pool.tensor_copy(whi[slot][:, part, :], raw[slot][:, part, :]).then_inc(split_done, 1)
                    pool.wait_ge(split_done, 4 * u + (step + 1))
                    pool.tensor_tensor(wlo[slot][:, part, :], raw[slot][:, part, :],
                                       whi[slot][:, part, :].bitcast(F32), ALU.subtract).then_inc(split_done, 1)

            split(0, 0, 1)
            split(1, 1, 1)
            for c in range(NC):
                part = slice(c * CHUNK, (c + 1) * CHUNK)
                pool.wait_ge(xT_high, c + 1)
                pool.tensor_tensor(xlo[:, part], xnT[:, part], xhi[:, part].bitcast(F32),
                                   ALU.subtract).then_inc(xT_split, 1)
            for h in range(2):
                half = slice(8 * h, 8 * h + 8)
                pool.wait_ge(sums_ready, h + 1)
                pool.tensor_tensor(aff[:, half, :], aff[:, half, :],
                                   wsum[:, 1, half].unsqueeze(2).broadcast_to([128, 8, EXPERTS]),
                                   ALU.mult).then_inc(weights_ready, 1)
                full = aff[:, half, :].rearrange("p t (c e) -> p (t c) e", c=2)
                for i in range(2):
                    pool.wait_ge(part_made, 2 * h + i + 1)
                    pool.tensor_tensor(full, full, wpart[:, half, :, i, :].rearrange("p t c e -> p (t c) e"),
                                       ALU.subtract).then_inc(rest_made, 1)
            split(2, 0, 2)
            with pool.Fori(1, PAIRS // 2) as j:
                split(2 * j + 1, 1, j + 1)
                split(2 * j + 2, 0, j + 2)

        @blk.scalar
        def _(act_e):
            for g in range(NT // 4):
                ln_root(act_e, moments, varied, rooted, g)

            def transposed(c):
                act_e.wait_ge(xT_ready, c + 1)
                part = slice(c * CHUNK, (c + 1) * CHUNK)
                act_e.activation(xnT[:, part], acc[c][:, :], ACT.Copy).then_inc(xT_raw, 1)
                act_e.activation(xhi[:, part], acc[c][:, :], ACT.Copy).then_inc(xT_high, 1)

            for h in range(2):
                transposed(2 * h)
                transposed(2 * h + 1)
            for h in range(2):
                half = slice(8 * h, 8 * h + 8)
                act_e.wait_ge(logits_ready, h + 1)
                act_e.activation(lg[:, half, :], LG[h][:, :].rearrange("p (t e) -> p t e", e=EXPERTS),
                                 ACT.Copy).then_inc(logits_out, 1)
                act_e.wait_ge(logits_out, h + 1)
                act_e.activation(aff[:, half, :], lg[:, half, :], ACT.Sigmoid).then_inc(affinity_ready, 1)

            def parts(h):
                half = slice(8 * h, 8 * h + 8)
                full = aff[:, half, :].rearrange("p t (c e) -> p (t c) e", c=2)
                for i in range(3):
                    if i == 0:
                        act_e.wait_ge(weights_ready, h + 1)
                    else:
                        act_e.wait_ge(rest_made, 2 * h + i)
                    act_e.activation(wpart[:, half, :, i, :].rearrange("p t c e -> p (t c) e"), full,
                                     ACT.Copy).then_inc(parts_ready if i == 2 else part_made, 1)

            def masks(c):
                act_e.wait_ge(maskT_ps, c + 1)
                act_e.activation(maskT[:, :, c * CHUNK:(c + 1) * CHUNK],
                                 acc[2 + c % 2][0:96, :].bitcast(BF16).rearrange("p (k t) -> p k t", k=2),
                                 ACT.Copy).then_inc(maskT_done, 1)

            def step(k, m):
                act_e.wait_ge(gate_done, k + 1)
                if not (isinstance(k, int) and k < 2):
                    act_e.wait_ge(gated_done, k - 1)
                act_e.activation(silu[m % 2][:, :], gate_ps[m % 2][:, :], ACT.Silu).then_inc(silu_done, 1)

            def high(k, m):
                act_e.wait_ge(act_done, k + 1)
                if not (isinstance(k, int) and k < 4):
                    act_e.wait_ge(down_done, k - 3)
                act_e.activation(ahi[m % 4][:, :], act[m % 2][:, :], ACT.Copy).then_inc(ahi_done, 1)

            parts(0)
            step(0, 0)
            step(1, 1)
            parts(1)
            high(0, 0)
            masks(0)
            masks(1)
            step(2, 2)
            high(1, 1)
            masks(2)
            masks(3)
            step(3, 3)
            high(2, 2)
            with act_e.Fori(0, PAIRS // 2) as j:
                for m in range(8):
                    k = 8 * j + (4 + m)
                    step(k, (4 + m) % 8)
                    high(k - 1, (3 + m) % 8)
            high(4 * PAIRS + 3, 3)
            for c in range(NC):
                act_e.wait_ge(down_done, 4 * PAIRS + c + 1)
                act_e.activation(yT[:, c * CHUNK:(c + 1) * CHUNK], acc[c][:, :], ACT.Copy, scale=0.5).then_inc(yT_done, 1)

        @blk.vector
        def _(dve):
            links = [0]

            def link(ins):
                links[0] += 1
                ins.then_inc(dve_link, 1)
                dve.wait_ge(dve_link, links[0])

            for g in range(NT // 4):
                ln_statistics(dve, link, x, stats, moments, g, varied)
                if g >= 1:
                    ln_apply(dve, link, x, xn, moments, g - 1, rooted, normed)
            ln_apply(dve, link, x, xn, moments, NT // 4 - 1, rooted, normed)
            for h in range(2):
                half = slice(8 * h, 8 * h + 8)
                dve.wait_ge(logits_out, h + 1)
                for t in range(8 * h, 8 * h + 8):
                    last = dve.max(top[:, t, :], lg[:, t, :])
                link(last)
                for t in range(8 * h, 8 * h + 8):
                    last = dve.match_replace(rep[:, t, :], top[:, t, :], lg[:, t, :], LOWEST)
                link(last)
                dve.wait_ge(affinity_ready, h + 1)
                link(dve.scalar_tensor_tensor(aff[:, half, :], rep[:, half, :], LOWEST, aff[:, half, :],
                                              ALU.is_equal, ALU.mult))
                link(dve.tensor_reduce(wsum[:, 0, half], aff[:, half, :], AX.X, ALU.add))
                link(dve.tensor_scalar(wsum[:, 0, half], wsum[:, 0, half], 1e-9, None, ALU.add))
                dve.reciprocal(wsum[:, 1, half], wsum[:, 0, half]).then_inc(sums_ready, 1)

            def gate_up(k, m):
                dve.wait_ge(silu_done, k + 1)
                dve.wait_ge(up_done, k + 1)
                if not (isinstance(k, int) and k < 2):
                    dve.wait_ge(act_done, k - 1)
                dve.tensor_tensor(gated[m % 2][:, :], silu[m % 2][:, :], up_ps[:, :], ALU.mult).then_inc(gated_done, 1)

            def weigh(k, m):
                dve.wait_ge(gated_done, k + 1)
                dve.wait_ge(mask_done, k + 1)
                if not (isinstance(k, int) and k < 2):
                    dve.wait_ge(alo_done, k - 1)
                dve.tensor_tensor(act[m % 2][:, :], gated[m % 2][:, :], mask_ps[:, :], ALU.mult).then_inc(act_done, 1)

            def low(k, m):
                dve.wait_ge(ahi_done, k + 1)
                dve.tensor_tensor(alo[m % 4][:, :], act[m % 2][:, :], ahi[m % 4][:, :].bitcast(F32),
                                  ALU.subtract).then_inc(alo_done, 1)

            gate_up(0, 0)
            weigh(0, 0)
            for k in range(1, 4):
                gate_up(k, k)
                weigh(k, k)
                low(k - 1, k - 1)
            with dve.Fori(0, PAIRS // 2) as j:
                for m in range(8):
                    k = 8 * j + (4 + m)
                    gate_up(k, (4 + m) % 8)
                    weigh(k, (4 + m) % 8)
                    low(k - 1, (3 + m) % 8)
            low(4 * PAIRS + 3, 3)
            for c in range(NC):
                dve.wait_ge(y_done, c + 1)
                dve.tensor_tensor(x_out[:, 4 * c:4 * c + 4, :], x[:, 4 * c:4 * c + 4, :],
                                  gate_ps[c % 2][:, :].rearrange("p (t d) -> p t d", t=4), ALU.add).then_inc(x_done, 1)

        @blk.tensor
        def _(pe):
            for h in range(2):
                for c in (2 * h, 2 * h + 1):
                    pe.wait_ge(normed, c + 1)
                    for t in range(4):
                        last = pe.transpose(acc[c][:, t * 128:(t + 1) * 128], xn[:, 4 * c + t, :], ident)
                    last.then_inc(xT_ready, 1)
            for h in range(2):
                pe.wait_ge(xT_raw, 2 * h + 2)
                if h == 0:
                    pe.wait_ge(router_loaded, 16)
                for t in range(8 * h, 8 * h + 8):
                    last = pe.matmul(LG[h][:, (t % 8) * EXPERTS:(t % 8 + 1) * EXPERTS],
                                     xnT[:, t * 128:(t + 1) * 128], rw[:, :], start=True, stop=True)
                last.then_inc(logits_ready, 1)

            def masks(c):
                pe.wait_ge(parts_ready, c // 2 + 1)
                if c >= 2:
                    pe.wait_ge(maskT_done, c - 1)
                for k in range(2):
                    for t in range(4):
                        out = acc[2 + c % 2][0:96, :].bitcast(BF16)[:, (4 * k + t) * 128:(4 * k + t + 1) * 128]
                        last = pe.transpose(out, wpart[:, 4 * c + t, k, :, :].rearrange("p a e -> p (a e)"), identb)
                last.then_inc(maskT_ps, 1)

            def triple(out, i, slot, hi, lo, first, last):
                pe.matmul(out, whi[slot][:, i, :], hi, start=first, stop=False)
                pe.matmul(out, whi[slot][:, i, :], lo, start=False, stop=False)
                return pe.matmul(out, wlo[slot][:, i, :], hi, start=False, stop=last)

            def up_step(slot, c, k, m):
                cs = slice(c * CHUNK, (c + 1) * CHUNK)
                static = isinstance(k, int)
                if not (static and k < 2):
                    pe.wait_ge(silu_done, k - 1)
                triple(gate_ps[m % 2][:, :], 0, slot, xhi[:, cs], xlo[:, cs], True, True).then_inc(gate_done, 1)
                if not (static and k < 1):
                    pe.wait_ge(gated_done, k)
                triple(up_ps[:, :], 1, slot, xhi[:, cs], xlo[:, cs], True, True).then_inc(up_done, 1)

            def mask_step(q, half, c, k):
                pe.wait_ge(act_done, k)
                cs = slice(c * CHUNK, (c + 1) * CHUNK)
                pe.matmul(mask_ps[:, :], sel[:, bass.ds(q, 1), :].rearrange("p a m -> p (a m)"),
                          maskT[:, half, cs], start=True, stop=True).then_inc(mask_done, 1)

            def down_step(slot, c, k, m, first=False, last=False, split=None):
                if split is not None:
                    pe.wait_ge(split_done, split)
                pe.wait_ge(alo_done, k + 1)
                done = triple(acc[c][:, :], 2, slot, ahi[m % 4][:, :], alo[m % 4][:, :], first, last)
                done.then_inc(down_done, 1)
                return done

            pe.wait_ge(split_done, 2)
            pe.wait_ge(zeroed, 2)
            pe.wait_ge(logits_out, 2)
            for c in range(4):
                pe.wait_ge(xT_split, c + 1)
                up_step(0, c, c, c)
                if c >= 1:
                    pe.wait_ge(act_done, c)
                pe.matmul(mask_ps[:, :], ones[:, 0:128], ones[:, :], start=True, stop=True).then_inc(mask_done, 1)
                if c >= LAG:
                    down_step(0, c - LAG, c - LAG, c - LAG, first=True, split=4 if c == LAG else None)
                if c in (1, 2):
                    masks(2 * c - 2)
                    masks(2 * c - 1)

            def body(j, first=False, last=False):
                for m in range(8):
                    du, c = divmod(m, 4)
                    k = 8 * j + (4 + m)
                    if c == 0:
                        pe.wait_ge(split_done, 8 * j + (6 + 4 * du))
                    up_step(1 - du, c, k, m + 4)
                    if first and m == 0:
                        pe.wait_ge(maskT_done, NC)
                    mask_step(j, du, c, k)
                    slot = (1 - du) if c >= LAG else du
                    down_step(slot, (c - LAG) % 4, k - LAG, (m + 4 - LAG) % 8,
                              first=first and m < LAG, last=last and m >= 4 + LAG,
                              split=8 * j + (8 + 4 * du) if c == LAG else None)

            body(0, first=True)
            with pe.Fori(1, PAIRS // 2 - 1) as j:
                body(j)
            body(PAIRS // 2 - 1, last=True)
            for c in range(4 - LAG, 4):
                down_step(0, c, 4 * PAIRS + c, c, last=True)
            for c in range(NC):
                pe.wait_ge(yT_done, c + 1)
                if c >= 2:
                    pe.wait_ge(x_done, c - 1)
                for t in range(4):
                    s = (4 * c + t) * 128
                    last = pe.transpose(gate_ps[c % 2][:, t * 128:(t + 1) * 128], yT[:, s:s + 128], ident)
                last.then_inc(y_done, 1)


HEADS, WIDTH = 8, 64
C, R = 32, 32
CQ = 64
IDX_HEADS = 4
FAR, LOCAL = 32, 64
TILES = L // 128
BLK = 16
PAIRS_B = 4
WIN = BLK + LOCAL
HEAD_KEYS = 96
SPAN = WIN + 128
GROUPS = 32
SCALE = (WIDTH + R) ** -0.5
PI = 3.14159265358979
OUT = -1.0e30
Q4 = R // 2
PICKS = (2, 1, 1, 2, 1, 1, 0, 0, 1, 1, 0, 0, 1, 1, 0, 0)


def place(i):
    return i // TILES, i % TILES


def width(i):
    k = i % TILES
    return 128 if k == 0 else 128 * k + 64


def halves(i):
    return [(s, min(s + 512, width(i))) for s in range(0, width(i), 512)]


def chunks(n):
    return range(4) if n % TILES else range(LOCAL // 32, 4)


def key_tiles(n, p):
    return range(n % TILES + (p >= 2))


def turned(i, p):
    tile, chunk = (i, 3) if p == 0 else (i + 1, p - 2)
    return [(tile, chunk)] if 0 <= tile < NT and chunk in chunks(tile) else []


def attended(i, p):
    tile, pair = (i - 1, 3) if p == 0 else (i, p - 2)
    return [(tile, pair)] if tile >= 0 and pair >= 0 else []


def plan():
    a_tasks, v_tasks, c_tasks = [], [], []
    for i in range(-4, NT):
        n, m = i + 1, i + 4
        for p in range(5):
            if i >= 0 and p < 4:
                a_tasks.append(("S", i, p))
            for tile, pair in attended(i, p):
                a_tasks.append(("ctx", tile, pair))
            if 0 <= n < NT and p in chunks(n):
                v_tasks += [("gather", n, 2 * p + g) for g in range(2)]
                c_tasks.append((n, p))
            if i >= 1 and p == 0:
                v_tasks.append(("out", i - 1))
            if p == 4 and 0 <= n < NT:
                a_tasks.append(("cq", n))
            if p == 4 and m < NT:
                a_tasks.append(("qi", m))
            if p == 4 and 0 <= n < NT:
                a_tasks.append(("qabs", n))
            if p == 4 and m < NT:
                a_tasks += [("score", m, s, h) for s in range(len(halves(m))) for h in range(IDX_HEADS)]
            if p == 4 and 0 <= n < NT:
                a_tasks += [("QT", n, h) for h in range(2)]
            if i >= 0 and p >= 1:
                a_tasks.append(("PT", i, p - 1))
            for tile, chunk in turned(i, p):
                a_tasks += [("GT", tile, 2 * chunk + g) for g in range(2)]
    a_tasks.append(("ctx", NT - 1, PAIRS_B - 1))
    v_tasks.append(("out", NT - 1))
    return tuple({k: u for u, k in enumerate(tasks)} for tasks in (a_tasks, v_tasks, c_tasks))


def _attn_constants():
    import numpy as np
    theta = (1.0 / np.float32(10000.0) ** (2.0 * np.arange(Q4, dtype=np.float32) / R)).astype(np.float32)
    t = np.arange(L).reshape(TILES, 128).T
    angle = np.zeros((128, 2 * TILES + 1, Q4))
    angle[:, :TILES] = (t[:, :, None].astype(np.float32) * theta).astype(np.float32)
    angle[:, TILES:2 * TILES] = (t + np.maximum(t - (LOCAL - 1), 0))[:, :, None] * theta.astype(np.float64)
    rank = LOCAL + np.arange(128) % FAR
    angle[:, 2 * TILES] = (rank[:, None].astype(np.float32) * theta).astype(np.float32)
    trig = np.stack([np.cos(angle), np.sin(angle)], 2).astype(np.float32)
    p, c = np.arange(128)[:, None], np.arange(128)[None, :]
    late = np.where(c <= p, 0.0, LOWEST).astype(np.float32)
    early = np.where(c > p, OUT * (1 + c / 1024.0), LOWEST)
    early = np.where(c <= p - LOCAL, 0.0, early).astype(np.float32)
    q = p // HEADS
    w = np.arange(WIN)[None, :]
    near = np.where((w >= q + 1) & (w <= q + LOCAL), 0.0, OUT)
    far = np.where(c // FAR == q % 4, 0.0, OUT)
    s = 128 * np.arange(TILES)[None, :] + p
    smask = np.concatenate([near, far], 1).astype(np.float32)
    smask = (smask.view(np.uint32) >> 16).astype(np.uint16)
    return {"trig": trig, "late": late, "early": early, "smask": smask,
            "keyno": s.astype(np.float32)}



def attn_loop(nc, x, x_out, ident, identb, xnT, kiT, wiq, wdq, keyT, ctab, muq_dram, trig, absorb, wvo, expo,
              idxw, late, early, smask, keyno, cpad, idx_dram, RA, RV, A_AT, V_AT, C_AT):
    ctx = ExitStack()

    def sb(name, shape, dt):
        return ctx.enter_context(nc.sbuf_tensor(name, shape, dt))

    def sem(name):
        return ctx.enter_context(nc.semaphore(name))

    with ctx:
        hot = sb("hot", [128, TILES, GROUPS, 128], FP16)
        idxb = sb("idxb", [128, 128 * FAR], FP16)
        relu = [sb(f"relu{i}", [128, 512], F32) for i in range(2)]
        score = [sb(f"score{i}", [128, L], F32) for i in range(2)]
        best = sb("best", [128, 4, 8], F32)
        which = sb("which", [128, 4, 8], mybir.dt.uint16)
        idx16 = [sb(f"idx16_{i}", [128, FAR], FP16) for i in range(2)]
        G = [sb(f"G{i}", [128, GROUPS, 64], F32) for i in range(2)]
        tmp = [sb(f"tmp{i}", [128, 8, Q4], F32) for i in range(4)]
        muq = [sb(f"muq{i}", [128, HEADS, R], F32) for i in range(2)]
        QI = sb("QI", [128, IDX_HEADS // 2, 128], F32)
        CQT = sb("CQT", [CQ, 128], F32)
        GT = sb("GT", [64, GROUPS * 128], F32)
        QN = sb("QN", [128, HEADS, 96], F32)
        QT = sb("QT", [96, 128, HEADS], F32)
        diag = [sb(f"diag{i}", [128, 2, 128], F32) for i in range(2)]
        P = [sb(f"P{i}", [128, 2, SPAN], F32) for i in range(2)]
        small = [sb(f"small{i}", [128, 4, 2], F32) for i in range(2)]
        PT = [sb(f"PT{i}", [128, 4, 128], F32) for i in range(2)]
        CT = sb("CT", [C, 128, HEADS], F32)
        cwin = [sb(f"cwin{i}", [WIN, 8, C], F32) for i in range(2)]
        chead = sb("chead", [HEAD_KEYS, C], F32)

        a_filled, a_emptied = sem("a_filled"), sem("a_emptied")
        v_filled, v_emptied = sem("v_filled"), sem("v_emptied")
        added = sem("added")
        picked = sem("picked")
        idx_stored = sem("idx_stored")
        idx_loaded = [sem(f"idx_loaded{p}") for p in range(4)]
        hot_ready = sem("hot_ready")
        muq_loaded = [sem(f"muq_loaded{i}") for i in range(2)]
        win_loaded = [sem(f"win_loaded{i}") for i in range(2)]
        head_loaded = sem("head_loaded")
        g_rotated = sem("g_rotated")
        q_rotated = sem("q_rotated")
        biased = sem("biased")
        inverted = sem("inverted")
        diag_ready = sem("diag_ready")
        vlink = sem("vlink")
        glink = sem("glink")

        blk = ctx.enter_context(nc.Block())

        def far_pairs(i):
            return range(PAIRS_B) if i % TILES else range(LOCAL // (2 * BLK), PAIRS_B)

        def step_place(u):
            return u // PAIRS_B, u % PAIRS_B

        def last_score(i):
            return A_AT[("score", i, len(halves(i)) - 1, IDX_HEADS - 1)]

        @blk.sync
        def _(sp):
            for i in range(-4, NT):
                n = i + 1
                if 0 <= n < NT:
                    if n >= 2:
                        sp.wait_ge(a_emptied, A_AT[("ctx", n - 2, PAIRS_B - 1)] + 1)
                    b, k = place(n)
                    if k == 0:
                        if b:
                            sp.wait_ge(a_emptied, A_AT[("ctx", n - TILES, PAIRS_B - 1)] + 1)
                        sp.dma_start(chead[:, :], cpad[b, 64:64 + HEAD_KEYS, :]).then_inc(head_loaded, 16)
                    for m in range(WIN // BLK):
                        lo = 128 * k + BLK * m
                        sp.dma_start(cwin[n % 2][BLK * m:BLK * (m + 1), :, :],
                                     cpad[b, lo:lo + 128, :].rearrange("(q p) c -> p q c", p=BLK)
                                     ).then_inc(win_loaded[n % 2], 16)
                    if n >= 2:
                        sp.wait_ge(q_rotated, 2 * (n - 1))
                    sp.dma_start(muq[n % 2][:, :, :].rearrange("p h r -> p (h r)"),
                                 muq_dram[n, :, :]
                                 ).then_inc(muq_loaded[n % 2], 16)
                if 0 <= i + 3 < NT:
                    m = i + 3
                    sp.wait_ge(picked, m + 1)
                    sp.dma_start(idx_dram[m % 2, :].rearrange("(p r) -> p r", r=FAR),
                                 idx16[m % 2][:, :]).then_inc(idx_stored, 16)
                    sp.wait_ge(idx_stored, 16 * (m + 1))
                    for p in chunks(m):
                        if m >= 1:
                            last = m - 1 if p in chunks(m - 1) else m - 2
                            if last >= 0:
                                sp.wait_ge(hot_ready, C_AT[(last, p)] + 1)
                        part = slice(1024 * p, 1024 * (p + 1))
                        sp.dma_start(idxb[:, part], idx_dram[m % 2, part].partition_broadcast(128)).then_inc(
                            idx_loaded[p], 16)

        @blk.gpsimd
        def _(pool):
            links = [0]

            def link(ins):
                links[0] += 1
                ins.then_inc(glink, 1)
                pool.wait_ge(glink, links[0])

            def rotate(dst, src, k, n):
                co, si = (trig[:, k, j, :].unsqueeze(1).broadcast_to([128, n, Q4]) for j in range(2))
                m1, m2 = src[:, :, 0:Q4], src[:, :, Q4:R]
                for out, m, a in ((0, m1, co), (1, m2, si), (2, m1, si), (3, m2, co)):
                    last = pool.tensor_tensor(tmp[out][:, 0:n, :], m, a, ALU.mult)
                link(last)
                pool.tensor_tensor(dst[:, :, 0:Q4], tmp[0][:, 0:n, :], tmp[1][:, 0:n, :], ALU.subtract)
                return pool.tensor_tensor(dst[:, :, Q4:R], tmp[2][:, 0:n, :], tmp[3][:, 0:n, :], ALU.add)

            def queries(n, k):
                if k == 0:
                    pool.wait_ge(muq_loaded[n % 2], 16 * (n // 2 + 1))
                    if n >= 1:
                        pool.wait_ge(a_emptied, A_AT[("QT", n - 1, 1)] + 1)
                dst = QN[:, :, 32 + 32 * k:64 + 32 * k]
                rotate(dst, muq[n % 2], TILES * k + n % TILES, HEADS).then_inc(q_rotated, 1)
                pool.wait_ge(q_rotated, 2 * n + k + 1)

            def far_keys(n, p):
                pool.wait_ge(v_emptied, V_AT[("gather", n, 2 * p + 1)] + 1)
                g = G[n % 2][:, 8 * p:8 * p + 8, C:]
                rotate(g, g, 2 * TILES, 8).then_inc(g_rotated, 1)
                pool.wait_ge(g_rotated, C_AT[(n, p)] + 1)

            def divisors(i, p):
                u = PAIRS_B * i + p
                pool.wait_ge(inverted, u + 1)
                if u >= 2:
                    pool.wait_ge(a_filled, A_AT[("PT", *step_place(u - 2))] + 1)
                pool.tensor_tensor(diag[u % 2][:, :, :], ident.unsqueeze(1).broadcast_to([128, 2, 128]),
                                   small[u % 2][:, 3, :].unsqueeze(2).broadcast_to([128, 2, 128]),
                                   ALU.mult).then_inc(diag_ready, 1)

            for i in range(-1, NT):
                n = i + 1
                for p in range(5):
                    if i >= 0 and p < 4:
                        divisors(i, p)
                    if n < NT and p in chunks(n):
                        far_keys(n, p)
                    if n < NT and p in (1, 2):
                        queries(n, p - 1)

        @blk.scalar
        def _(act):
            step = [0]

            def empty(key, dst, src, func=ACT.Copy):
                act.wait_ge(a_filled, A_AT[key] + 1)
                act.activation(dst, src, func).then_inc(a_emptied, 1)

            def ring(key):
                return RA[A_AT[key] % len(RA)]

            def scores(i):
                for s, (lo, hi) in enumerate(halves(i)):
                    for h in range(IDX_HEADS):
                        k = step[0]
                        if k >= 2:
                            act.wait_ge(added, k - 1)
                        empty(("score", i, s, h), relu[k % 2][:, 0:hi - lo], ring(("score", i, s, h))[:, 0:hi - lo],
                              ACT.Relu)
                        step[0] += 1

            def exps(i, p):
                u = PAIRS_B * i + p
                act.wait_ge(biased, u + 1)
                w = SPAN if p in far_pairs(i) else HEAD_KEYS
                for k in range(2):
                    last = act.activation(P[u % 2][:, k, 0:w], ring(("S", i, p))[:, k * w:(k + 1) * w], ACT.Exp,
                                          scale=expo[:, 0:1], bias=small[u % 2][:, 1, k:k + 1],
                                          accum_out=small[u % 2][:, 2, k:k + 1])
                last.then_inc(a_emptied, 1)

            def weights_out(i, p):
                u = PAIRS_B * i + p
                key = ("PT", i, p)
                act.wait_ge(a_filled, A_AT[key] + 1)
                if u >= 2:
                    prior = (u - 2) // PAIRS_B, (u - 2) % PAIRS_B
                    act.wait_ge(a_emptied, A_AT[("ctx", *prior)] + 1)
                rows = WIN if p in far_pairs(i) else HEAD_KEYS
                last = act.activation(PT[u % 2][0:rows, 0:2, :],
                                      ring(key)[0:rows, 0:256].rearrange("p (k t) -> p k t", k=2), ACT.Copy)
                if p in far_pairs(i):
                    last = act.activation(PT[u % 2][:, 2:4, :],
                                          ring(key)[:, 256:512].rearrange("p (k t) -> p k t", k=2), ACT.Copy)
                last.then_inc(a_emptied, 1)

            def context_out(i, p):
                if i >= 1 and p == 0:
                    act.wait_ge(v_emptied, V_AT[("out", i - 1)] + 1)
                key = ("ctx", i, p)
                empty(key, CT[:, 32 * p:32 * p + 32, :], ring(key)[0:C, 0:256].rearrange("c (t h) -> c t h", h=HEADS))

            for i in range(-4, NT):
                n, m = i + 1, i + 4
                for p in range(5):
                    if i >= 0 and p < 4:
                        exps(i, p)
                    for tile, pair in attended(i, p):
                        context_out(tile, pair)
                    if p == 4 and 0 <= n < NT:
                        if n >= 1:
                            act.wait_ge(a_emptied, A_AT[("QT", n - 1, 1)] + 1)
                        empty(("cq", n), CQT[:, :], ring(("cq", n))[0:CQ, 0:128])
                    if p == 4 and m < NT:
                        key = ("qi", m)
                        if m >= 1:
                            act.wait_ge(a_emptied, last_score(m - 1) + 1)
                        empty(key, QI[:, :, :], ring(key)[:, 0:256].rearrange("p (h t) -> p h t", h=IDX_HEADS // 2))
                    if p == 4 and 0 <= n < NT:
                        key = ("qabs", n)
                        empty(key, QN[:, :, 0:C], ring(key)[:, 0:256].rearrange("p (h c) -> p h c", c=C))
                    if p == 4 and m < NT:
                        scores(m)
                    if p == 4 and 0 <= n < NT:
                        for h in range(2):
                            key = ("QT", n, h)
                            empty(key, QT[:, :, 4 * h:4 * h + 4],
                                  ring(key)[0:96, :].rearrange("c (h t) -> c t h", h=4))
                    if i >= 0 and p >= 1:
                        weights_out(i, p - 1)
                    for tile, chunk in turned(i, p):
                        for q in (2 * chunk, 2 * chunk + 1):
                            empty(("GT", tile, q), GT[:, q * 512:(q + 1) * 512], ring(("GT", tile, q))[0:64, :])
            context_out(NT - 1, PAIRS_B - 1)

        @blk.vector
        def _(dve):
            links, step = [0], [0]

            def link(ins):
                links[0] += 1
                ins.then_inc(vlink, 1)
                dve.wait_ge(vlink, links[0])

            def ring(key):
                dve.wait_ge(v_filled, V_AT[key] + 1)
                return RV[V_AT[key] % len(RV)]

            def add_scores(i):
                I = score[i % 2]
                for s, (lo, hi) in enumerate(halves(i)):
                    for h in range(IDX_HEADS):
                        k = step[0]
                        dve.wait_ge(a_emptied, A_AT[("score", i, s, h)] + 1)
                        r = relu[k % 2][:, 0:hi - lo]
                        if h == 0:
                            ins = dve.tensor_scalar(I[:, lo:hi], r, idxw[:, 0:1], None, ALU.mult)
                        else:
                            ins = dve.scalar_tensor_tensor(I[:, lo:hi], r, idxw[:, h:h + 1], I[:, lo:hi],
                                                           ALU.mult, ALU.add)
                        ins.then_inc(added, 1)
                        dve.wait_ge(added, k + 1)
                        step[0] += 1
                w = width(i)
                link(dve.tensor_tensor(I[:, w - 128:w], I[:, w - 128:w], (late if i % TILES else early)[:, :], ALU.add))

            def pick(i, r, part):
                I = score[i % 2][:, 0:width(i)]
                if part == 0:
                    link(dve.max(best[:, r, :], I))
                elif part == 1:
                    link(dve.max_index(which[:, r, :], best[:, r, :], I))
                elif part == 2 and r < 3:
                    link(dve.match_replace(I, best[:, r, :], I, LOWEST * 1.1))
                elif part == 2:
                    if i >= 2:
                        dve.wait_ge(idx_stored, 16 * (i - 1))
                    dve.tensor_copy(idx16[i % 2][:, :], which[:, :, :].rearrange("p a k -> p (a k)")).then_inc(
                        picked, 1)

            def one_hot(i, p, part):
                tiles = [j for j in key_tiles(i, p) if j // 2 == part]
                if part == 0:
                    dve.wait_ge(idx_loaded[p], 16 * sum(p in chunks(j) for j in range(i + 1)))
                for j in tiles:
                    ins = dve.tensor_scalar(hot[:, j, 8 * p:8 * p + 8, :].rearrange("p g q -> p (g q)"),
                                            idxb[:, 1024 * p:1024 * (p + 1)], keyno[:, j:j + 1], None,
                                            ALU.is_equal)
                    if j == key_tiles(i, p)[-1]:
                        ins.then_inc(hot_ready, 1)

            def biases(i, p):
                u = PAIRS_B * i + p
                f = small[u % 2]
                w = SPAN if p in far_pairs(i) else HEAD_KEYS
                key = ("S", i, p)
                dve.wait_ge(a_filled, A_AT[key] + 1)
                if u >= 2:
                    dve.wait_ge(a_emptied, A_AT[("S", *step_place(u - 2))] + 1)
                link(dve.tensor_reduce(f[:, 0, :], RA[A_AT[key] % len(RA)][:, 0:2 * w].rearrange("p (k c) -> p k c", k=2),
                                       AX.X, ALU.max))
                dve.tensor_scalar(f[:, 1, :], f[:, 0, :], expo[:, 1:2], None, ALU.mult).then_inc(biased, 1)

            def invert(i, p):
                u = PAIRS_B * i + p
                dve.wait_ge(a_emptied, A_AT[("S", i, p)] + 1)
                if u >= 2:
                    dve.wait_ge(diag_ready, u - 1)
                dve.reciprocal(small[u % 2][:, 3, :], small[u % 2][:, 2, :]).then_inc(inverted, 1)

            def out(i):
                o = ring(("out", i))
                dve.tensor_tensor(x_out[:, i, :], x[:, i, :], o[:, 0:D], ALU.add).then_inc(v_emptied, 1)

            for i in range(-4, NT):
                n, nn, nnn, m = i + 1, i + 2, i + 3, i + 4
                for p in range(5):
                    if i >= 0 and p < 4:
                        biases(i, p)
                    for g in range(4):
                        if 0 <= n < NT and p in chunks(n) and g % 2:
                            key = ("gather", n, 2 * p + g // 2)
                            ps = ring(key)[:, :].rearrange("p (g a d) -> p g d a", g=4, a=2)
                            if n >= 2 and g == 1:
                                dve.wait_ge(a_emptied, A_AT[("ctx", n - 2, PAIRS_B - 1)] + 1)
                            four = slice(8 * p + 2 * g - 2, 8 * p + 2 * g + 2)
                            dve.tensor_reduce(G[n % 2][:, four, :], ps, AX.X, ALU.add).then_inc(v_emptied, 1)
                        if 0 <= nn < NT and p - 1 in chunks(nn):
                            one_hot(nn, p - 1, g)
                        if 0 <= nnn < NT and p < 4:
                            first = sum(PICKS[:4 * p + g])
                            for q in range(first, first + PICKS[4 * p + g]):
                                pick(nnn, q // 3, q % 3)
                        if i >= 0 and p < 4 and g == 1:
                            invert(i, p)
                    if i >= 1 and p == 0:
                        out(i - 1)
                    if p == 4 and m < NT:
                        add_scores(m)
            out(NT - 1)

        @blk.tensor
        def _(pe):
            def ra(key, after=None):
                u = A_AT[key]
                need = max(u - len(RA) + 1, A_AT[after] + 1 if after else 0)
                if need > 0:
                    pe.wait_ge(a_emptied, need)
                return RA[u % len(RA)]

            def rv(key):
                u = V_AT[key]
                if u >= len(RV):
                    pe.wait_ge(v_emptied, u - len(RV) + 1)
                return RV[u % len(RV)]

            def index_queries(i):
                o = ra(("qi", i))
                tokens = xnT[:, 128 * i:128 * i + 128]
                for h in range(IDX_HEADS // 2):
                    last = pe.matmul(o[:, h * 128:(h + 1) * 128], wiq[:, 128 * h:128 * h + 128], tokens,
                                     start=True, stop=True)
                last.then_inc(a_filled, 1)

            def index_scores(i):
                at = L * place(i)[0]
                for s, (lo, hi) in enumerate(halves(i)):
                    for h in range(IDX_HEADS):
                        o = ra(("score", i, s, h), ("qi", i))
                        rows = slice(64 * (h % 2), 64 * (h % 2) + 64)
                        pe.matmul(o[:, 0:hi - lo], QI[rows, h // 2, :], kiT[rows, at + lo:at + hi],
                                  start=True, stop=True).then_inc(a_filled, 1)

            def queries(n):
                o = ra(("cq", n))
                pe.matmul(o[0:CQ, 0:128], wdq[:, :], xnT[:, 128 * n:128 * n + 128],
                          start=True, stop=True).then_inc(a_filled, 1)

            def absorbed(n):
                o = ra(("qabs", n), ("cq", n))
                pe.matmul(o[:, 0:256], CQT[:, :], absorb[:, :, :].rearrange("k h c -> k (h c)"),
                          start=True, stop=True).then_inc(a_filled, 1)

            def scores(i, p):
                far = p in far_pairs(i)
                w = SPAN if far else HEAD_KEYS
                b, tile = place(i)
                o = ra(("S", i, p), ("GT", i, 2 * p + 1) if p >= 2 else ("QT", i, 1))
                for k in range(2):
                    blk_no = 2 * p + k
                    q = QT[:, blk_no * BLK:(blk_no + 1) * BLK, :].rearrange("c t h -> c (t h)")
                    if far:
                        lo = 128 * tile + BLK * blk_no
                        pe.matmul(o[:, k * w:(k + 1) * w], identb, smask[:, :], start=True, stop=False)
                        pe.matmul(o[:, k * w:k * w + WIN], q, keyT[:, b, lo:lo + WIN], start=False, stop=False)
                        for g in range(4):
                            at = (4 * blk_no + g) * 128
                            last = pe.matmul(o[32 * g:32 * g + 32, k * w + WIN:(k + 1) * w],
                                             q[0:64, 32 * g:32 * g + 32], GT[:, at:at + 128],
                                             start=False, stop=True)
                    else:
                        last = pe.matmul(o[:, k * w:(k + 1) * w], q, keyT[:, b, 64:64 + w], start=True, stop=True)
                last.then_inc(a_filled, 1)

            def gather(n, p):
                pe.wait_ge(hot_ready, C_AT[(n, p)] + 1)
                tiles = key_tiles(n, p)
                first = TILES * place(n)[0]
                for g in range(2 * p, 2 * p + 2):
                    o = rv(("gather", n, g))
                    for k in range(4):
                        for j in tiles:
                            last = pe.matmul(o[:, 128 * k:128 * k + 128], hot[:, j, 4 * g + k, :],
                                             ctab[:, first + j, :, :].rearrange("s k d -> s (k d)"),
                                             start=(j == 0), stop=(j == tiles[-1]))
                    last.then_inc(v_filled, 1)

            def weights_turned(i, p):
                u = PAIRS_B * i + p
                pe.wait_ge(diag_ready, u + 1)
                o = ra(("PT", i, p))
                far = p in far_pairs(i)
                w = WIN if far else HEAD_KEYS
                for k in range(2):
                    last = pe.matmul(o[0:w, 128 * k:128 * k + 128], P[u % 2][:, k, 0:w], diag[u % 2][:, k, :],
                                     start=True, stop=True)
                if far:
                    for k in range(2):
                        last = pe.matmul(o[:, 256 + 128 * k:384 + 128 * k], P[u % 2][:, k, WIN:SPAN],
                                         diag[u % 2][:, k, :], start=True, stop=True)
                last.then_inc(a_filled, 1)

            def gathered_turned(n, p):
                pe.wait_ge(g_rotated, C_AT[(n, p)] + 1)
                for g in range(2):
                    o = ra(("GT", n, 2 * p + g))
                    for k in range(4):
                        last = pe.transpose(o[0:64, 128 * k:128 * k + 128], G[n % 2][:, 8 * p + 4 * g + k, :], ident)
                    last.then_inc(a_filled, 1)

            def attend(i, p):
                u = PAIRS_B * i + p
                o = ra(("ctx", i, p), ("PT", i, p))
                if p == 0:
                    pe.wait_ge(win_loaded[i % 2], 80 * (i // 2 + 1))
                    if i % TILES == 0:
                        pe.wait_ge(head_loaded, 16 * (i // TILES + 1))
                for k in range(2):
                    blk_no = 2 * p + k
                    part = slice(128 * k, 128 * k + 128)
                    if p not in far_pairs(i):
                        last = pe.matmul(o[0:C, part], chead[:, :], PT[u % 2][0:HEAD_KEYS, k, :],
                                         start=True, stop=True)
                        continue
                    pe.matmul(o[0:C, part], cwin[i % 2][:, blk_no, :], PT[u % 2][0:WIN, k, :],
                              start=True, stop=False)
                    for g in range(4):
                        last = pe.matmul(o[0:C, 128 * k + 32 * g:128 * k + 32 * g + 32],
                                         G[i % 2][:, 4 * blk_no + g, 0:C], PT[u % 2][:, 2 + k, 32 * g:32 * g + 32],
                                         start=False, stop=(g == 3))
                last.then_inc(a_filled, 1)

            def queries_turned(n):
                pe.wait_ge(q_rotated, 2 * n + 2)
                for h in range(2):
                    o = ra(("QT", n, h), ("qabs", n))
                    for k in range(4):
                        last = pe.transpose(o[0:96, 128 * k:128 * k + 128], QN[:, 4 * h + k, :], ident)
                    last.then_inc(a_filled, 1)

            def out(i):
                o = rv(("out", i))
                pe.wait_ge(a_emptied, A_AT[("ctx", i, PAIRS_B - 1)] + 1)
                for h in range(HEADS):
                    last = pe.matmul(o[:, 0:D], CT[:, :, h], wvo[:, h, :], start=(h == 0), stop=(h == HEADS - 1))
                last.then_inc(v_filled, 1)

            for i in range(-4, NT):
                n, m = i + 1, i + 4
                for p in range(5):
                    if i >= 0 and p < 4:
                        scores(i, p)
                    for tile, pair in attended(i, p):
                        attend(tile, pair)
                    if 0 <= n < NT and p in chunks(n):
                        gather(n, p)
                    if i >= 1 and p == 0:
                        out(i - 1)
                    if p == 4 and 0 <= n < NT:
                        queries(n)
                    if p == 4 and m < NT:
                        index_queries(m)
                    if p == 4 and 0 <= n < NT:
                        absorbed(n)
                    if p == 4 and m < NT:
                        index_scores(m)
                    if p == 4 and 0 <= n < NT:
                        queries_turned(n)
                    if i >= 0 and p >= 1:
                        weights_turned(i, p - 1)
                    for tile, chunk in turned(i, p):
                        gathered_turned(tile, chunk)
            attend(NT - 1, PAIRS_B - 1)
            out(NT - 1)


def attn_phase(nc, t, x, x_out, const, banks):
    ctx = ExitStack()

    def sb(name, shape, dt):
        return ctx.enter_context(nc.sbuf_tensor(name, shape, dt))

    def sem(name):
        return ctx.enter_context(nc.semaphore(name))

    A_AT, V_AT, C_AT = plan()
    with ctx:
        ident, identb = const["ident"], const["identb"]
        kiT = sb("kiT", [128, NT * 128], F32)
        xnT = sb("a_xnT", [128, NT * 128], F32)
        wiq = sb("wiq", [128, 256], F32)
        wdq = sb("wdq", [128, CQ], F32)
        keyT = sb("keyT", [96, B, 64 + L], F32)
        ctab = sb("ctab", [128, NT, 2, 64], FP16)
        expo = sb("expo", [128, 2], F32)
        trig = sb("trig", [128, 2 * TILES + 1, 2, Q4], F32)
        absorb = sb("absorb", [CQ, HEADS, C], F32)
        wvo = sb("wvo", [C, HEADS, D], F32)
        idxw = sb("idxw", [128, IDX_HEADS], F32)
        late = sb("late", [128, 128], F32)
        early = sb("early", [128, 128], F32)
        smask = sb("smask", [128, SPAN], BF16)
        keyno = sb("keyno", [128, TILES], F32)
        muq_dram = nc.dram_tensor("muq_dram", (NT, 128, HEADS * R), F32, kind="Internal").ap()
        cpad = nc.dram_tensor("cpad", (B, 64 + L, C), F32, kind="Internal").ap()
        idx_dram = nc.dram_tensor("idx_dram", (2, 128 * FAR), FP16, kind="Internal").ap()
        RA, RV = banks[0:5], banks[5:8]

        prep = ExitStack()
        with prep:
            def sb(name, shape, dt):
                return prep.enter_context(nc.sbuf_tensor(name, shape, dt))

            def sem(name):
                return prep.enter_context(nc.semaphore(name))

            stats = sb("a_stats", [128, NT, 6], F32)
            moments = sb("a_moments", [128, NT, 5], F32)
            xn = sb("a_xn", [128, NT, D], F32)
            wkv = sb("wkv", [128, C + R], F32)
            cqT = sb("cqT", [CQ, NT * 128], F32)
            wqr = sb("wqr", [CQ, HEADS * R], F32)
            wik = sb("wik", [128, 2, 64], F32)
            wuq = sb("wuq", [CQ, 512], F32)
            wuk = sb("wuk", [C, 512], F32)
            wuv = sb("wuv", [C, 512], F32)
            wout = sb("wout", [128, 4, D], F32)
            wuqT = sb("wuqT", [128, 4, CQ], F32)
            wukT = sb("wukT", [128, 4, C], F32)
            wuvT = sb("wuvT", [128, 4, C], F32)
            delta = sb("delta", [128, 6, Q4], F32)
            base = sb("base", [128, 2 * TILES + 1, 2, Q4], F32)
            tt = sb("tt", [128, 2 * TILES + 1, Q4], F32)
            peak = sb("peak", [128, 4], F32)
            peak_all = sb("peak_all", [1, 1], F32)
            ones = sb("a_ones", [1, 128], F32)
            kn = sb("kn", [128, NT, C + R], F32)
            sp_a = sb("sp_a", [128, NT, R], F32)
            key3 = sb("key3", [128, NT, 96], F32)
            val = sb("val", [128, NT, 64], F32)
            rt = sb("rt", [128, NT, Q4], F32)
            qsp = sb("qsp", [128, NT, HEADS * R], F32)

            up_loads = sem("up_loads")
            loads = sem("a_loads")
            a_link = sem("a_link")
            v_link = sem("v_link")
            filled = sem("p_filled")
            emptied = sem("p_emptied")
            varied = sem("a_varied")
            rooted = sem("a_rooted")
            normed = sem("a_normed")
            kn_soft = sem("kn_soft")
            key_ready = sem("key_ready")
            key_filled = sem("key_filled")
            pads = sem("pads")
            cstored = sem("cstored")
            scaled = sem("scaled")
            peak_step = sem("peak_step")
            peak_made = sem("peak_made")
            q_filled = sem("q_filled")
            q_abs = sem("q_abs")
            q_soft = sem("q_soft")
            muq_done = sem("muq_done")
            q_stored = sem("q_stored")
            quarter = sem("quarter")
            half_pi = sb("half_pi", [128, 1], F32)
            sined = sem("sined")
            NLOAD = 14

            order = ["wuqT", "wukT", "wuvT", "absorb0", "absorb1", "wvo0", "wvo1"] + [("xT", c) for c in range(NC)]
            order += [("kn", h) for h in range(2)] + [("cqT", c) for c in range(NC)] + [("kiT", c) for c in range(NC)]
            at = {k: u for u, k in enumerate(order)}
            blk = prep.enter_context(nc.Block())

            @blk.sync
            def _(sp):
                for dst, src in ((wuq[:, :], t["attn_W_uq"]), (wuk[:, :], t["attn_W_uk"]), (wuv[:, :], t["attn_W_uv"]),
                                 (wout[:, :, :], t["attn_W_out"].rearrange("(k p) n -> p k n", p=128))):
                    sp.dma_start(dst, src).then_inc(up_loads, 16)
                for dst, src in ((wkv[:, 0:C], t["attn_W_dkv"]), (wkv[:, C:], t["attn_W_kr"]), (wdq[:, :], t["attn_W_dq"]),
                                 (wqr[:, :], t["attn_W_qr"]), (wik[:, 0, :], t["attn_idx_wk"]),
                                 (wik[:, 1, :], t["attn_idx_wk"]), (wiq[:, :], t["attn_idx_wq"]),
                                 (idxw[:, :], t["attn_idx_w"].partition_broadcast(128)),
                                 (delta[:, 0, :], t["attn_raw_delta"].partition_broadcast(128)),
                                 (base[:, :, :, :], t["trig"]), (late[:, :], t["late"]), (early[:, :], t["early"]),
                                 (smask[:, :].bitcast(mybir.dt.uint16), t["smask"]), (keyno[:, :], t["keyno"])):
                    sp.dma_start(dst, src).then_inc(loads, 16)
                sp.wait_ge(pads, 3)
                for b in range(B):
                    sp.dma_start(cpad[b, 0:64, :], key3[0:64, b, 32:64]).then_inc(cstored, 16)
                sp.wait_ge(scaled, 1)
                for b in range(B):
                    sp.dma_start(cpad[b, 64:64 + L, :].rearrange("(n p) c -> p n c", p=128),
                                 val[:, TILES * b:TILES * (b + 1), 0:C]).then_inc(cstored, 16)
                for c in range(4):
                    sp.wait_ge(muq_done, 2 * c + 2)
                    sp.dma_start(muq_dram[4 * c:4 * c + 4, :, :].rearrange("n p c -> p n c"),
                                 qsp[:, 4 * c:4 * c + 4, :]).then_inc(q_stored, 16)
                sp.wait_ge(cstored, 64)
                sp.wait_ge(q_stored, 64)

            @blk.gpsimd
            def _(pool):
                pool.memset(half_pi[:, :], PI / 2).then_inc(quarter, 1)
                pool.memset(ones[:, :], 1.0).then_inc(pads, 1)
                pool.memset(key3[:, :, 32:64], 0.0).then_inc(pads, 1)
                pool.memset(keyT[:, :, 0:64], 0.0).then_inc(pads, 1)

            @blk.scalar
            def _(act):
                links = [0]

                def link(ins):
                    links[0] += 1
                    ins.then_inc(a_link, 1)
                    act.wait_ge(a_link, links[0])

                def empty(key, dst, src):
                    act.wait_ge(filled, at[key] + 1)
                    act.activation(dst, src, ACT.Copy).then_inc(emptied, 1)

                def bank(key):
                    return banks[at[key] % 8]

                ln_root(act, moments, varied, rooted, 0)
                ln_root(act, moments, varied, rooted, 1)
                empty("wuqT", wuqT[:, :, :], bank("wuqT")[:, 0:4 * CQ].rearrange("p (k c) -> p k c", k=4))
                empty("wukT", wukT[:, :, :], bank("wukT")[:, 0:4 * C].rearrange("p (k c) -> p k c", k=4))
                empty("wuvT", wuvT[:, :, :], bank("wuvT")[:, 0:4 * C].rearrange("p (k c) -> p k c", k=4))
                ln_root(act, moments, varied, rooted, 2)
                for s in range(2):
                    empty(f"absorb{s}", absorb[:, :, :].rearrange("p (j s) c -> p s j c", s=2)[:, s, :, :],
                          bank(f"absorb{s}")[0:CQ, 0:128].rearrange("p (j c) -> p j c", c=C))
                ln_root(act, moments, varied, rooted, 3)
                for s in range(2):
                    empty(f"wvo{s}", wvo[:, :, :].rearrange("p (j s) c -> p s j c", s=2)[:, s, :, :],
                          bank(f"wvo{s}")[0:C, :].rearrange("p (j d) -> p j d", d=D))
                for c in range(NC):
                    empty(("xT", c), xnT[:, c * 512:(c + 1) * 512], bank(("xT", c))[:, :])
                for h in range(2):
                    empty(("kn", h), kn[:, 8 * h:8 * h + 8, :],
                          bank(("kn", h))[:, :].rearrange("p (n c) -> p n c", c=64))
                act.wait_ge(emptied, at[("kn", 1)] + 1)
                link(act.activation(sp_a[:, :, :], kn[:, :, C:], ACT.Abs))
                link(act.activation(sp_a[:, :, :], sp_a[:, :, :], ACT.Exp, scale=-1.0))
                act.activation(sp_a[:, :, :], sp_a[:, :, :], ACT.Ln, bias=1.0).then_inc(kn_soft, 1)
                for c in range(NC):
                    empty(("cqT", c), cqT[:, c * 512:(c + 1) * 512], bank(("cqT", c))[0:CQ, :])
                for c in range(NC):
                    empty(("kiT", c), kiT[:, c * 512:(c + 1) * 512], bank(("kiT", c))[:, :])
                act.wait_ge(loads, 16 * NLOAD)
                link(act.activation(delta[:, 1, :], delta[:, 0, :], ACT.Sigmoid))
                link(act.activation(delta[:, 2, :], delta[:, 1, :], ACT.Sin, scale=-PI))
                act.wait_ge(quarter, 1)
                act.activation(delta[:, 3, :], delta[:, 1, :], ACT.Sin, scale=-PI, bias=half_pi[:, :]).then_inc(sined, 1)
                for c in range(NT // 2):
                    act.wait_ge(q_filled, c + 1)
                    act.activation(qsp[:, 2 * c:2 * c + 2, :], banks[c][:, :].rearrange("p (n c) -> p n c", n=2),
                                   ACT.Abs).then_inc(q_abs, 1)
                    act.wait_ge(q_abs, c + 1)
                    two = qsp[:, 2 * c:2 * c + 2, :]
                    last = act.activation(two, two, ACT.Exp, scale=-1.0)
                link(last)
                for c in range(NT // 2):
                    two = qsp[:, 2 * c:2 * c + 2, :]
                    act.activation(two, two, ACT.Ln, bias=1.0).then_inc(q_soft, 1)
                for c in range(NC):
                    dst = keyT[:, c // 2, 64 + (c % 2) * 512:64 + (c % 2 + 1) * 512]
                    act.wait_ge(key_filled, c + 1)
                    act.activation(dst, banks[c][0:96, :], ACT.Copy)

            @blk.vector
            def _(dve):
                links = [0]

                def link(ins):
                    links[0] += 1
                    ins.then_inc(v_link, 1)
                    dve.wait_ge(v_link, links[0])

                for g in range(NT // 4):
                    ln_statistics(dve, link, x, stats, moments, g, varied)
                    if g >= 1:
                        ln_apply(dve, link, x, xn, moments, g - 1, rooted, normed)
                ln_apply(dve, link, x, xn, moments, NT // 4 - 1, rooted, normed)

                dve.wait_ge(kn_soft, 1)
                dve.scalar_tensor_tensor(val[:, :, C:], kn[:, :, C:], 0.0, sp_a[:, :, :], ALU.max, ALU.add)
                link(dve.tensor_copy(val[:, :, 0:C], kn[:, :, 0:C]))
                dve.tensor_reduce(peak[:, 0:1], val[:, :, :].rearrange("p n c -> p (n c)"), AX.X, ALU.max,
                                  apply_absolute_value=True).then_inc(peak_made, 1)
                dve.wait_ge(peak_step, 1)
                dve.tensor_reduce(peak_all[:, :], banks[7][0:1, 0:128], AX.X, ALU.max).then_inc(peak_made, 1)
                dve.wait_ge(peak_step, 2)
                link(dve.tensor_scalar(peak[:, 1:2], banks[7][:, 128:129], 2.0 ** -60, None, ALU.max))
                link(dve.tensor_scalar(peak[:, 2:3].bitcast(mybir.dt.int32), peak[:, 1:2].bitcast(mybir.dt.int32),
                                       0x7F800000, None, ALU.bitwise_and))
                link(dve.reciprocal(peak[:, 3:4], peak[:, 2:3]))
                dve.tensor_scalar(peak[:, 3:4], peak[:, 3:4], 2.0 ** 14, None, ALU.mult)
                dve.tensor_scalar(peak[:, 2:3], peak[:, 2:3], 2.0 ** -14, None, ALU.mult).then_inc(peak_made, 1)
                dve.wait_ge(peak_made, 3)
                link(dve.tensor_scalar(expo[:, 0:1], peak[:, 2:3], SCALE, None, ALU.mult))
                dve.tensor_scalar(expo[:, 1:2], peak[:, 2:3], -SCALE, None, ALU.mult)
                dve.tensor_scalar(val[:, :, :], val[:, :, :], peak[:, 3:4], None, ALU.mult).then_inc(scaled, 1)
                dve.wait_ge(scaled, 1)
                dve.wait_ge(pads, 3)
                link(dve.tensor_copy(key3[:, :, 0:C], val[:, :, 0:C]))
                dve.wait_ge(loads, 16 * NLOAD)
                dve.wait_ge(sined, 1)
                sh, ch, sd, cd = (delta[:, k, :] for k in (2, 3, 4, 5))
                link(dve.tensor_tensor(sd, sh, ch, ALU.mult))
                link(dve.tensor_scalar(sd, sd, 2.0, None, ALU.mult))
                link(dve.tensor_tensor(cd, sh, sh, ALU.mult))
                link(dve.tensor_scalar(cd, cd, -2.0, 1.0, ALU.mult, ALU.add))
                n = 2 * TILES + 1

                def wide(ap):
                    return ap.unsqueeze(1).broadcast_to([128, n, Q4])

                for k, sign in ((0, ALU.subtract), (1, ALU.add)):
                    link(dve.tensor_tensor(trig[:, :, k, :], base[:, :, k, :], wide(cd), ALU.mult))
                    link(dve.tensor_tensor(tt[:, :, :], base[:, :, 1 - k, :], wide(sd), ALU.mult))
                    link(dve.tensor_tensor(trig[:, :, k, :], trig[:, :, k, :], tt[:, :, :], sign))

                for b in range(B):
                    n = slice(TILES * b, TILES * (b + 1))
                    co, si = trig[:, 0:TILES, 0, :], trig[:, 0:TILES, 1, :]
                    m1, m2 = val[:, n, C:C + Q4], val[:, n, C + Q4:]
                    for dst, a, z, op in ((slice(64, 80), co, si, ALU.subtract), (slice(80, 96), si, co, ALU.add)):
                        link(dve.tensor_tensor(key3[:, n, dst], m1, a, ALU.mult))
                        link(dve.tensor_tensor(rt[:, n, :], m2, z, ALU.mult))
                        last = dve.tensor_tensor(key3[:, n, dst], key3[:, n, dst], rt[:, n, :], op)
                        if b == 0 or op == ALU.subtract:
                            link(last)
                last.then_inc(key_ready, 1)
                link(dve.tensor_copy(ctab[:, :, 0, :], val[:, :, :]))
                link(dve.tensor_tensor(kn[:, :, :], val[:, :, :], ctab[:, :, 0, :], ALU.subtract))
                link(dve.tensor_copy(ctab[:, :, 1, :], kn[:, :, :]))
                dve.wait_ge(emptied, at["wvo1"] + 1)
                dve.tensor_scalar(wvo[:, :, :], wvo[:, :, :], peak[0:C, 2:3], None, ALU.mult)
                for c in range(NT // 2):
                    dve.wait_ge(q_soft, c + 1)
                    two = qsp[:, 2 * c:2 * c + 2, :].rearrange("p n c -> p (n c)")
                    dve.scalar_tensor_tensor(two, banks[c][:, :], 0.0, two, ALU.max, ALU.add).then_inc(muq_done, 1)

            @blk.tensor
            def _(pe):
                def bank(key):
                    if at[key] >= 8:
                        pe.wait_ge(emptied, at[key] - 7)
                    return banks[at[key] % 8]

                pe.wait_ge(up_loads, 64)
                for key, src, rows in (("wuqT", wuq, CQ), ("wukT", wuk, C), ("wuvT", wuv, C)):
                    o = bank(key)
                    for k in range(4):
                        last = pe.transpose(o[:, k * rows:(k + 1) * rows], src[:, k * 128:(k + 1) * 128],
                                            ident[0:rows, 0:rows])
                    last.then_inc(filled, 1)
                pe.wait_ge(emptied, at["wuvT"] + 1)
                for s in range(2):
                    rows = slice(64 * s, 64 * s + 64)
                    o = bank(f"absorb{s}")
                    for j in range(4):
                        last = pe.matmul(o[0:CQ, j * C:(j + 1) * C], wuqT[rows, j, :], wukT[rows, j, :],
                                         start=True, stop=True)
                    last.then_inc(filled, 1)
                for s in range(2):
                    rows = slice(64 * s, 64 * s + 64)
                    o = bank(f"wvo{s}")
                    for j in range(4):
                        last = pe.matmul(o[0:C, j * D:(j + 1) * D], wuvT[rows, j, :], wout[rows, j, :],
                                         start=True, stop=True)
                    last.then_inc(filled, 1)
                for c in range(NC):
                    pe.wait_ge(normed, c + 1)
                    o = bank(("xT", c))
                    for k in range(4):
                        last = pe.transpose(o[:, k * 128:(k + 1) * 128], xn[:, 4 * c + k, :], ident)
                    last.then_inc(filled, 1)
                pe.wait_ge(loads, 16 * NLOAD)
                for g in range(2):
                    o = bank(("kn", g))
                    pe.wait_ge(emptied, at[("xT", 2 * g + 1)] + 1)
                    for k in range(8):
                        n = 8 * g + k
                        last = pe.matmul(o[:, k * 64:(k + 1) * 64], xnT[:, n * 128:(n + 1) * 128], wkv[:, :],
                                         start=True, stop=True)
                    last.then_inc(filled, 1)
                for c in range(NC):
                    pe.matmul(bank(("cqT", c))[0:CQ, :], wdq[:, :], xnT[:, c * 512:(c + 1) * 512],
                              start=True, stop=True).then_inc(filled, 1)
                for c in range(NC):
                    pe.matmul(bank(("kiT", c))[:, :], wik[:, :, :].rearrange("d a k -> d (a k)"),
                              xnT[:, c * 512:(c + 1) * 512], start=True, stop=True).then_inc(filled, 1)
                pe.wait_ge(emptied, at[("kiT", NC - 1)] + 1)
                pe.wait_ge(peak_made, 1)
                pe.transpose(banks[7][0:1, 0:128], peak[:, 0:1], ident).then_inc(peak_step, 1)
                for c in range(NT // 2):
                    if c == 1:
                        pe.wait_ge(pads, 3)
                        pe.wait_ge(peak_made, 2)
                        pe.matmul(banks[7][:, 128:129], ones[:, :], peak_all[:, :], start=True,
                                  stop=True).then_inc(peak_step, 1)
                    if c == 7:
                        pe.wait_ge(peak_made, 3)
                    for k in range(2):
                        n = 2 * c + k
                        last = pe.matmul(banks[c][:, k * 256:(k + 1) * 256], cqT[:, n * 128:(n + 1) * 128], wqr[:, :],
                                         start=True, stop=True)
                    last.then_inc(q_filled, 1)
                pe.wait_ge(key_ready, 1)
                for c in range(NC):
                    pe.wait_ge(muq_done, c + 1)
                    for k in range(4):
                        last = pe.transpose(banks[c][0:96, k * 128:(k + 1) * 128], key3[:, 4 * c + k, :], ident)
                    last.then_inc(key_filled, 1)
        attn_loop(nc, x, x_out, ident, identb, xnT, kiT, wiq, wdq, keyT, ctab, muq_dram, trig, absorb, wvo, expo,
                  idxw, late, early, smask, keyno, cpad, idx_dram, RA, RV, A_AT, V_AT, C_AT)


def macaron_kernel(nc, t, out):
    ctx = ExitStack()
    with ctx:
        def sb(name, shape, dt):
            return ctx.enter_context(nc.sbuf_tensor(name, shape, dt))

        xs = sb("xs", [128, NT, D], F32)
        ident = sb("ident", [128, 128], F32)
        identb = sb("identb", [128, 128], BF16)
        sel = sb("sel", [96, PAIRS // 2, 128], BF16)
        banks = [ctx.enter_context(nc.psum_tensor(f"bank{i}", [128, 512], F32)) for i in range(8)]
        start_loaded = ctx.enter_context(nc.semaphore("start_loaded"))
        stored = ctx.enter_context(nc.semaphore("stored"))

        with nc.Block() as blk:
            @blk.sync
            def _(sp):
                sp.dma_start(xs[:, :, :], t["x"].rearrange("b (n p) d -> p (b n) d", p=128)).then_inc(start_loaded, 16)
                sp.dma_start(ident[:, :], t["ident"]).then_inc(start_loaded, 16)
                sp.dma_start(identb[:, :].bitcast(mybir.dt.uint16), t["identb"]).then_inc(start_loaded, 16)
                sp.dma_start(sel[:, :, :].bitcast(mybir.dt.uint16), t["sel"]).then_inc(start_loaded, 16)
                sp.wait_ge(start_loaded, 64)

        const = {"ident": ident[:, :], "identb": identb[:, :], "sel": sel}
        w = {k: t[f"ffn_{n}"] for k, n in (("router", "router_w"), ("sgate", "shared_gate_w"), ("sup", "shared_up_w"),
                                           ("sdown", "shared_down_w"), ("gate", "expert_gate_k"),
                                           ("up", "expert_up_k"), ("down", "expert_down_k"))}
        ffn_phase(nc, "f1", xs[:, :, :], xs, w, const, banks)
        attn_phase(nc, t, xs, xs, const, banks)
        ffn_phase(nc, "f2", xs[:, :, :], xs, w, const, banks)
    
        with nc.Block() as blk:
            @blk.sync
            def _(sp):
                sp.dma_start(out.rearrange("b (n p) d -> p (b n) d", p=128), xs[:, :, :]).then_inc(stored, 16)
                sp.wait_ge(stored, 16)


_FFN = ['ffn_router_w', 'ffn_shared_gate_w', 'ffn_shared_up_w', 'ffn_shared_down_w', 'ffn_expert_gate_k',
        'ffn_expert_up_k', 'ffn_expert_down_k']
_ATTN = ['attn_W_dkv', 'attn_W_uk', 'attn_W_uv', 'attn_W_dq', 'attn_W_uq', 'attn_W_qr', 'attn_W_kr', 'attn_W_out',
         'attn_idx_wq', 'attn_idx_wk', 'attn_idx_w', 'attn_raw_delta']


def _constants():
    import numpy as np
    one = 0x3F80
    c = {"ident": np.eye(128, dtype=np.float32), "identb": (np.eye(128) * one).astype(np.uint16)}
    sel = np.zeros((96, PAIRS // 2, 128), np.uint16)
    for part in range(3):
        for q in range(PAIRS // 2):
            for s in range(2):
                sel[part * 32 + 2 * q + s, q, 64 * s:64 * s + 64] = one
    c["sel"] = sel
    c.update(_attn_constants())
    return c


def kernel(**inputs):
    import numpy as _np
    import concourse.bacc as _bacc
    from concourse import mybir as _mybir
    from concourse.bass_utils import run_bass_kernel_spmd as _run

    nc = _bacc.Bacc("TRN2", target_bir_lowering=False, num_devices=1)
    arrays, t = {}, {}

    def take(name, a):
        arrays[f"in_{name}_dram"] = a
        t[name] = nc.dram_tensor(f"in_{name}_dram", a.shape, _mybir.dt.from_np(a.dtype), kind="ExternalInput").ap()

    take("x", _np.ascontiguousarray(inputs["L0_attn_x"]))
    for name in _FFN + _ATTN:
        take(name, _np.ascontiguousarray(inputs["L0_" + name]))
    for name, a in _constants().items():
        take(name, a)
    out = nc.dram_tensor("out_0_dram", (B, L, D), _mybir.dt.float32, kind="ExternalOutput").ap()
    macaron_kernel(nc, t, out)
    r = _run(nc, [arrays], core_ids=[0])
    return r.results[0]["out_0_dram"]
```
